# Optimizing a Trainium2 kernel written in Bass

```python
import numpy as np
import jax
import jax.numpy as jnp

def _softmax(x, axis=-1):
    return jax.nn.softmax(x, axis=axis)

def _gelu(x):
    return jax.nn.gelu(x, approximate=True)

def _silu(x):
    return jax.nn.silu(x)

def _sigmoid(x):
    return jax.nn.sigmoid(x)

def _layernorm(x, axis=-1, eps=1e-05):
    m = jnp.mean(x, axis=axis, keepdims=True)
    v = jnp.var(x, axis=axis, keepdims=True)
    return (x - m) / jnp.sqrt(v + eps)

def _scatter_add(tgt, idx, src, axis=0):
    return tgt.at[idx].add(src)

def _segment_sum(src, seg, n):
    return jax.ops.segment_sum(src, seg, n)
kernel_name = 'mk_gnn_preln_d2_gnn_r8_ed3b66'

def setup_inputs(seed: int=0):
    np.random.seed(seed)
    _w = jnp.asarray

    def _rec_inputs():
        import jax
        import jax.numpy as jnp
        _gk = jax.random.key(seed)
        x = -8.776e-05 + 1 * jax.random.normal(jax.random.fold_in(_gk, 1), (12500, 128), jnp.float32)
        src = jax.random.randint(jax.random.fold_in(_gk, 2), (200000,), 0, 12500, jnp.int32)
        dst = jnp.minimum((12500 * jax.random.uniform(jax.random.fold_in(_gk, 3), (200000,)) ** 2.0).astype(jnp.int32), 99999)
        _o = jnp.argsort(dst, stable=True)
        src = src[_o]
        dst = dst[_o]
        edge_attr_3 = -0.000451519 + 1.00018 * jax.random.normal(jax.random.fold_in(_gk, 12), (200000, 3), jnp.float32)
        edge_attr_64 = 0.000167468 + 1.0002 * jax.random.normal(jax.random.fold_in(_gk, 13), (200000, 64), jnp.float32)
        edge_weight = jax.random.uniform(jax.random.fold_in(_gk, 15), (200000,), jnp.float32, 0.0, 0.999998)
        return (x, src, dst, edge_attr_3, edge_attr_64, edge_weight)
    x, src, dst, edge_attr_3, edge_attr_64, edge_weight = _rec_inputs()

    def _L0_gnn_setup():
        import jax, jax.numpy as jnp
        import numpy as np
        N = 5000
        E = 80000
        ND = 128
        ED = 64
        LN_EPS = 1e-05
        key = jax.random.key(seed)
        ks = jax.random.split(key, 16)
        s = lambda k, shape, fan_in: jax.random.normal(k, shape, dtype=jnp.float32) * (1.0 / np.sqrt(fan_in))
        return {'node_features': jax.random.normal(ks[0], (N, ND), dtype=jnp.float32), 'edge_indices': jax.random.randint(ks[1], (2, E), 0, N, dtype=jnp.int32), 'edge_features': jax.random.normal(ks[2], (E, ED), dtype=jnp.float32), 'W1': s(ks[3], (2 * ND + ED, ND), 2 * ND + ED), 'b1': jnp.zeros((ND,), jnp.float32), 'ln_g': jnp.ones((ND,), jnp.float32), 'ln_b': jnp.zeros((ND,), jnp.float32), 'W2': s(ks[4], (ND, ND), ND), 'b2': jnp.zeros((ND,), jnp.float32), 'gate_w': s(ks[5], (ED, 1), ED), 'gate_b': jnp.zeros((1,), jnp.float32), 'W_ih': s(ks[6], (3 * ND, ND), ND), 'b_ih': jnp.zeros((3 * ND,), jnp.float32), 'W_hh': s(ks[7], (3 * ND, ND), ND), 'b_hh': jnp.zeros((3 * ND,), jnp.float32)}
    _L0_gnn_all = _L0_gnn_setup()
    _L0_gnn_in = {k: v for k, v in _L0_gnn_all.items() if k in ('W1', 'b1', 'ln_g', 'ln_b', 'W2', 'b2', 'gate_w', 'gate_b', 'W_ih', 'b_ih', 'W_hh', 'b_hh')}
    del _L0_gnn_all

    def _L1_gnn_setup():
        import jax, jax.numpy as jnp
        import numpy as np
        N = 6250
        E = 100000
        MUL = 32
        NB = 8
        R_MAX = 1.0
        AVG = 16.0
        SQ3 = 3.0 ** 0.5

        def _radial_embedding(r):
            x = jnp.clip(r / R_MAX, 0.0, 1.0)
            centers = jnp.arange(NB, dtype=jnp.float32) / (NB - 1)
            sigma = 1.0 / (NB - 1)
            emb = jnp.exp(-0.5 * ((x[:, None] - centers[None, :]) / sigma) ** 2)
            emb = emb * NB ** 0.5 * (r <= R_MAX).astype(jnp.float32)[:, None]
            return emb
        key = jax.random.key(seed)
        k = jax.random.split(key, 12)
        inp = {'node_feats': jax.random.normal(k[0], (N, 4 * MUL), dtype=jnp.float32), 'edge_vec': jax.random.normal(k[1], (E, 3), dtype=jnp.float32), 'edge_length': jax.random.uniform(k[2], (E,), dtype=jnp.float32), 'senders': jax.random.randint(k[3], (E,), 0, N, dtype=jnp.int32), 'receivers': jax.random.randint(k[4], (E,), 0, N, dtype=jnp.int32), 'num_nodes': N, 'W_up0': jax.random.normal(k[5], (MUL, MUL), dtype=jnp.float32), 'W_up1': jax.random.normal(k[6], (MUL, MUL), dtype=jnp.float32), 'mlp_w0': jax.random.normal(k[7], (NB, 64), dtype=jnp.float32) / NB ** 0.5, 'mlp_b0': jnp.zeros((64,), dtype=jnp.float32), 'mlp_w1': jax.random.normal(k[8], (64, 64), dtype=jnp.float32) / 8.0, 'mlp_b1': jnp.zeros((64,), dtype=jnp.float32), 'mlp_w2': jax.random.normal(k[9], (64, 4 * MUL), dtype=jnp.float32) / 8.0, 'mlp_b2': jnp.zeros((4 * MUL,), dtype=jnp.float32), 'W_out0': jax.random.normal(k[10], (2 * MUL, MUL), dtype=jnp.float32), 'W_out1': jax.random.normal(k[11], (2 * MUL, MUL), dtype=jnp.float32)}
        return inp
    _L1_gnn_all = _L1_gnn_setup()
    _L1_gnn_in = {k: v for k, v in _L1_gnn_all.items() if k in ('W_up0', 'W_up1', 'mlp_w0', 'mlp_b0', 'mlp_w1', 'mlp_b1', 'mlp_w2', 'mlp_b2', 'W_out0', 'W_out1')}
    del _L1_gnn_all
    return {'x': x, 'src': src, 'dst': dst, 'edge_attr_3': edge_attr_3, 'edge_attr_64': edge_attr_64, 'edge_weight': edge_weight, 'L0_gnn_W1': _L0_gnn_in['W1'], 'L0_gnn_b1': _L0_gnn_in['b1'], 'L0_gnn_ln_g': _L0_gnn_in['ln_g'], 'L0_gnn_ln_b': _L0_gnn_in['ln_b'], 'L0_gnn_W2': _L0_gnn_in['W2'], 'L0_gnn_b2': _L0_gnn_in['b2'], 'L0_gnn_gate_w': _L0_gnn_in['gate_w'], 'L0_gnn_gate_b': _L0_gnn_in['gate_b'], 'L0_gnn_W_ih': _L0_gnn_in['W_ih'], 'L0_gnn_b_ih': _L0_gnn_in['b_ih'], 'L0_gnn_W_hh': _L0_gnn_in['W_hh'], 'L0_gnn_b_hh': _L0_gnn_in['b_hh'], 'L1_gnn_W_up0': _L1_gnn_in['W_up0'], 'L1_gnn_W_up1': _L1_gnn_in['W_up1'], 'L1_gnn_mlp_w0': _L1_gnn_in['mlp_w0'], 'L1_gnn_mlp_b0': _L1_gnn_in['mlp_b0'], 'L1_gnn_mlp_w1': _L1_gnn_in['mlp_w1'], 'L1_gnn_mlp_b1': _L1_gnn_in['mlp_b1'], 'L1_gnn_mlp_w2': _L1_gnn_in['mlp_w2'], 'L1_gnn_mlp_b2': _L1_gnn_in['mlp_b2'], 'L1_gnn_W_out0': _L1_gnn_in['W_out0'], 'L1_gnn_W_out1': _L1_gnn_in['W_out1']}

def reference(x, src, dst, edge_attr_3, edge_attr_64, edge_weight, L0_gnn_W1, L0_gnn_b1, L0_gnn_ln_g, L0_gnn_ln_b, L0_gnn_W2, L0_gnn_b2, L0_gnn_gate_w, L0_gnn_gate_b, L0_gnn_W_ih, L0_gnn_b_ih, L0_gnn_W_hh, L0_gnn_b_hh, L1_gnn_W_up0, L1_gnn_W_up1, L1_gnn_mlp_w0, L1_gnn_mlp_b0, L1_gnn_mlp_w1, L1_gnn_mlp_b1, L1_gnn_mlp_w2, L1_gnn_mlp_b2, L1_gnn_W_out0, L1_gnn_W_out1):
    import jax
    import jax.numpy as jnp

    def _L0_gnn_ref(node_features, edge_indices, edge_features, W1, b1, ln_g, ln_b, W2, b2, gate_w, gate_b, W_ih, b_ih, W_hh, b_hh):
        import jax, jax.numpy as jnp
        import numpy as np
        N = 5000
        E = 80000
        ND = 128
        ED = 64
        LN_EPS = 1e-05
        src, dst = (edge_indices[0], edge_indices[1])
        edge_inputs = jnp.concatenate([node_features[src], node_features[dst], edge_features], axis=1)
        h = edge_inputs @ W1 + b1
        mu = jnp.mean(h, axis=-1, keepdims=True)
        var = jnp.var(h, axis=-1, keepdims=True)
        h = (h - mu) * jax.lax.rsqrt(var + LN_EPS) * ln_g + ln_b
        h = jax.nn.relu(h)
        messages = h @ W2 + b2
        gate = jax.nn.sigmoid(edge_features @ gate_w + gate_b)
        messages = messages * gate
        agg = jax.ops.segment_sum(messages, dst, num_segments=node_features.shape[0])
        gi = agg @ W_ih.T + b_ih
        gh = node_features @ W_hh.T + b_hh
        i_r, i_z, i_n = jnp.split(gi, 3, axis=1)
        h_r, h_z, h_n = jnp.split(gh, 3, axis=1)
        r = jax.nn.sigmoid(i_r + h_r)
        z = jax.nn.sigmoid(i_z + h_z)
        n = jnp.tanh(i_n + r * h_n)
        return (1.0 - z) * n + z * node_features

    def _L1_gnn_ref(node_feats, edge_vec, edge_length, senders, receivers, num_nodes, W_up0, W_up1, mlp_w0, mlp_b0, mlp_w1, mlp_b1, mlp_w2, mlp_b2, W_out0, W_out1):
        import jax, jax.numpy as jnp
        import numpy as np
        N = 6250
        E = 100000
        MUL = 32
        NB = 8
        R_MAX = 1.0
        AVG = 16.0
        SQ3 = 3.0 ** 0.5

        def _radial_embedding(r):
            x = jnp.clip(r / R_MAX, 0.0, 1.0)
            centers = jnp.arange(NB, dtype=jnp.float32) / (NB - 1)
            sigma = 1.0 / (NB - 1)
            emb = jnp.exp(-0.5 * ((x[:, None] - centers[None, :]) / sigma) ** 2)
            emb = emb * NB ** 0.5 * (r <= R_MAX).astype(jnp.float32)[:, None]
            return emb
        f32 = jnp.float32
        rhat = edge_vec / (jnp.linalg.norm(edge_vec, axis=-1, keepdims=True) + 1e-12)
        Y1 = SQ3 * rhat
        emb = _radial_embedding(edge_length)
        h = jax.nn.silu(emb @ mlp_w0 + mlp_b0)
        h = jax.nn.silu(h @ mlp_w1 + mlp_b1)
        w = (h @ mlp_w2 + mlp_b2).reshape(-1, 4, MUL)
        s = node_feats[:, :MUL]
        v = node_feats[:, MUL:].reshape(-1, MUL, 3)
        xs = s @ W_up0 / f32(MUL) ** 0.5
        xv = jnp.einsum('nmc,mk->nkc', v, W_up1) / f32(MUL) ** 0.5
        ss = xs[senders]
        vv = xv[senders]
        m0 = w[:, 0] * ss
        m1 = w[:, 1][:, :, None] * ss[:, :, None] * Y1[:, None, :]
        m2 = w[:, 2][:, :, None] * vv
        m3 = w[:, 3] * (jnp.einsum('emc,ec->em', vv, Y1) / SQ3)
        mid_s = jnp.concatenate([m0, m3], axis=1)
        mid_v = jnp.concatenate([m1, m2], axis=1)
        msg_s = jax.ops.segment_sum(mid_s, receivers, num_segments=num_nodes)
        msg_v = jax.ops.segment_sum(mid_v, receivers, num_segments=num_nodes)
        out_s = msg_s @ W_out0 / f32(2 * MUL) ** 0.5
        out_v = jnp.einsum('nmc,mk->nkc', msg_v, W_out1) / f32(2 * MUL) ** 0.5
        out = jnp.concatenate([out_s, out_v.reshape(-1, 3 * MUL)], axis=1)
        return out / max(AVG, 1e-08)
    edge_index = jnp.stack([src, dst])
    h = jnp.maximum(_layernorm(x, axis=-1), 0.0)
    x = x + _L0_gnn_ref(h, edge_index, edge_attr_64, L0_gnn_W1, L0_gnn_b1, L0_gnn_ln_g, L0_gnn_ln_b, L0_gnn_W2, L0_gnn_b2, L0_gnn_gate_w, L0_gnn_gate_b, L0_gnn_W_ih, L0_gnn_b_ih, L0_gnn_W_hh, L0_gnn_b_hh)
    h = jnp.maximum(_layernorm(x, axis=-1), 0.0)
    x = x + _L1_gnn_ref(h, edge_attr_3, edge_weight, src, dst, 12500, L1_gnn_W_up0, L1_gnn_W_up1, L1_gnn_mlp_w0, L1_gnn_mlp_b0, L1_gnn_mlp_w1, L1_gnn_mlp_b1, L1_gnn_mlp_w2, L1_gnn_mlp_b2, L1_gnn_W_out0, L1_gnn_W_out1)
    return x

_drawn_inputs = setup_inputs


def setup_inputs(seed=0):
    import zlib

    import numpy as np

    out = dict(_drawn_inputs(seed))
    spreads = {'L0_gnn_b1': (0.0, 0.1),
     'L0_gnn_ln_g': (1.0, 0.2),
     'L0_gnn_ln_b': (0.0, 0.1),
     'L0_gnn_b2': (0.0, 0.1),
     'L0_gnn_b_ih': (0.0, 0.387),
     'L0_gnn_b_hh': (0.0, 0.435),
     'L1_gnn_mlp_b0': (0.0, 0.611),
     'L1_gnn_mlp_b1': (0.0, 0.283),
     'L1_gnn_mlp_b2': (0.0, 0.1)}
    factors = {}
    for name, (base, spread) in spreads.items():
        noise = np.random.default_rng([zlib.crc32(name.encode()), seed]).standard_normal(out[name].shape)
        drawn = base * np.exp(spread * noise) if base else spread * noise
        out[name] = jnp.asarray(drawn.astype(out[name].dtype))
    for name, factor in factors.items():
        out[name] = (out[name] * factor).astype(out[name].dtype)
    return out
```

```python
import concourse.bass as bass
from concourse import mybir
from contextlib import ExitStack

F32 = mybir.dt.float32
BF16 = mybir.dt.bfloat16
I32 = mybir.dt.int32
ALU = mybir.AluOpType
ACT = mybir.ActivationFunctionType
AX = mybir.AxisListType

P = 128
D = 128
ED = 64
TILES = 4
GROUP = TILES * P
QUAD = 4 * P
UNROLL = 8
BATCH = 4
SUM_LAG = 6
MUL = 32
NB = 8
HID = 64
MSG = 9 * MUL
EPS = 1e-5
SQ3 = 3.0 ** 0.5
SPLITS = 3


def tile_offset(i):
    return (i % 2) * (GROUP // 2) + (i // 2) * P


def reached(step, n):
    return not isinstance(step, int) or step >= n


def layout(N, E):
    NP = -(-(N + 1 + P) // QUAD) * QUAD
    NG = -(-E // GROUP)
    NG = -(-NG // UNROLL) * UNROLL
    windows = N // P + 1
    J = -(-(NG * windows + UNROLL) // P)
    return NP, NG, J


def program(nc, io, N, E):
    NP, NG, J = layout(N, E)
    dram = {}

    def scratch(name, shape, dt):
        dram[name] = nc.dram_tensor(name, shape, dt).ap()

    scratch("a_table", (NP, D + 1), F32)
    scratch("b_table", (NP, SPLITS * D), BF16)
    scratch("hT_nodes", (D, NP), F32)
    scratch("x1_nodes", (NP, D), F32)
    scratch("u_table", (NP, D), F32)
    scratch("y_edges", (P, NG * TILES * 3), F32)
    scratch("emb_edges", (NB, NG * GROUP), F32)
    scratch("group_lo", (1, NG), I32)
    scratch("group_extra", (1, NG), I32)
    scratch("group_end", (1, NG), F32)
    scratch("group_step", (1, NG), F32)
    scratch("item_group", (1, P * J), I32)
    scratch("item_base", (1, P * J), I32)
    scratch("item_base_f", (1, P * J), F32)
    scratch("sum_base", (1, P * J + UNROLL), I32)

    with ExitStack() as ctx:
        def sb(name, shape, dt):
            return ctx.enter_context(nc.sbuf_tensor(name, shape, dt))

        keep = {
            "agg": sb("agg", [P, 2, NP], F32),
            "iota": sb("iota", [P, P], F32),
            "ident": sb("ident", [P, P], F32),
            "eps": sb("eps", [P, 1], F32),
            "meta_in": [ctx.enter_context(nc.semaphore(f"meta_in{u}")) for u in range(UNROLL)],
            "edge_in": [ctx.enter_context(nc.semaphore(f"edge_in{u}")) for u in range(UNROLL)],
            "gathered": [ctx.enter_context(nc.semaphore(f"gathered{u}")) for u in range(UNROLL)],
            "base_in": [ctx.enter_context(nc.semaphore(f"base_in{b}")) for b in range(UNROLL // BATCH)],
            "started": ctx.enter_context(nc.semaphore("started")),
            "ctl": sb("ctl", [1, 4], I32),
        }
        prepare(nc, io, dram, keep, N, NP, NG, J)
        node_tables(nc, io, dram, keep, NP)
        gated_edges(nc, io, dram, keep, NP, NG, J)
        gru_nodes(nc, io, dram, keep, NP)
        tensor_edges(nc, io, dram, keep, NP, NG, J)
        output_nodes(nc, io, dram, keep, NP)


def prepare(nc, io, dram, keep, N, NP, NG, J):
    agg, iota, ident, eps, ctl = (keep[k] for k in ("agg", "iota", "ident", "eps", "ctl"))
    PG = NG // UNROLL
    C = NG * GROUP // P
    with ExitStack() as ctx:
        def sb(name, shape, dt):
            return ctx.enter_context(nc.sbuf_tensor("prep_" + name, shape, dt))

        def sem(name):
            return ctx.enter_context(nc.semaphore("prep_" + name))

        dst_rows = sb("dst_rows", [PG, UNROLL, GROUP], I32)
        lo4 = sb("lo4", [PG, UNROLL], I32)
        hi4 = sb("hi4", [PG, UNROLL], I32)
        span4 = sb("span4", [PG, UNROLL], I32)
        extra4 = sb("extra4", [PG, UNROLL], I32)
        lo_row = sb("lo_row", [1, NG], I32)
        extra_row = sb("extra_row", [1, NG], I32)
        group_row = sb("group_row", [1, NG], I32)
        count = sb("count", [1, NG], F32)
        ones = sb("ones", [1, NG], F32)
        end_row = sb("end_row", [1, NG], F32)
        start_row = sb("start_row", [1, NG], F32)
        shift_row = sb("shift_row", [1, NG], F32)
        step_row = sb("step_row", [1, NG], F32)
        total = sb("total", [1, 2], I32)
        end_all = sb("end_all", [P, NG], F32)
        step_all = sb("step_all", [P, NG], F32)
        lo0 = sb("lo0", [P, 1], I32)
        slot = sb("slot", [P, J], F32)
        group_of = sb("group_of", [P, J], F32)
        base_of = sb("base_of", [P, J], F32)
        passed = sb("passed", [P, J], F32)
        live = sb("live", [P, J], F32)
        group_int = sb("group_int", [P, J], I32)
        base_int = sb("base_int", [P, J], I32)
        base_f = sb("base_f", [P, J], F32)
        lo_row_f = sb("lo_row_f", [1, NG], F32)
        first = sb("first", [1, SUM_LAG], I32)
        assert 5 * C <= NP
        vec = agg[:, 0, 0:3 * C].rearrange("p (c k) -> p c k", k=3)
        norm, dist, inside = (agg[:, 1, i * C:(i + 1) * C] for i in range(3))
        emb = agg[:, 1, 3 * C:5 * C].rearrange("p (s c) -> p s c", s=2)
        centers = sb("centers", [P, NB], F32)

        dst_in, edges_in, const_in = sem("dst_in"), sem("edges_in"), sem("const_in")
        spans_out, spans_in = sem("spans_out"), sem("spans_in")
        steps_out, steps_in = sem("steps_out"), sem("steps_in")
        items_out, edges_out = sem("items_out"), sem("edges_out")
        spans, listed, items, iotas = sem("spans"), sem("listed"), sem("items"), sem("iotas")
        squared, summed, rooted, unit = sem("squared"), sem("summed"), sem("rooted"), sem("unit")
        clipped, shifted, bell, masked = sem("clipped"), sem("shifted"), sem("bell"), sem("masked")
        emb_out = [sem("emb_out0"), sem("emb_out1")]
        chain = sem("chain")
        block = ctx.enter_context(nc.Block())

        @block.sync
        def _(sp):
            sp.dma_start(dst_rows[:], io["dst_flat"].rearrange("a (p q e) -> (a p) q e", p=PG, q=UNROLL)).then_inc(dst_in, 16)
            sp.dma_start(vec, io["edge_vec"]).then_inc(edges_in, 16)
            sp.dma_start(dist, io["edge_dist"]).then_inc(edges_in, 16)
            sp.dma_start(ident[:], io["ident"]).then_inc(const_in, 16)
            sp.wait_ge(spans, 1)
            sp.dma_start(dram["group_lo"].rearrange("a (p q) -> (a p) q", p=PG), lo4[:]).then_inc(spans_out, 16)
            sp.dma_start(dram["group_extra"].rearrange("a (p q) -> (a p) q", p=PG), extra4[:]).then_inc(spans_out, 16)
            sp.wait_ge(spans_out, 32)
            sp.dma_start(lo_row[:], dram["group_lo"]).then_inc(spans_in, 16)
            sp.dma_start(extra_row[:], dram["group_extra"]).then_inc(spans_in, 16)
            sp.dma_start(lo0[:], dram["group_lo"][:, 0:1].broadcast_to([P, 1])).then_inc(spans_in, 16)
            sp.wait_ge(listed, 1)
            sp.dma_start(dram["group_end"], end_row[:]).then_inc(steps_out, 16)
            sp.dma_start(dram["group_step"], step_row[:]).then_inc(steps_out, 16)
            sp.wait_ge(steps_out, 32)
            sp.dma_start(end_all[:], dram["group_end"].broadcast_to([P, NG])).then_inc(steps_in, 16)
            sp.dma_start(step_all[:], dram["group_step"].broadcast_to([P, NG])).then_inc(steps_in, 16)
            sp.wait_ge(items, 1)
            sp.wait_ge(iotas, 1)
            several = sp.value_load(ctl[0:1, 1:2], min_val=0, max_val=1)
            with sp.If(several == 1):
                sp.dma_start(dram["item_group"].rearrange("a (p j) -> (a p) j", p=P), group_int[:]).then_inc(items_out, 16)
                sp.dma_start(dram["item_base"].rearrange("a (p j) -> (a p) j", p=P), base_int[:]).then_inc(items_out, 16)
                sp.dma_start(dram["sum_base"][:, SUM_LAG:SUM_LAG + P * J].rearrange("a (p j) -> (a p) j", p=P),
                             base_int[:]).then_inc(items_out, 16)
                sp.dma_start(dram["item_base_f"].rearrange("a (p j) -> (a p) j", p=P), base_f[:]).then_inc(items_out, 16)
            with sp.Else():
                sp.dma_start(dram["item_group"][:, 0:NG], group_row[:]).then_inc(items_out, 16)
                sp.dma_start(dram["item_base"][:, 0:NG], lo_row[:]).then_inc(items_out, 16)
                sp.dma_start(dram["sum_base"][:, SUM_LAG:SUM_LAG + NG], lo_row[:]).then_inc(items_out, 16)
                sp.dma_start(dram["item_base_f"][:, 0:NG], lo_row_f[:]).then_inc(items_out, 16)
            sp.dma_start(dram["sum_base"][:, 0:SUM_LAG], first[:]).then_inc(items_out, 16)
            sp.wait_ge(unit, 1)
            sp.dma_start(dram["y_edges"], vec.rearrange("p c k -> p (c k)")).then_inc(edges_out, 16)
            for b in range(NB):
                sp.wait_ge(masked, b + 1)
                sp.dma_start(dram["emb_edges"][b:b + 1, :].rearrange("a (p c) -> (a p) c", p=P),
                             emb[:, b % 2, :]).then_inc(emb_out[b % 2], 16)
            sp.wait_ge(items_out, 16 * 5)
            sp.wait_ge(edges_out, 16)
            sp.wait_ge(steps_in, 32)
            sp.wait_ge(const_in, 16)
            for s in emb_out:
                sp.wait_ge(s, 16 * NB // 2)

        @block.gpsimd
        def _(pool):
            nc.gpsimd.iota(group_row[:], [[1, NG]], base=0, channel_multiplier=0)
            nc.gpsimd.iota(slot[:], [[1, J]], base=0, channel_multiplier=J, allow_small_or_imprecise_dtypes=True)
            nc.gpsimd.iota(centers[:], [[-1, NB]], base=0, channel_multiplier=0, allow_small_or_imprecise_dtypes=True)
            nc.gpsimd.iota(iota[:], [[1, P]], base=0, channel_multiplier=0,
                           allow_small_or_imprecise_dtypes=True).then_inc(iotas, 1)

        @block.vector
        def _(dve):
            done = [0]

            def then(instruction):
                done[0] += 1
                instruction.then_inc(chain, 1)
                dve.wait_ge(chain, done[0])

            nc.vector.memset(eps[:], EPS)
            nc.vector.memset(first[:], 0)
            nc.vector.memset(ones[:], 1.0)
            dve.wait_ge(dst_in, 16)
            nc.vector.tensor_reduce(lo4[:], dst_rows[:], AX.X, ALU.min)
            then(nc.vector.tensor_reduce(hi4[:], dst_rows[:], AX.X, ALU.max))
            then(nc.vector.tensor_tensor(span4[:], hi4[:], lo4[:], ALU.subtract))
            nc.vector.tensor_scalar(extra4[:], span4[:], P.bit_length() - 1, None, ALU.arith_shift_right).then_inc(spans, 1)
            dve.wait_ge(spans_in, 48)
            nc.vector.tensor_copy(lo_row_f[:], lo_row[:])
            then(nc.vector.tensor_scalar(count[:], extra_row[:], 1.0, None, ALU.add))
            then(nc.vector.tensor_tensor_scan(end_row[:], ones[:], count[:], 0.0, ALU.mult, ALU.add))
            then(nc.vector.tensor_tensor(start_row[:], end_row[:], count[:], ALU.subtract))
            then(nc.vector.scalar_tensor_tensor(out=shift_row[:], in0=start_row[:], scalar=-float(P), in1=lo_row[:],
                                                op0=ALU.mult, op1=ALU.add))
            nc.vector.memset(step_row[0:1, NG - 1:NG], 0.0)
            nc.vector.tensor_tensor(step_row[0:1, 0:NG - 1], shift_row[0:1, 1:NG], shift_row[0:1, 0:NG - 1], ALU.subtract)
            then(nc.vector.tensor_scalar(total[0:1, 0:1], end_row[0:1, NG - 1:NG], -1.0, None, ALU.add))
            nc.vector.tensor_scalar(ctl[0:1, 0:1], total[0:1, 0:1], UNROLL.bit_length() - 1, None, ALU.arith_shift_right)
            then(nc.vector.tensor_scalar(ctl[0:1, 1:2], end_row[0:1, NG - 1:NG], float(NG), None, ALU.is_gt))
            nc.vector.memset(ctl[0:1, 2:4], 0).then_inc(listed, 1)
            several = dve.value_load(ctl[0:1, 1:2], min_val=0, max_val=1)
            dve.wait_ge(steps_in, 32)
            dve.wait_ge(iotas, 1)
            with dve.If(several == 1):
                nc.vector.memset(group_of[:], 0.0)
                nc.vector.tensor_scalar(base_of[:], slot[:], float(P), lo0[:, 0:1], ALU.mult, ALU.add).then_inc(chain, 1)
                dve.wait_ge(chain, done[0] + 1)
                with dve.Fori(0, NG) as g:
                    nc.vector.tensor_scalar(passed[:], slot[:], end_all[:, bass.ds(g, 1)], step_all[:, bass.ds(g, 1)],
                                            ALU.is_ge, ALU.mult)
                    nc.vector.scalar_tensor_tensor(out=group_of[:], in0=slot[:], scalar=end_all[:, bass.ds(g, 1)],
                                                   in1=group_of[:], op0=ALU.is_ge, op1=ALU.add).then_inc(chain, 1)
                    dve.wait_ge(chain, 2 * g + done[0] + 2)
                    nc.vector.tensor_tensor(base_of[:], base_of[:], passed[:], ALU.add).then_inc(chain, 1)
                    dve.wait_ge(chain, 2 * g + done[0] + 3)
                after = done[0] + 1 + 2 * NG
                nc.vector.tensor_scalar(live[:], slot[:], end_all[:, NG - 1:NG], None, ALU.is_lt)
                nc.vector.tensor_scalar(base_of[:], base_of[:], -float(NP - P), None, ALU.add).then_inc(chain, 1)
                dve.wait_ge(chain, after + 1)
                nc.vector.tensor_tensor(group_int[:], group_of[:], live[:], ALU.mult)
                nc.vector.tensor_tensor(base_of[:], base_of[:], live[:], ALU.mult).then_inc(chain, 1)
                dve.wait_ge(chain, after + 2)
                nc.vector.tensor_scalar(base_int[:], base_of[:], float(NP - P), None, ALU.add)
                nc.vector.tensor_scalar(base_f[:], base_of[:], float(NP - P), None, ALU.add).then_inc(chain, 1)
                dve.wait_ge(chain, after + 3)
            nc.vector.memset(ones[0:1, 0:1], 1.0).then_inc(items, 1)
            dve.wait_ge(edges_in, 32)
            nc.vector.tensor_scalar(inside, dist, 1.0, float(NB) ** 0.5, ALU.is_le, ALU.mult).then_inc(clipped, 1)
            dve.wait_ge(clipped, 1)
            nc.vector.tensor_scalar(dist, dist, 0.0, 1.0, ALU.max, ALU.min).then_inc(clipped, 1)
            sq = emb[:, 0, :]
            for k in range(3):
                if k:
                    nc.vector.tensor_tensor(emb[:, 1, :], vec[:, :, k], vec[:, :, k], ALU.mult).then_inc(squared, 1)
                    dve.wait_ge(squared, 2 * k)
                    nc.vector.tensor_tensor(sq, sq, emb[:, 1, :], ALU.add).then_inc(squared, 1)
                else:
                    nc.vector.tensor_tensor(sq, vec[:, :, k], vec[:, :, k], ALU.mult).then_inc(squared, 1)
                dve.wait_ge(squared, 2 * k + 1)
            dve.wait_ge(rooted, 1)
            nc.vector.tensor_scalar(norm, norm, 1e-12, None, ALU.add).then_inc(summed, 1)
            dve.wait_ge(summed, 1)
            nc.vector.reciprocal(norm, norm).then_inc(summed, 1)
            dve.wait_ge(summed, 2)
            nc.vector.tensor_scalar(norm, norm, SQ3, None, ALU.mult).then_inc(summed, 1)
            dve.wait_ge(summed, 3)
            nc.vector.tensor_tensor(vec, vec, norm.unsqueeze(2).broadcast_to([P, C, 3]), ALU.mult).then_inc(unit, 1)
            for b in range(NB):
                dve.wait_ge(bell, b + 1)
                nc.vector.tensor_tensor(emb[:, b % 2, :], emb[:, b % 2, :], inside, ALU.mult).then_inc(masked, 1)

        @block.scalar
        def _(act):
            act.wait_ge(squared, 5)
            nc.scalar.activation(norm, emb[:, 0, :], ACT.Sqrt).then_inc(rooted, 1)
            act.wait_ge(rooted, 1)
            act.wait_ge(clipped, 2)
            act.wait_ge(iotas, 1)
            for b in range(NB):
                if b >= 2:
                    act.wait_ge(emb_out[b % 2], 16 * (b // 2))
                nc.scalar.activation(emb[:, b % 2, :], dist, ACT.Square, bias=centers[:, b:b + 1],
                                     scale=float(NB - 1)).then_inc(shifted, 1)
                act.wait_ge(shifted, b + 1)
                nc.scalar.activation(emb[:, b % 2, :], emb[:, b % 2, :], ACT.Exp, scale=-0.5).then_inc(bell, 1)


def node_tables(nc, io, dram, keep, NP):
    ident = keep["ident"]
    NQ = NP // QUAD
    LAST = 2
    with ExitStack() as ctx:
        def sb(name, shape, dt):
            return ctx.enter_context(nc.sbuf_tensor("tables_" + name, shape, dt))

        def pb(name, shape):
            return ctx.enter_context(nc.psum_tensor("tables_" + name, shape, F32))

        def sem(name):
            return ctx.enter_context(nc.semaphore("tables_" + name))

        wab = sb("wab", [P, 2, D], F32)
        b1 = sb("b1", [P, 1, D], F32)
        gate_b = sb("gate_b", [P, 1], F32)
        means = sb("means", [P, 3], F32)
        x = sb("x", [P, 2, 4, D], F32)
        stats = sb("stats", [P, 4, 6], F32)
        mv = sb("mv", [P, 4, 2], F32)
        rstd = sb("rstd", [P, 4], F32)
        neg = sb("neg", [P, 4], F32)
        h = sb("h", [P, 4, D], F32)
        hT = sb("hT", [P, 2, QUAD], F32)
        a_out = sb("a_out", [P, 2, 4, D + 1], F32)
        b_f32 = sb("b_f32", [P, 4, D], F32)
        rest = sb("rest", [P, 2, 4, D], F32)
        b_out = sb("b_out", [P, 2, 4, SPLITS, D], BF16)
        hT_ps = pb("hT_ps", [P, 4, D])
        ab_ps = pb("ab_ps", [P, 4, 2, D])

        w_in, centred, chain, zeroed = sem("w_in"), sem("centred"), sem("chain"), sem("zeroed")
        x_in = [sem("x_in0"), sem("x_in1")]
        a_stored = [sem("a_stored0"), sem("a_stored1")]
        b_stored = [sem("b_stored0"), sem("b_stored1")]
        hT_stored = [sem("hT_stored0"), sem("hT_stored1")]
        joining = sem("joining")
        measured, moments, scaled, offset, relued = (sem(n) for n in ("measured", "moments", "scaled", "offset", "relued"))
        turned, hT_ready, multiplied, a_ready, b_read = (sem(n) for n in ("turned", "hT_ready", "multiplied", "a_ready", "b_read"))
        part0, rest0, part1, rest1, part2 = (sem(n) for n in ("part0", "rest0", "part1", "rest1", "part2"))
        block = ctx.enter_context(nc.Block())

        def over_quads(eng, step, lag):
            for q in range(2):
                step(q, q)
            if NQ // 2 > 1:
                with eng.Fori(1, NQ // 2) as k:
                    step(2 * k, 0)
                    step(2 * k + 1, 1)
            for q in range(max(2, NQ - NQ % 2), NQ + lag):
                step(q, q % 2)

        def use(q, s):
            return q // 2 + 1 if isinstance(q, int) else (q - s) // 2 + 1

        def valid(q):
            return not isinstance(q, int) or 0 <= q < NQ

        @block.sync
        def _(sp):
            sp.dma_start(wab[:], io["w1_nodes"]).then_inc(w_in, 16)
            sp.dma_start(b1[:, 0, :], io["b1"].broadcast_to([P, D])).then_inc(w_in, 16)
            sp.dma_start(gate_b[:], io["gate_b"].broadcast_to([P, 1])).then_inc(w_in, 16)

            def step(q, s):
                if valid(q):
                    if reached(q, 2):
                        sp.wait_ge(relued, q - 1)
                    sp.dma_start(x[:, s], io["x"][bass.ds(q * QUAD, QUAD), :].rearrange("(t p) d -> p t d", p=P)).then_inc(x_in[s], 16)
                if valid(q - LAST):
                    r = q - LAST
                    sp.wait_ge(hT_ready, r + 1)
                    sp.dma_start(dram["hT_nodes"][:, bass.ds(r * QUAD, QUAD)], hT[:, s]).then_inc(hT_stored[s], 16)
                    sp.wait_ge(a_ready, r + 1)
                    sp.dma_start(dram["a_table"][bass.ds(r * QUAD, QUAD), :].rearrange("(t p) d -> p t d", p=P),
                                 a_out[:, s]).then_inc(a_stored[s], 16)
                    sp.wait_ge(part2, r + 1)
                    sp.dma_start(dram["b_table"][bass.ds(r * QUAD, QUAD), :].rearrange("(t p) d -> p t d", p=P),
                                 b_out[:, s].rearrange("p t k d -> p t (k d)")).then_inc(b_stored[s], 16)

            over_quads(sp, step, LAST)
            for s in range(2):
                uses = (NQ + 1 - s) // 2
                for stored in (hT_stored, a_stored, b_stored):
                    sp.wait_ge(stored[s], 16 * uses)

        @block.vector
        def _(dve):
            dve.wait_ge(w_in, 48)
            nc.vector.tensor_reduce(means[:, 0:2], wab[:], AX.X, ALU.add)
            nc.vector.tensor_reduce(means[:, 2:3], b1[:], AX.X, ALU.add).then_inc(chain, 1)
            dve.wait_ge(chain, 1)
            nc.vector.tensor_scalar(means[:], means[:], 1.0 / D, None, ALU.mult).then_inc(chain, 1)
            dve.wait_ge(chain, 2)
            for k in range(2):
                nc.vector.tensor_scalar(wab[:, k, :], wab[:, k, :], means[:, k:k + 1], None, ALU.subtract)
            nc.vector.tensor_scalar(b1[:, 0, :], b1[:, 0, :], means[:, 2:3], None, ALU.subtract)
            for s in range(2):
                for t in range(4):
                    last = nc.vector.tensor_copy(a_out[:, s, t, D:D + 1], gate_b[:])
            last.then_inc(centred, 1)
            dve.wait_ge(centred, 1)

            def step(q, s):
                if valid(q):
                    dve.wait_ge(x_in[s], 16 * use(q, s))
                    if reached(q, 1):
                        dve.wait_ge(offset, q)
                    for t in range(4):
                        last = nc.vector.bn_stats(stats[:, t, :], x[:, s, t, :])
                    last.then_inc(measured, 1)
                    dve.wait_ge(measured, q + 1)
                    dve.sem_inc(joining, 1)
                    for t in range(4):
                        last = nc.vector.bn_aggr(mv[:, t, :], stats[:, t, :])
                    last.then_inc(moments, 1)
                    dve.wait_ge(moments, q + 1)
                    dve.wait_ge(scaled, 2 * q + 2)
                    if reached(q, 1):
                        dve.wait_ge(relued, q)
                    nc.vector.scalar_tensor_tensor(out=neg[:], in0=mv[:, :, 0], scalar=-1.0, in1=rstd[:],
                                                   op0=ALU.mult, op1=ALU.mult).then_inc(offset, 1)
                if valid(q - 1):
                    r, z = q - 1, 1 - s
                    dve.wait_ge(turned, r + 1)
                    if reached(r, 2):
                        dve.wait_ge(multiplied, r - 1)
                        dve.wait_ge(hT_stored[z], 16 * (use(r, z) - 1))
                    nc.vector.tensor_copy(hT[:, z], hT_ps[:].rearrange("p t d -> p (t d)")).then_inc(hT_ready, 1)
                    dve.wait_ge(multiplied, r + 1)
                    if reached(r, 2):
                        dve.wait_ge(a_stored[z], 16 * (use(r, z) - 1))
                    if reached(r, 1):
                        dve.wait_ge(rest0, r)
                        dve.wait_ge(part0, r)
                    nc.vector.tensor_copy(b_f32[:], ab_ps[:, :, 1, :])
                    nc.vector.tensor_tensor(a_out[:, z, :, 0:D], ab_ps[:, :, 0, :],
                                            b1[:].broadcast_to([P, 4, D]), ALU.add).then_inc(a_ready, 1)

            over_quads(dve, step, 1)

        @block.scalar
        def _(act):
            nc.scalar.preload_act_table_set("natural_log_exp_and_others")

            def step(q, s):
                if valid(q):
                    act.wait_ge(moments, q + 1)
                    if reached(q, 1):
                        act.wait_ge(relued, q)
                    nc.scalar.activation(rstd[:], mv[:, :, 1], ACT.Ln, bias=keep["eps"][:]).then_inc(scaled, 1)
                    act.wait_ge(scaled, 2 * q + 1)
                    nc.scalar.activation(rstd[:], rstd[:], ACT.Exp, scale=-0.5).then_inc(scaled, 1)
                    act.wait_ge(scaled, 2 * q + 2)
                    act.wait_ge(offset, q + 1)
                    if reached(q, 1):
                        act.wait_ge(turned, q)
                    for t in range(4):
                        last = nc.scalar.activation(h[:, t, :], x[:, s, t, :], ACT.Relu, bias=neg[:, t:t + 1],
                                                    scale=rstd[:, t:t + 1])
                    last.then_inc(relued, 1)
                if valid(q - 1):
                    r, z = q - 1, 1 - s
                    act.wait_ge(a_ready, r + 1)
                    if reached(r, 2):
                        act.wait_ge(b_stored[z], 16 * (use(r, z) - 1))
                    nc.scalar.copy(b_out[:, z, :, 0, :], b_f32[:]).then_inc(part0, 1)
                    act.wait_ge(rest0, r + 1)
                    nc.scalar.copy(b_out[:, z, :, 1, :], rest[:, 0]).then_inc(part1, 1)
                    act.wait_ge(rest1, r + 1)
                    nc.scalar.copy(b_out[:, z, :, 2, :], rest[:, 1]).then_inc(part2, 1)

            over_quads(act, step, 1)

        @block.gpsimd
        def _(pool):
            nc.gpsimd.memset(keep["agg"][:], 0.0).then_inc(zeroed, 1)

            def step(q, s):
                pool.wait_ge(part0, q + 1)
                if reached(q, 1):
                    pool.wait_ge(part1, q)
                    pool.wait_ge(rest1, q)
                nc.gpsimd.tensor_tensor(rest[:, 0], b_f32[:], b_out[:, s, :, 0, :], ALU.subtract).then_inc(rest0, 1)
                pool.wait_ge(rest0, q + 1)
                pool.wait_ge(part1, q + 1)
                if reached(q, 1):
                    pool.wait_ge(part2, q)
                nc.gpsimd.tensor_tensor(rest[:, 1], rest[:, 0], b_out[:, s, :, 1, :], ALU.subtract).then_inc(rest1, 1)

            over_quads(pool, step, 0)
            pool.wait_ge(zeroed, 1)

        @block.tensor
        def _(pe):
            def step(q, s):
                if valid(q):
                    pe.wait_ge(relued, q + 1)
                    if reached(q, 1):
                        pe.wait_ge(hT_ready, q)
                    for t in range(4):
                        last = nc.tensor.transpose(hT_ps[:, t, :], h[:, t, :], ident[:])
                    last.then_inc(turned, 1)
                if valid(q - 1):
                    r, z = q - 1, 1 - s
                    pe.wait_ge(hT_ready, r + 1)
                    if reached(r, 1):
                        pe.wait_ge(a_ready, r)
                    for t in range(4):
                        last = nc.tensor.matmul(ab_ps[:, t].rearrange("p k d -> p (k d)"), hT[:, z, t * P:(t + 1) * P],
                                                wab[:].rearrange("p k d -> p (k d)"), start=True, stop=True)
                    last.then_inc(multiplied, 1)

            pe.wait_ge(centred, 1)
            over_quads(pe, step, 1)


def over_items(eng, step, passes, lag):
    for u in range(UNROLL):
        step(u, u, -1)
    with eng.Fori(1, passes) as k:
        for u in range(UNROLL):
            step(k * UNROLL + u, u, -1)
    for u in range(lag):
        step(passes * UNROLL + u, u % UNROLL, u)


def load_pass(nc, engine, table, item, count, highest):
    return nc.values_load_multi_w_load_instructions(
        table[0:1, bass.ds(item, count)], engines=(engine,), min_val=0, max_val=highest,
        skip_runtime_bounds_check_because="prepare() keeps the list of items within these bounds")[1]


def stage(item, drained, lag):
    return drained < lag and reached(item, lag)


def gated_edges(nc, io, dram, keep, NP, NG, J):
    agg, iota, ident, ctl = keep["agg"], keep["iota"], keep["ident"], keep["ctl"]
    PRE = D + 1
    MIN_PASSES, MAX_PASSES = NG // UNROLL, P * J // UNROLL
    with ExitStack() as ctx:
        def sb(name, shape, dt):
            return ctx.enter_context(nc.sbuf_tensor("gated_" + name, shape, dt))

        def pb(name, shape):
            return ctx.enter_context(nc.psum_tensor("gated_" + name, shape, F32))

        def sem(name):
            return ctx.enter_context(nc.semaphore("gated_" + name))

        w_edge = sb("w_edge", [P, 2, PRE], F32)
        w_mean = sb("w_mean", [P, 2], F32)
        ln_g = sb("ln_g", [P, D], F32)
        ln_b = sb("ln_b", [P, 1, D], F32)
        meta = sb("meta", [P, UNROLL, 2 * TILES], I32)
        base = sb("base", [P, UNROLL], F32)
        feat = sb("feat", [P, UNROLL, GROUP // 2], F32)
        b_win = sb("b_win", [P, UNROLL, SPLITS * D], BF16)
        gath = sb("gath", [P, UNROLL, TILES, PRE], F32)
        by_node = sb("by_node", [P, 2, GROUP], BF16)
        by_edge = sb("by_edge", [P, UNROLL, TILES, P], F32)
        pre = sb("pre", [P, 2, TILES, PRE], F32)
        junk = sb("junk", [P, D], F32)
        ss = sb("ss", [P, TILES], F32)
        rstd = sb("rstd", [P, 2, TILES], F32)
        gexp = sb("gexp", [P, 2, TILES], F32)
        gate = sb("gate", [P, 2, TILES], F32)
        normed = sb("normed", [P, 2, TILES, D], F32)
        msg = sb("msg", [P, 2, TILES, D], F32)
        turned_ps = [pb(f"turned_ps{i}", [P, GROUP]) for i in range(2)]
        pre_ps = [pb(f"pre_ps{i}", [P, 2, 512]) for i in range(2)]
        agg_ps = [pb(f"agg_ps{i}", [P, 512]) for i in range(2)]

        w_in, centred, chain = sem("w_in"), sem("centred"), sem("chain")
        meta_in, edge_in, gathered, base_in, started = (keep[k] for k in ("meta_in", "edge_in", "gathered", "base_in", "started"))
        by_edge_built, turned, by_node_built = sem("by_edge_built"), sem("turned"), sem("by_node_built")
        pre_mm, pre_summed, squares, logs, measured = (sem(n) for n in ("pre_mm", "pre_summed", "squares", "logs", "measured"))
        scaled, normed_s, gated, msg_ready, agg_mm, acc_done = (sem(n) for n in ("scaled", "normed", "gated", "msg_ready", "agg_mm", "acc_done"))
        block = ctx.enter_context(nc.Block())

        def use(item, u):
            return item // UNROLL + 1 if isinstance(item, int) else (item - u) // UNROLL + 1

        @block.sync
        def _(sp):
            sp.dma_start(w_edge[:], io["w1_edges"]).then_inc(w_in, 16)
            sp.dma_start(ln_g[:], io["ln_g"].broadcast_to([P, D])).then_inc(w_in, 16)
            sp.dma_start(ln_b[:, 0, :], io["ln_b"].broadcast_to([P, D])).then_inc(w_in, 16)
            passes = sp.value_load(ctl[0:1, 0:1], min_val=MIN_PASSES - 1, max_val=MAX_PASSES - 1) + 1

            loaded = {}

            def step(w, u, drained):
                if u == 0:
                    loaded["group"] = load_pass(nc, mybir.EngineType.SP, dram["item_group"], w, UNROLL, NG - 1)
                    loaded["base"] = load_pass(nc, mybir.EngineType.SP, dram["item_base"], w, UNROLL, NP - P)
                g, first = loaded["group"][u], loaded["base"][u]
                if u % BATCH == 0:
                    if reached(w, UNROLL):
                        sp.wait_ge(by_edge_built, w - UNROLL + BATCH)
                    sp.dma_start(base[:, u:u + BATCH],
                                 dram["item_base_f"][0:1, bass.ds(w, BATCH)].broadcast_to([P, BATCH])).then_inc(base_in[u // BATCH], 16)
                if reached(w, UNROLL):
                    sp.wait_ge(pre_summed, w - UNROLL + 1)
                sp.dma_start(meta[:, u], io["meta"][bass.ds(g, 1)].rearrange("a p k -> (a p) k")).then_inc(meta_in[u], 16)
                sp.dma_start(feat[:, u], io["edge_feat"][bass.ds(g, 1)].rearrange("a p k -> (a p) k")).then_inc(edge_in[u], 16)
                sp.dma_start(b_win[:, u], dram["b_table"][bass.ds(first, P), :]).then_inc(edge_in[u], 16)

            over_items(sp, step, passes, 0)

        @block.gpsimd
        def _(pool):
            passes = pool.value_load(ctl[0:1, 0:1], min_val=MIN_PASSES - 1, max_val=MAX_PASSES - 1) + 1

            def step(w, u, drained):
                pool.wait_ge(meta_in[u], 16 * use(w, u))
                if reached(w, UNROLL):
                    pool.wait_ge(pre_summed, w - UNROLL + 1)
                pool.sem_inc(started, 1)
                for i in range(TILES):
                    nc.gpsimd.indirect_dma_start(
                        gath[:, u, i, :], None, dram["a_table"],
                        bass.IndirectOffsetOnAxis(ap=meta[:, u, i:i + 1], axis=0)).then_inc(gathered[u], 16)

            over_items(pool, step, passes, 0)

        @block.tensor
        def _(pe):
            passes = pe.value_load(ctl[0:1, 0:1], min_val=MIN_PASSES - 1, max_val=MAX_PASSES - 1) + 1
            pe.wait_ge(centred, 1)

            def step(w, u, drained):
                if stage(w, drained, 1):
                    r, v, z = w - 1, (u - 1) % 2, (u - 1) % UNROLL
                    pe.wait_ge(by_edge_built, r + 1)
                    if reached(r, 2):
                        pe.wait_ge(by_node_built, r - 1)
                    for i in range(TILES):
                        last = nc.tensor.transpose(turned_ps[v][:, i * P:(i + 1) * P], by_edge[:, z, i, :], ident[:])
                    last.then_inc(turned, 1)
                if stage(w, drained, 5):
                    r, v, z = w - 5, (u - 5) % 2, (u - 5) % UNROLL
                    pe.wait_ge(msg_ready, r + 1)
                    if reached(r, 2):
                        pe.wait_ge(acc_done, r - 1)
                    for i in range(TILES):
                        nc.tensor.matmul(agg_ps[v][:, 0:P], msg[:, v, i, :], by_edge[:, z, i, :],
                                         start=(i == 0), stop=(i == TILES - 1))
                    for i in range(TILES):
                        last = nc.tensor.matmul(agg_ps[v][0:1, P:2 * P], gate[:, v, i:i + 1], by_edge[:, z, i, :],
                                                start=(i == 0), stop=(i == TILES - 1))
                    last.then_inc(agg_mm, 1)
                if stage(w, drained, 2):
                    r, v, z = w - 2, u % 2, (u - 2) % UNROLL
                    pe.wait_ge(edge_in[z], 32 * use(r, z))
                    if reached(r, 2):
                        pe.wait_ge(pre_summed, r - 1)
                    for t in range(2):
                        nc.tensor.matmul(pre_ps[v][:, t, 0:2 * PRE], feat[:, z, t * P:(t + 1) * P],
                                         w_edge[:].rearrange("p h d -> p (h d)"), start=True, stop=False)
                        if t == 0:
                            pe.wait_ge(by_node_built, r + 1)
                        for half in range(2):
                            i = 2 * t + half
                            for k in range(SPLITS):
                                last = nc.tensor.matmul(pre_ps[v][:, t, half * PRE:half * PRE + D],
                                                        by_node[:, v, i * P:(i + 1) * P], b_win[:, z, k * D:(k + 1) * D],
                                                        start=False, stop=(half == 1 and k == SPLITS - 1))
                    last.then_inc(pre_mm, 1)

            over_items(pe, step, passes, SUM_LAG)

        @block.vector
        def _(dve):
            passes = dve.value_load(ctl[0:1, 0:1], min_val=MIN_PASSES - 1, max_val=MAX_PASSES - 1) + 1
            dve.wait_ge(w_in, 48)
            nc.vector.tensor_reduce(w_mean[:], w_edge[:, :, 0:D], AX.X, ALU.add).then_inc(chain, 1)
            dve.wait_ge(chain, 1)
            nc.vector.tensor_scalar(w_mean[:], w_mean[:], 1.0 / D, None, ALU.mult).then_inc(chain, 1)
            dve.wait_ge(chain, 2)
            for half in range(2):
                last = nc.vector.tensor_scalar(w_edge[:, half, 0:D], w_edge[:, half, 0:D], w_mean[:, half:half + 1],
                                               None, ALU.subtract)
            last.then_inc(centred, 1)
            loaded = {}

            def step(w, u, drained):
                if u == 0:
                    loaded["first"] = load_pass(nc, mybir.EngineType.DVE, dram["sum_base"], w,
                                                UNROLL if drained < 0 else SUM_LAG, NP - P)
                if stage(w, drained, 3):
                    r, v, z = w - 3, (u - 3) % 2, (u - 3) % UNROLL
                    dve.wait_ge(pre_mm, r + 1)
                    dve.wait_ge(gathered[z], 16 * TILES * use(r, z))
                    if reached(r, 2):
                        dve.wait_ge(normed_s, r - 1)
                    nc.vector.tensor_tensor(
                        pre[:, v].rearrange("p (t h) d -> p t h d", h=2),
                        pre_ps[v][:, :, 0:2 * PRE].rearrange("p t (h d) -> p t h d", h=2),
                        gath[:, z].rearrange("p (t h) d -> p t h d", h=2), ALU.add).then_inc(pre_summed, 1)
                if stage(w, drained, 4):
                    r, v = w - 4, u % 2
                    dve.wait_ge(measured, r + 1)
                    if reached(r, 2):
                        dve.wait_ge(msg_ready, r - 1)
                        dve.wait_ge(agg_mm, r - 1)
                    nc.vector.tensor_scalar(gate[:, v], gexp[:, v], 1.0, None, ALU.add).then_inc(gated, 1)
                    for i in range(TILES):
                        last = nc.vector.scalar_tensor_tensor(out=normed[:, v, i, :], in0=pre[:, v, i, 0:D],
                                                              scalar=rstd[:, v, i:i + 1], in1=ln_g[:],
                                                              op0=ALU.mult, op1=ALU.mult)
                    last.then_inc(scaled, 1)
                    dve.wait_ge(gated, 2 * r + 1)
                    nc.vector.reciprocal(gate[:, v], gate[:, v]).then_inc(gated, 1)
                    dve.wait_ge(scaled, r + 1)
                    nc.vector.tensor_tensor(normed[:, v], normed[:, v], ln_b[:].broadcast_to([P, TILES, D]),
                                            ALU.add).then_inc(normed_s, 1)
                if stage(w, drained, 0):
                    dve.wait_ge(meta_in[u], 16 * use(w, u))
                    dve.wait_ge(base_in[u // BATCH], 16 * use(w, u))
                    if reached(w, UNROLL):
                        dve.wait_ge(agg_mm, w - UNROLL + 1)
                    nc.vector.scalar_tensor_tensor(
                        out=by_edge[:, u], in0=iota[:].unsqueeze(1).broadcast_to([P, TILES, P]), scalar=base[:, u:u + 1],
                        in1=meta[:, u, TILES:2 * TILES].unsqueeze(2).broadcast_to([P, TILES, P]),
                        op0=ALU.add, op1=ALU.is_equal).then_inc(by_edge_built, 1)
                if stage(w, drained, SUM_LAG):
                    r, v, first = w - SUM_LAG, u % 2, loaded["first"][u]
                    dve.wait_ge(agg_mm, r + 1)
                    if reached(r, 1):
                        dve.wait_ge(acc_done, r)
                    nc.vector.tensor_tensor(agg[0:1, 1, bass.ds(first, P)], agg[0:1, 1, bass.ds(first, P)],
                                            agg_ps[v][0:1, P:2 * P], ALU.add)
                    nc.vector.tensor_tensor(agg[:, 0, bass.ds(first, P)], agg[:, 0, bass.ds(first, P)],
                                            agg_ps[v][:, 0:P], ALU.add).then_inc(acc_done, 1)

            over_items(dve, step, passes, SUM_LAG)

        @block.scalar
        def _(act):
            nc.scalar.preload_act_table_set("natural_log_exp_and_others")
            passes = act.value_load(ctl[0:1, 0:1], min_val=MIN_PASSES - 1, max_val=MAX_PASSES - 1) + 1

            def step(w, u, drained):
                if stage(w, drained, 1):
                    r, v = w - 1, (u - 1) % 2
                    act.wait_ge(turned, r + 1)
                    if reached(r, 2):
                        act.wait_ge(pre_mm, r - 1)
                    nc.scalar.copy(by_node[:, v], turned_ps[v][:]).then_inc(by_node_built, 1)
                if stage(w, drained, 3):
                    r, v = w - 3, (u - 3) % 2
                    act.wait_ge(pre_summed, r + 1)
                    if reached(r, 2):
                        act.wait_ge(normed_s, r - 1)
                        act.wait_ge(gated, 2 * r - 2)
                    if reached(r, 1):
                        act.wait_ge(measured, r)
                    for i in range(TILES):
                        if i or reached(r, 1):
                            act.wait_ge(squares, TILES * r + i)
                        nc.scalar.activation(junk[:], pre[:, v, i, 0:D], ACT.Square,
                                             accum_out=ss[:, i:i + 1]).then_inc(squares, 1)
                    nc.scalar.activation(gexp[:, v], pre[:, v, :, D], ACT.Exp, scale=-1.0)
                    act.wait_ge(squares, TILES * (r + 1))
                    nc.scalar.activation(rstd[:, v], ss[:], ACT.Ln, bias=keep["eps"][:], scale=1.0 / D).then_inc(logs, 1)
                    act.wait_ge(logs, r + 1)
                    nc.scalar.activation(rstd[:, v], rstd[:, v], ACT.Exp, scale=-0.5).then_inc(measured, 1)
                if stage(w, drained, 4):
                    r, v = w - 4, u % 2
                    act.wait_ge(normed_s, r + 1)
                    act.wait_ge(gated, 2 * r + 2)
                    if reached(r, 2):
                        act.wait_ge(agg_mm, r - 1)
                    for i in range(TILES):
                        last = nc.scalar.activation(msg[:, v, i, :], normed[:, v, i, :], ACT.Relu,
                                                    scale=gate[:, v, i:i + 1])
                    last.then_inc(msg_ready, 1)

            over_items(act, step, passes, SUM_LAG)


def gru_nodes(nc, io, dram, keep, NP):
    agg, ident = keep["agg"], keep["ident"]
    NQ = NP // QUAD
    UP = 1.0 / float(MUL) ** 0.5
    with ExitStack() as ctx:
        def sb(name, shape, dt):
            return ctx.enter_context(nc.sbuf_tensor("gru_" + name, shape, dt))

        def pb(name):
            return ctx.enter_context(nc.psum_tensor("gru_" + name, [P, QUAD], F32))

        def sem(name):
            return ctx.enter_context(nc.semaphore("gru_" + name))

        w2 = sb("w2", [P, D], F32)
        b2 = sb("b2", [1, D], F32)
        w_ih = sb("w_ih", [P, 3 * D], F32)
        w_hh = sb("w_hh", [P, 3 * D], F32)
        b_ih = sb("b_ih", [P, 3], F32)
        b_hh = sb("b_hh", [P, 3], F32)
        b_sum = sb("b_sum", [P, 3], F32)
        w_up = sb("w_up", [P, D], F32)
        x = sb("x", [P, 2, 4, D], F32)
        hT = sb("hT", [P, 2, QUAD], F32)
        mT = sb("mT", [P, QUAD], F32)
        rT = sb("rT", [P, QUAD], F32)
        zT = sb("zT", [P, QUAD], F32)
        nT = sb("nT", [P, QUAD], F32)
        oT = sb("oT", [P, QUAD], F32)
        x1 = sb("x1", [P, 4, D], F32)
        stats = sb("stats", [P, 4, 6], F32)
        mv = sb("mv", [P, 4, 2], F32)
        rstd = sb("rstd", [P, 4], F32)
        neg = sb("neg", [P, 4], F32)
        h2 = sb("h2", [P, 4, D], F32)
        h2T = sb("h2T", [P, QUAD], F32)
        up = sb("up", [P, 4, D], F32)
        m_ps, r_ps, z_ps, i_ps, n_ps, o_ps, h_ps, u_ps = (pb(n) for n in (
            "m_ps", "r_ps", "z_ps", "i_ps", "n_ps", "o_ps", "h_ps", "u_ps"))

        w_in, biases = sem("w_in"), sem("biases")
        x_in = [sem("x_in0"), sem("x_in1")]
        hT_in = [sem("hT_in0"), sem("hT_in1")]
        m_mm, m_copied, gates_mm, rz_ready = (sem(n) for n in ("m_mm", "m_copied", "gates_mm", "rz_ready"))
        chain, n_in, n_ready, o_ready, o_turned = (sem(n) for n in ("chain", "n_in", "n_ready", "o_ready", "o_turned"))
        joining = sem("joining")
        x1_ready, measured, moments, rooted, inverted, offset, relued = (sem(n) for n in (
            "x1_ready", "measured", "moments", "rooted", "inverted", "offset", "relued"))
        h_turned, h2T_ready, u_mm, u_ready = (sem(n) for n in ("h_turned", "h2T_ready", "u_mm", "u_ready"))
        x1_stored, u_stored, cleared = sem("x1_stored"), sem("u_stored"), sem("cleared")
        block = ctx.enter_context(nc.Block())

        def over_quads(eng, step, lag):
            for q in range(4):
                step(q, q % 2)
            if NQ // 2 > 2:
                with eng.Fori(2, NQ // 2) as k:
                    step(2 * k, 0)
                    step(2 * k + 1, 1)
            for q in range(max(4, NQ - NQ % 2), NQ + lag):
                step(q, q % 2)

        def use(q, s):
            return q // 2 + 1 if isinstance(q, int) else (q - s) // 2 + 1

        def valid(q):
            return not isinstance(q, int) or 0 <= q < NQ

        def rows(table, q):
            return table[bass.ds(q * QUAD, QUAD), :].rearrange("(t p) d -> p t d", p=P)

        def flat(t):
            return t[:].rearrange("p t d -> p (t d)")

        @block.sync
        def _(sp):
            for tile, name in ((w2, "w2"), (b2, "b2"), (w_ih, "w_ih"), (w_hh, "w_hh"), (b_ih, "b_ih"), (b_hh, "b_hh"), (w_up, "w_up")):
                sp.dma_start(tile[:], io[name]).then_inc(w_in, 16)

            def step(q, s):
                if valid(q):
                    if reached(q, 2):
                        sp.wait_ge(o_ready, q - 1)
                    sp.dma_start(hT[:, s], dram["hT_nodes"][:, bass.ds(q * QUAD, QUAD)]).then_inc(hT_in[s], 16)
                    if reached(q, 2):
                        sp.wait_ge(x1_ready, q - 1)
                    sp.dma_start(x[:, s], io["x"][bass.ds(q * QUAD, QUAD), :].rearrange("(t p) d -> p t d", p=P)).then_inc(x_in[s], 16)
                if valid(q - 2):
                    sp.wait_ge(x1_ready, q - 1)
                    sp.dma_start(rows(dram["x1_nodes"], q - 2), x1[:]).then_inc(x1_stored, 16)
                if valid(q - 3):
                    sp.wait_ge(u_ready, q - 2)
                    sp.dma_start(rows(dram["u_table"], q - 3), up[:]).then_inc(u_stored, 16)

            over_quads(sp, step, 3)
            sp.wait_ge(x1_stored, 16 * NQ)
            sp.wait_ge(u_stored, 16 * NQ)

        @block.gpsimd
        def _(pool):
            pool.wait_ge(m_copied, NQ)
            nc.gpsimd.memset(agg[:], 0.0).then_inc(cleared, 1)
            pool.wait_ge(cleared, 1)

        @block.tensor
        def _(pe):
            pe.wait_ge(w_in, 16 * 7)

            def step(q, s):
                if valid(q - 2):
                    r = q - 2
                    pe.wait_ge(relued, r + 1)
                    if reached(r, 1):
                        pe.wait_ge(h2T_ready, r)
                    for t in range(4):
                        last = nc.tensor.transpose(h_ps[:, t * P:(t + 1) * P], h2[:, t, :], ident[:])
                    last.then_inc(h_turned, 1)
                if valid(q):
                    cols = bass.ds(q * QUAD, QUAD)
                    if reached(q, 1):
                        pe.wait_ge(m_copied, q)
                    nc.tensor.matmul(m_ps[:], w2[:], agg[:, 0, cols], start=True, stop=False)
                    nc.tensor.matmul(m_ps[:], b2[:], agg[0:1, 1, cols], start=False, stop=True).then_inc(m_mm, 1)
                    pe.wait_ge(hT_in[s], 16 * use(q, s))
                    if reached(q, 1):
                        pe.wait_ge(rz_ready, 2 * q)
                        pe.wait_ge(n_in, 2 * q)
                    nc.tensor.matmul(r_ps[:], w_hh[:, 0:D], hT[:, s], start=True, stop=False)
                    nc.tensor.matmul(z_ps[:], w_hh[:, D:2 * D], hT[:, s], start=True, stop=False)
                    nc.tensor.matmul(n_ps[:], w_hh[:, 2 * D:3 * D], hT[:, s], start=True, stop=True)
                    pe.wait_ge(m_copied, q + 1)
                    nc.tensor.matmul(r_ps[:], w_ih[:, 0:D], mT[:], start=False, stop=True)
                    nc.tensor.matmul(z_ps[:], w_ih[:, D:2 * D], mT[:], start=False, stop=True)
                    nc.tensor.matmul(i_ps[:], w_ih[:, 2 * D:3 * D], mT[:], start=True, stop=True).then_inc(gates_mm, 1)
                if valid(q - 2):
                    r = q - 2
                    pe.wait_ge(h2T_ready, r + 1)
                    if reached(r, 1):
                        pe.wait_ge(u_ready, r)
                    for t in range(4):
                        last = nc.tensor.matmul(u_ps[:, t * P:(t + 1) * P], h2T[:, t * P:(t + 1) * P], w_up[:], start=True, stop=True)
                    last.then_inc(u_mm, 1)
                if valid(q - 1):
                    r = q - 1
                    pe.wait_ge(o_ready, r + 1)
                    if reached(r, 1):
                        pe.wait_ge(x1_ready, r)
                    for t in range(4):
                        last = nc.tensor.transpose(o_ps[:, t * P:(t + 1) * P], oT[:, t * P:(t + 1) * P], ident[:])
                    last.then_inc(o_turned, 1)

            over_quads(pe, step, 2)

        @block.scalar
        def _(act):
            act.wait_ge(biases, 1)

            def step(q, s):
                if valid(q - 2):
                    r = q - 2
                    act.wait_ge(h_turned, r + 1)
                    if reached(r, 1):
                        act.wait_ge(u_mm, r)
                    nc.scalar.copy(h2T[:], h_ps[:]).then_inc(h2T_ready, 1)
                if valid(q):
                    act.wait_ge(m_mm, q + 1)
                    if reached(q, 1):
                        act.wait_ge(gates_mm, q)
                    nc.scalar.copy(mT[:], m_ps[:]).then_inc(m_copied, 1)
                    act.wait_ge(gates_mm, q + 1)
                    if reached(q, 1):
                        act.wait_ge(o_ready, q)
                    nc.scalar.activation(rT[:], r_ps[:], ACT.Sigmoid, bias=b_sum[:, 0:1]).then_inc(rz_ready, 1)
                    nc.scalar.activation(zT[:], z_ps[:], ACT.Sigmoid, bias=b_sum[:, 1:2]).then_inc(rz_ready, 1)
                if valid(q - 2):
                    r = q - 2
                    act.wait_ge(u_mm, r + 1)
                    if reached(r, 1):
                        act.wait_ge(u_stored, 16 * r)
                    nc.scalar.activation(flat(up), u_ps[:], ACT.Copy, scale=UP).then_inc(u_ready, 1)
                if valid(q):
                    act.wait_ge(n_in, 2 * q + 2)
                    nc.scalar.activation(nT[:], nT[:], ACT.Tanh, bias=b_ih[:, 2:3]).then_inc(n_ready, 1)
                if valid(q - 1):
                    r = q - 1
                    act.wait_ge(moments, r + 1)
                    nc.scalar.activation(rstd[:], mv[:, :, 1], ACT.Sqrt, bias=keep["eps"][:]).then_inc(rooted, 1)
                    act.wait_ge(offset, r + 1)
                    if reached(r, 1):
                        act.wait_ge(h_turned, r)
                    for t in range(4):
                        last = nc.scalar.activation(h2[:, t, :], x1[:, t, :], ACT.Relu, bias=neg[:, t:t + 1], scale=rstd[:, t:t + 1])
                    last.then_inc(relued, 1)

            over_quads(act, step, 2)

        @block.vector
        def _(dve):
            dve.wait_ge(w_in, 16 * 7)
            nc.vector.tensor_tensor(b_sum[:], b_ih[:], b_hh[:], ALU.add).then_inc(biases, 1)

            def step(q, s):
                if valid(q):
                    dve.wait_ge(rz_ready, 2 * q + 2)
                    nc.vector.scalar_tensor_tensor(out=nT[:], in0=n_ps[:], scalar=b_hh[:, 2:3], in1=rT[:],
                                                   op0=ALU.add, op1=ALU.mult).then_inc(n_in, 1)
                    dve.wait_ge(n_in, 2 * q + 1)
                    nc.vector.tensor_tensor(nT[:], nT[:], i_ps[:], ALU.add).then_inc(n_in, 1)
                if valid(q - 1):
                    r = q - 1
                    dve.wait_ge(o_turned, r + 1)
                    dve.wait_ge(x_in[1 - s], 16 * use(r, 1 - s))
                    if reached(r, 1):
                        dve.wait_ge(relued, r)
                        dve.wait_ge(x1_stored, 16 * r)
                    nc.vector.tensor_tensor(flat(x1), x[:, 1 - s].rearrange("p t d -> p (t d)"), o_ps[:], ALU.add).then_inc(x1_ready, 1)
                    dve.wait_ge(x1_ready, r + 1)
                    if reached(r, 1):
                        dve.wait_ge(offset, r)
                    for t in range(4):
                        last = nc.vector.bn_stats(stats[:, t, :], x1[:, t, :])
                    last.then_inc(measured, 1)
                    dve.wait_ge(measured, r + 1)
                    dve.sem_inc(joining, 1)
                    for t in range(4):
                        last = nc.vector.bn_aggr(mv[:, t, :], stats[:, t, :])
                    last.then_inc(moments, 1)
                if valid(q):
                    dve.wait_ge(n_ready, q + 1)
                    if reached(q, 1):
                        dve.wait_ge(o_turned, q)
                    nc.vector.tensor_tensor(oT[:], hT[:, s], nT[:], ALU.subtract).then_inc(chain, 1)
                    dve.wait_ge(chain, 2 * q + 1)
                    nc.vector.tensor_tensor(oT[:], oT[:], zT[:], ALU.mult).then_inc(chain, 1)
                    dve.wait_ge(chain, 2 * q + 2)
                    nc.vector.tensor_tensor(oT[:], oT[:], nT[:], ALU.add).then_inc(o_ready, 1)
                if valid(q - 1):
                    r = q - 1
                    dve.wait_ge(rooted, r + 1)
                    nc.vector.reciprocal(rstd[:], rstd[:]).then_inc(inverted, 1)
                    dve.wait_ge(inverted, r + 1)
                    nc.vector.scalar_tensor_tensor(out=neg[:], in0=mv[:, :, 0], scalar=-1.0, in1=rstd[:],
                                                   op0=ALU.mult, op1=ALU.mult).then_inc(offset, 1)

            over_quads(dve, step, 1)


def tensor_edges(nc, io, dram, keep, NP, NG, J):
    agg, iota, ctl = keep["agg"], keep["iota"], keep["ctl"]
    MIN_PASSES, MAX_PASSES = NG // UNROLL, P * J // UNROLL
    HALF = GROUP // 2
    KIN = 2 * NB
    VEC = slice(MUL, 4 * MUL)
    with ExitStack() as ctx:
        def sb(name, shape, dt):
            return ctx.enter_context(nc.sbuf_tensor("tensor_" + name, shape, dt))

        def pb(name, shape):
            return ctx.enter_context(nc.psum_tensor("tensor_" + name, shape, F32))

        def sem(name):
            return ctx.enter_context(nc.semaphore("tensor_" + name))

        mlp0 = sb("mlp0", [P, P], F32)
        mlp1 = sb("mlp1", [P, P], F32)
        mlp2 = sb("mlp2", [P, 2 * D], F32)
        bias0 = sb("bias0", [P, 1], F32)
        bias1 = sb("bias1", [P, 1], F32)
        bias2 = sb("bias2", [1, 2 * D], F32)
        bias2_rest = sb("bias2_rest", [1, 2 * D], F32)
        bias2_part = sb("bias2_part", [1, SPLITS, 2 * D], BF16)
        ones = sb("ones", [1, P], BF16)
        meta = sb("meta", [P, UNROLL, 2 * TILES], I32)
        base = sb("base", [P, UNROLL], F32)
        y = sb("y", [P, UNROLL, TILES, 3], F32)
        emb = sb("emb", [P, UNROLL, HALF], F32)
        gath = sb("gath", [P, UNROLL, TILES, D], F32)
        h0 = sb("h0", [P, 2, HALF], F32)
        h1 = sb("h1", [P, 2, HALF], F32)
        by_edge = sb("by_edge", [P, 2, TILES, P], F32)
        msg = sb("msg", [P, 2, TILES, MSG], F32)
        prod = sb("prod", [P, TILES, 3, MUL], F32)
        dot = sb("dot", [P, TILES, MUL], F32)
        h0_ps = pb("h0_ps", [P, 512])
        h1_ps = pb("h1_ps", [P, 512])
        w_ps = [pb(f"w_ps{i}", [P, TILES, D]) for i in range(2)]
        agg_ps = [pb(f"agg_ps{i}", [P, 512]) for i in range(4)]

        w_in, cleared, split, ready = sem("w_in"), sem("cleared"), sem("split"), sem("ready")
        meta_in, edge_in, gathered, base_in, started = (keep[k] for k in ("meta_in", "edge_in", "gathered", "base_in", "started"))
        h0_mm, h0_ready, h1_mm, h1_ready, w_mm = (sem(n) for n in ("h0_mm", "h0_ready", "h1_mm", "h1_ready", "w_mm"))
        built, scal, prods, dots, msg_ready, agg_mm, acc_done = (sem(n) for n in ("built", "scal", "prods", "dots", "msg_ready", "agg_mm", "acc_done"))
        block = ctx.enter_context(nc.Block())

        def use(item, u):
            return item // UNROLL + 1 if isinstance(item, int) else (item - u) // UNROLL + 1

        @block.sync
        def _(sp):
            for tile, name in ((mlp0, "mlp0"), (mlp1, "mlp1"), (mlp2, "mlp2"), (bias0, "mlp_b0"), (bias1, "mlp_b1"), (bias2, "mlp_b2")):
                sp.dma_start(tile[:], io[name]).then_inc(w_in, 16)
            passes = sp.value_load(ctl[0:1, 0:1], min_val=MIN_PASSES - 1, max_val=MAX_PASSES - 1) + 1
            sp.wait_ge(cleared, 1)

            loaded = {}

            def step(w, u, drained):
                if u == 0:
                    loaded["group"] = load_pass(nc, mybir.EngineType.SP, dram["item_group"], w, UNROLL, NG - 1)
                g = loaded["group"][u]
                if u % BATCH == 0:
                    if reached(w, UNROLL):
                        sp.wait_ge(built, w - UNROLL + BATCH)
                    sp.dma_start(base[:, u:u + BATCH],
                                 dram["item_base_f"][0:1, bass.ds(w, BATCH)].broadcast_to([P, BATCH])).then_inc(base_in[u // BATCH], 16)
                if reached(w, UNROLL):
                    sp.wait_ge(msg_ready, w - UNROLL + 1)
                sp.dma_start(meta[:, u], io["meta"][bass.ds(g, 1)].rearrange("a p k -> (a p) k")).then_inc(meta_in[u], 16)
                sp.dma_start(y[:, u].rearrange("p i k -> p (i k)"),
                             dram["y_edges"][:, bass.ds(g * (TILES * 3), TILES * 3)]).then_inc(edge_in[u], 16)
                for half in range(2):
                    sp.dma_start(emb[half * NB:(half + 1) * NB, u],
                                 dram["emb_edges"][:, bass.ds(g * GROUP + half * HALF, HALF)]).then_inc(edge_in[u], 16)

            over_items(sp, step, passes, 0)

        @block.gpsimd
        def _(pool):
            passes = pool.value_load(ctl[0:1, 0:1], min_val=MIN_PASSES - 1, max_val=MAX_PASSES - 1) + 1
            meta_before = pool.snap(16 * passes)

            def step(w, u, drained):
                pool.wait_ge(meta_in[u], 16 * use(w, u) + meta_before)
                if reached(w, UNROLL):
                    pool.wait_ge(msg_ready, w - UNROLL + 1)
                pool.sem_inc(started, 1)
                for i in range(TILES):
                    nc.gpsimd.indirect_dma_start(
                        gath[:, u, i, :], None, dram["u_table"],
                        bass.IndirectOffsetOnAxis(ap=meta[:, u, i:i + 1], axis=0)).then_inc(gathered[u], 16)

            over_items(pool, step, passes, 0)

        @block.tensor
        def _(pe):
            passes = pe.value_load(ctl[0:1, 0:1], min_val=MIN_PASSES - 1, max_val=MAX_PASSES - 1) + 1
            edges_before = pe.snap(32 * passes)
            pe.wait_ge(ready, 1)
            pe.wait_ge(w_in, 16 * 6)

            def step(w, u, drained):
                if stage(w, drained, 2):
                    r, v = w - 2, u % 2
                    pe.wait_ge(h1_ready, r + 1)
                    if reached(r, 2):
                        pe.wait_ge(msg_ready, r - 1)
                    for t in range(2):
                        out = w_ps[v][:, 2 * t:2 * t + 2, :].rearrange("p h d -> p (h d)")
                        for k in range(SPLITS):
                            nc.tensor.matmul(out, ones[:], bias2_part[:, k, :], start=(k == 0), stop=False)
                        last = nc.tensor.matmul(out, h1[:, v, t * P:(t + 1) * P], mlp2[:], start=False, stop=True)
                    last.then_inc(w_mm, 1)
                if stage(w, drained, 0):
                    pe.wait_ge(edge_in[u], 48 * use(w, u) + edges_before)
                    if reached(w, 1):
                        pe.wait_ge(h0_ready, w)
                    nc.tensor.matmul(h0_ps[:, 0:HALF], mlp0[:], emb[:, u], start=True, stop=True).then_inc(h0_mm, 1)
                if stage(w, drained, 1):
                    r, v = w - 1, (u + 1) % 2
                    pe.wait_ge(h0_ready, r + 1)
                    if reached(r, 1):
                        pe.wait_ge(h1_ready, r)
                    nc.tensor.matmul(h1_ps[:, 0:HALF], mlp1[:], h0[:, v], start=True, stop=True).then_inc(h1_mm, 1)
                if stage(w, drained, 4):
                    r, v, a = w - 4, u % 2, u % 4
                    pe.wait_ge(msg_ready, r + 1)
                    if reached(r, 4):
                        pe.wait_ge(acc_done, r - 3)
                    for c in range(2):
                        for i in range(TILES):
                            last = nc.tensor.matmul(agg_ps[a][:, c * P:(c + 1) * P],
                                                    msg[:, v, i, MUL + c * P:MUL + (c + 1) * P], by_edge[:, v, i, :],
                                                    start=(i == 0), stop=(i == TILES - 1))
                    last.then_inc(agg_mm, 1)

            over_items(pe, step, passes, SUM_LAG)

        @block.scalar
        def _(act):
            passes = act.value_load(ctl[0:1, 0:1], min_val=MIN_PASSES - 1, max_val=MAX_PASSES - 1) + 1
            act.wait_ge(w_in, 16 * 6)

            def step(w, u, drained):
                if stage(w, drained, 0):
                    v = u % 2
                    act.wait_ge(h0_mm, w + 1)
                    if reached(w, 2):
                        act.wait_ge(h1_mm, w - 1)
                    nc.scalar.activation(h0[:, v], h0_ps[:, 0:HALF], ACT.Silu, bias=bias0[:]).then_inc(h0_ready, 1)
                if stage(w, drained, 1):
                    r, v = w - 1, (u + 1) % 2
                    act.wait_ge(h1_mm, r + 1)
                    if reached(r, 2):
                        act.wait_ge(w_mm, r - 1)
                    nc.scalar.activation(h1[:, v], h1_ps[:, 0:HALF], ACT.Silu, bias=bias1[:]).then_inc(h1_ready, 1)

            over_items(act, step, passes, 1)

        @block.vector
        def _(dve):
            passes = dve.value_load(ctl[0:1, 0:1], min_val=MIN_PASSES - 1, max_val=MAX_PASSES - 1) + 1
            meta_before = dve.snap(16 * passes)
            edges_before = dve.snap(32 * passes)
            gathers_before = dve.snap(16 * TILES * passes)
            nc.vector.memset(emb[:], 0.0).then_inc(cleared, 1)
            nc.vector.memset(ones[:], 1.0)
            dve.wait_ge(w_in, 16 * 6)
            nc.vector.tensor_copy(bias2_part[:, 0, :], bias2[:]).then_inc(split, 1)
            dve.wait_ge(split, 1)
            nc.vector.tensor_tensor(bias2_rest[:], bias2[:], bias2_part[:, 0, :], ALU.subtract).then_inc(split, 1)
            dve.wait_ge(split, 2)
            nc.vector.tensor_copy(bias2_part[:, 1, :], bias2_rest[:]).then_inc(split, 1)
            dve.wait_ge(split, 3)
            nc.vector.tensor_tensor(bias2_rest[:], bias2_rest[:], bias2_part[:, 1, :], ALU.subtract).then_inc(split, 1)
            dve.wait_ge(split, 4)
            nc.vector.tensor_copy(bias2_part[:, 2, :], bias2_rest[:]).then_inc(ready, 1)

            loaded = {}

            def step(w, u, drained):
                if u == 0:
                    loaded["first"] = load_pass(nc, mybir.EngineType.DVE, dram["sum_base"], w,
                                                UNROLL if drained < 0 else SUM_LAG, NP - P)
                if stage(w, drained, SUM_LAG):
                    r, a, first = w - SUM_LAG, (u - SUM_LAG) % 4, loaded["first"][u]
                    dve.wait_ge(agg_mm, r + 1)
                    if reached(r, 1):
                        dve.wait_ge(acc_done, r)
                    nc.vector.tensor_tensor(agg[:, :, bass.ds(first, P)], agg[:, :, bass.ds(first, P)],
                                            agg_ps[a][:, 0:2 * P].rearrange("p (c n) -> p c n", c=2), ALU.add).then_inc(acc_done, 1)
                if stage(w, drained, 3):
                    r, v, z = w - 3, (u - 3) % 2, (u - 3) % UNROLL
                    dve.wait_ge(meta_in[z], 16 * use(r, z) + meta_before)
                    if reached(r, 2):
                        dve.wait_ge(agg_mm, r - 1)
                    dve.wait_ge(base_in[z // BATCH], 16 * use(r, z) + meta_before)
                    nc.vector.scalar_tensor_tensor(
                        out=by_edge[:, v], in0=iota[:].unsqueeze(1).broadcast_to([P, TILES, P]), scalar=base[:, z:z + 1],
                        in1=meta[:, z, TILES:2 * TILES].unsqueeze(2).broadcast_to([P, TILES, P]),
                        op0=ALU.add, op1=ALU.is_equal).then_inc(built, 1)
                    dve.wait_ge(gathered[z], 16 * TILES * use(r, z) + gathers_before)
                    dve.wait_ge(edge_in[z], 48 * use(r, z) + edges_before)
                    m, g, wt = msg[:, v], gath[:, z], w_ps[v]
                    vec = g[:, :, VEC].rearrange("p i (c k) -> p i c k", c=3)
                    if reached(r, 1):
                        dve.wait_ge(dots, r)
                    nc.vector.tensor_tensor(prod[:], vec, y[:, z].unsqueeze(3).broadcast_to([P, TILES, 3, MUL]),
                                            ALU.mult).then_inc(prods, 1)
                    dve.wait_ge(w_mm, r + 1)
                    nc.vector.tensor_tensor(m[:, :, 0:2 * MUL].rearrange("p i (j k) -> p i j k", j=2),
                                            wt[:, :, 0:2 * MUL].rearrange("p i (j k) -> p i j k", j=2),
                                            g[:, :, 0:MUL].unsqueeze(2).broadcast_to([P, TILES, 2, MUL]), ALU.mult).then_inc(scal, 1)
                    dve.wait_ge(prods, r + 1)
                    if reached(r, 1):
                        dve.wait_ge(msg_ready, r)
                    nc.vector.tensor_reduce(dot[:], prod[:].rearrange("p i c k -> p i k c"), AX.X, ALU.add).then_inc(dots, 1)
                    nc.vector.tensor_tensor(m[:, :, 3 * MUL:6 * MUL].rearrange("p i (c k) -> p i c k", c=3), vec,
                                            wt[:, :, 3 * MUL:4 * MUL].unsqueeze(2).broadcast_to([P, TILES, 3, MUL]), ALU.mult)
                    dve.wait_ge(scal, r + 1)
                    nc.vector.tensor_tensor(m[:, :, 6 * MUL:9 * MUL].rearrange("p i (c k) -> p i c k", c=3),
                                            m[:, :, 0:MUL].unsqueeze(2).broadcast_to([P, TILES, 3, MUL]),
                                            y[:, z].unsqueeze(3).broadcast_to([P, TILES, 3, MUL]), ALU.mult)
                    dve.wait_ge(dots, r + 1)
                    nc.vector.scalar_tensor_tensor(out=m[:, :, 2 * MUL:3 * MUL], in0=dot[:], scalar=1.0 / SQ3,
                                                   in1=wt[:, :, 2 * MUL:3 * MUL], op0=ALU.mult, op1=ALU.mult).then_inc(msg_ready, 1)

            over_items(dve, step, passes, SUM_LAG)


def output_nodes(nc, io, dram, keep, NP):
    agg = keep["agg"]
    NQ = NP // QUAD
    SCALE = 1.0 / (float(2 * MUL) ** 0.5 * 16.0)
    with ExitStack() as ctx:
        def sb(name, shape, dt):
            return ctx.enter_context(nc.sbuf_tensor("final_" + name, shape, dt))

        def sem(name):
            return ctx.enter_context(nc.semaphore("final_" + name))

        w_out = sb("w_out", [P, 2, D], F32)
        sums = sb("sums", [P, 2, 2, QUAD], F32)
        x1 = sb("x1", [P, 2, 4, D], F32)
        out = sb("out", [P, 2, 4, D], F32)
        out_ps = [ctx.enter_context(nc.psum_tensor(f"final_out_ps{i}", [P, 4, D], F32)) for i in range(2)]
        w_in = sem("w_in")
        x1_in = [sem("x1_in0"), sem("x1_in1")]
        stored = [sem("stored0"), sem("stored1")]
        copied, out_mm, out_ready = sem("copied"), sem("out_mm"), sem("out_ready")
        block = ctx.enter_context(nc.Block())

        def valid(q):
            return not isinstance(q, int) or 0 <= q < NQ

        def over_quads(eng, step, lag=0):
            for q in range(2):
                step(q, q)
            if NQ // 2 > 1:
                with eng.Fori(1, NQ // 2) as k:
                    step(2 * k, 0)
                    step(2 * k + 1, 1)
            for q in range(max(2, NQ - NQ % 2), NQ + lag):
                step(q, q % 2)

        def use(q, s):
            return q // 2 + 1 if isinstance(q, int) else (q - s) // 2 + 1

        def rows(table, q):
            return table[bass.ds(q * QUAD, QUAD), :].rearrange("(t p) d -> p t d", p=P)

        @block.sync
        def _(sp):
            sp.dma_start(w_out[:], io["w_out"]).then_inc(w_in, 16)

            def step(q, s):
                if reached(q, 2):
                    sp.wait_ge(out_ready, q - 1)
                if valid(q):
                    sp.dma_start(x1[:, s], rows(dram["x1_nodes"], q)).then_inc(x1_in[s], 16)
                if valid(q - 1):
                    sp.wait_ge(out_ready, q)
                    sp.dma_start(rows(io["out"], q - 1), out[:, 1 - s]).then_inc(stored[1 - s], 16)

            over_quads(sp, step, 1)
            for s in range(2):
                sp.wait_ge(stored[s], 16 * ((NQ + 1 - s) // 2))

        @block.scalar
        def _(act):
            def step(q, s):
                if reached(q, 2):
                    act.wait_ge(out_mm, q - 1)
                nc.scalar.copy(sums[:, s], agg[:, :, bass.ds(q * QUAD, QUAD)]).then_inc(copied, 1)

            over_quads(act, step)

        @block.tensor
        def _(pe):
            pe.wait_ge(w_in, 16)

            def step(q, s):
                pe.wait_ge(copied, q + 1)
                if reached(q, 2):
                    pe.wait_ge(out_ready, q - 1)
                for t in range(4):
                    for c in range(2):
                        last = nc.tensor.matmul(out_ps[s][:, t, :], sums[:, s, c, t * P:(t + 1) * P], w_out[:, c, :],
                                                start=(c == 0), stop=(c == 1))
                last.then_inc(out_mm, 1)

            over_quads(pe, step)

        @block.vector
        def _(dve):
            def step(q, s):
                dve.wait_ge(out_mm, q + 1)
                dve.wait_ge(x1_in[s], 16 * use(q, s))
                if reached(q, 2):
                    dve.wait_ge(stored[s], 16 * (use(q, s) - 1))
                nc.vector.scalar_tensor_tensor(out=out[:, s], in0=out_ps[s][:], scalar=SCALE, in1=x1[:, s],
                                               op0=ALU.mult, op1=ALU.add).then_inc(out_ready, 1)

            over_quads(dve, step)


def kernel(**inputs):
    import numpy as np
    import concourse.bacc as bacc
    from concourse.bass_utils import run_bass_kernel_spmd

    a = {k: np.asarray(v) for k, v in inputs.items()}
    N, E = a["x"].shape[0], a["src"].shape[0]
    NP, NG, J = layout(N, E)
    EP = NG * GROUP

    def padded(rows, n, value=0):
        out = np.full((n,) + rows.shape[1:], value, rows.dtype)
        out[:rows.shape[0]] = rows
        return out

    def by_tile(edges):
        v = edges.reshape(NG, 2, 2, P, -1)
        return np.ascontiguousarray(v.transpose(0, 3, 2, 1, 4)).reshape(NG, P, TILES, -1)

    src, dst = padded(a["src"], EP), padded(a["dst"], EP, N)
    feat = padded(a["edge_attr_64"], EP).reshape(NG, 2, GROUP // 2, ED)
    vec = by_tile(padded(a["edge_attr_3"], EP))
    w1 = a["L0_gnn_W1"]
    f32 = np.float32
    w1_edges = np.zeros((2, ED, 2, D + 1), f32)
    mlp0, mlp1 = np.zeros((P, 2, HID), f32), np.zeros((2, HID, 2, HID), f32)
    mlp2 = np.zeros((2, HID, 2, D), f32)
    order = [1, 0, 3, 2]
    w3 = a["L1_gnn_mlp_w2"].reshape(HID, 4, MUL)[:, order].reshape(HID, D)
    b3 = a["L1_gnn_mlp_b2"].reshape(4, MUL)[order].reshape(D)
    for half in range(2):
        w1_edges[half, :, half, 0:D] = w1[2 * D:]
        w1_edges[half, :, half, D] = a["L0_gnn_gate_w"][:, 0]
        mlp0[half * NB:(half + 1) * NB, half] = a["L1_gnn_mlp_w0"]
        mlp1[half, :, half] = a["L1_gnn_mlp_w1"]
        mlp2[half, :, half] = w3
    w_up = np.zeros((D, 4, MUL), f32)
    w_up[0:MUL, 0] = a["L1_gnn_W_up0"]
    w_out = np.zeros((8, MUL, D), f32)
    w_out[0, :, 0:MUL] = a["L1_gnn_W_out0"][0:MUL]
    w_out[1, :, 0:MUL] = a["L1_gnn_W_out0"][MUL:]
    for c in range(3):
        w_up[MUL + c::3, 1 + c] = a["L1_gnn_W_up1"]
        w_out[2 + c, :, MUL + c::3] = a["L1_gnn_W_out1"][MUL:]
        w_out[5 + c, :, MUL + c::3] = a["L1_gnn_W_out1"][0:MUL]

    arrays = {
        "x": padded(a["x"], NP),
        "meta": np.concatenate([by_tile(src), by_tile(dst)], axis=2)[..., 0],
        "dst_flat": dst.reshape(1, EP),
        "edge_feat": feat.transpose(0, 1, 3, 2).reshape(NG, P, GROUP // 2),
        "edge_vec": vec.transpose(1, 0, 2, 3).reshape(P, NG * TILES, 3),
        "edge_dist": padded(a["edge_weight"], EP).reshape(P, EP // P),
        "ident": np.eye(P, dtype=f32),
        "w1_nodes": w1[:2 * D].reshape(2, D, D).transpose(1, 0, 2),
        "b1": a["L0_gnn_b1"].reshape(1, D),
        "w1_edges": w1_edges.reshape(P, 2, D + 1),
        "gate_b": a["L0_gnn_gate_b"].reshape(1, 1),
        "ln_g": a["L0_gnn_ln_g"].reshape(1, D),
        "ln_b": a["L0_gnn_ln_b"].reshape(1, D),
        "w2": a["L0_gnn_W2"],
        "b2": a["L0_gnn_b2"].reshape(1, D),
        "w_ih": a["L0_gnn_W_ih"].T,
        "w_hh": a["L0_gnn_W_hh"].T,
        "b_ih": a["L0_gnn_b_ih"].reshape(3, D).T,
        "b_hh": a["L0_gnn_b_hh"].reshape(3, D).T,
        "w_up": w_up.reshape(D, D),
        "mlp0": mlp0.reshape(P, P),
        "mlp1": mlp1.reshape(P, P),
        "mlp2": mlp2.reshape(P, 2 * D),
        "mlp_b0": np.concatenate([a["L1_gnn_mlp_b0"]] * 2).reshape(P, 1),
        "mlp_b1": np.concatenate([a["L1_gnn_mlp_b1"]] * 2).reshape(P, 1),
        "mlp_b2": np.concatenate([b3, b3]).reshape(1, 2 * D),
        "w_out": w_out.reshape(2, P, D).transpose(1, 0, 2),
    }
    arrays = {k: np.ascontiguousarray(v) for k, v in arrays.items()}
    nc = bacc.Bacc("TRN2", target_bir_lowering=False, num_devices=1)
    io = {k: nc.dram_tensor(f"in_{k}", v.shape, mybir.dt.from_np(v.dtype), kind="ExternalInput").ap() for k, v in arrays.items()}
    io["out"] = nc.dram_tensor("out_nodes", (NP, D), F32, kind="ExternalOutput").ap()
    program(nc, io, N, E)
    result = run_bass_kernel_spmd(nc, [{f"in_{k}": v for k, v in arrays.items()}], core_ids=[0])
    return result.results[0]["out_nodes"][:N]
```

```python
import concourse.bass as bass
from concourse import mybir
from contextlib import ExitStack

F32 = mybir.dt.float32
BF16 = mybir.dt.bfloat16
I32 = mybir.dt.int32
ALU = mybir.AluOpType
ACT = mybir.ActivationFunctionType
AX = mybir.AxisListType

P = 128
D = 128
ED = 64
TILES = 4
GROUP = TILES * P
QUAD = 4 * P
SLOTS = 4
UNROLL = 8
BATCH = 4
SUM_LAG = 6
MUL = 32
NB = 8
HID = 64
MSG = 9 * MUL
EPS = 1e-5
SQ3 = 3.0 ** 0.5
SPLITS = 3


def tile_offset(i):
    return (i % 2) * (GROUP // 2) + (i // 2) * P


def reached(step, n):
    return not isinstance(step, int) or step >= n


def layout(N, E):
    NP = -(-(N + 1 + P) // QUAD) * QUAD
    NG = -(-E // GROUP)
    NG = -(-NG // UNROLL) * UNROLL
    windows = N // P + 1
    J = -(-(NG * windows + UNROLL) // P)
    return NP, NG, J


def program(nc, io, N, E):
    NP, NG, J = layout(N, E)
    dram = {}

    def scratch(name, shape, dt):
        dram[name] = nc.dram_tensor(name, shape, dt).ap()

    scratch("a_table", (NP, D + 1), F32)
    scratch("b_table", (NP, SPLITS * D), BF16)
    scratch("u_table", (NP, D), F32)
    scratch("y_edges", (P, NG * TILES * 3), F32)
    scratch("emb_edges", (NB, NG * GROUP), F32)
    scratch("group_lo", (1, NG), I32)
    scratch("group_extra", (1, NG), I32)
    scratch("group_end", (1, NG), F32)
    scratch("group_step", (1, NG), F32)
    scratch("item_group", (1, P * J), I32)
    scratch("item_base", (1, P * J), I32)
    scratch("item_base_f", (1, P * J), F32)
    scratch("sum_base", (1, P * J + UNROLL), I32)

    with ExitStack() as ctx:
        def sb(name, shape, dt):
            return ctx.enter_context(nc.sbuf_tensor(name, shape, dt))

        keep = {
            "agg": sb("agg", [P, 2, NP], F32),
            "nodes": sb("nodes", [P, NP], F32),
            "iota": sb("iota", [P, P], F32),
            "ident": sb("ident", [P, P], F32),
            "eps": sb("eps", [P, 1], F32),
            "meta_in": [ctx.enter_context(nc.semaphore(f"meta_in{u}")) for u in range(UNROLL)],
            "edge_in": [ctx.enter_context(nc.semaphore(f"edge_in{u}")) for u in range(UNROLL)],
            "gathered": [ctx.enter_context(nc.semaphore(f"gathered{u}")) for u in range(UNROLL)],
            "base_in": [ctx.enter_context(nc.semaphore(f"base_in{b}")) for b in range(UNROLL // BATCH)],
            "started": ctx.enter_context(nc.semaphore("started")),
            "ctl": sb("ctl", [1, 4], I32),
        }
        prepare(nc, io, dram, keep, N, NP, NG, J)
        node_tables(nc, io, dram, keep, NP)
        gated_edges(nc, io, dram, keep, NP, NG, J)
        gru_nodes(nc, io, dram, keep, NP)
        tensor_edges(nc, io, dram, keep, NP, NG, J)
        output_nodes(nc, io, dram, keep, NP)


def prepare(nc, io, dram, keep, N, NP, NG, J):
    agg, iota, ident, eps, ctl = (keep[k] for k in ("agg", "iota", "ident", "eps", "ctl"))
    PG = NG // UNROLL
    C = NG * GROUP // P
    with ExitStack() as ctx:
        def sb(name, shape, dt):
            return ctx.enter_context(nc.sbuf_tensor("prep_" + name, shape, dt))

        def sem(name):
            return ctx.enter_context(nc.semaphore("prep_" + name))

        dst_rows = sb("dst_rows", [PG, UNROLL, GROUP], I32)
        lo4 = sb("lo4", [PG, UNROLL], I32)
        hi4 = sb("hi4", [PG, UNROLL], I32)
        span4 = sb("span4", [PG, UNROLL], I32)
        extra4 = sb("extra4", [PG, UNROLL], I32)
        lo_row = sb("lo_row", [1, NG], I32)
        extra_row = sb("extra_row", [1, NG], I32)
        group_row = sb("group_row", [1, NG], I32)
        count = sb("count", [1, NG], F32)
        ones = sb("ones", [1, NG], F32)
        end_row = sb("end_row", [1, NG], F32)
        start_row = sb("start_row", [1, NG], F32)
        shift_row = sb("shift_row", [1, NG], F32)
        step_row = sb("step_row", [1, NG], F32)
        total = sb("total", [1, 2], I32)
        end_all = sb("end_all", [P, NG], F32)
        step_all = sb("step_all", [P, NG], F32)
        lo0 = sb("lo0", [P, 1], I32)
        slot = sb("slot", [P, J], F32)
        group_of = sb("group_of", [P, J], F32)
        base_of = sb("base_of", [P, J], F32)
        passed = sb("passed", [P, J], F32)
        live = sb("live", [P, J], F32)
        group_int = sb("group_int", [P, J], I32)
        base_int = sb("base_int", [P, J], I32)
        base_f = sb("base_f", [P, J], F32)
        lo_row_f = sb("lo_row_f", [1, NG], F32)
        first = sb("first", [1, SUM_LAG], I32)
        assert 8 * C <= NP
        vec = agg[:, 1, 0:3 * C].rearrange("p (c k) -> p c k", k=3)
        norm, dist, inside = (agg[:, 1, i * C:(i + 1) * C] for i in range(3, 6))
        emb = agg[:, 1, 6 * C:8 * C].rearrange("p (s c) -> p s c", s=2)
        centers = sb("centers", [P, NB], F32)

        dst_in, edges_in, const_in = sem("dst_in"), sem("edges_in"), sem("const_in")
        spans_out, spans_in = sem("spans_out"), sem("spans_in")
        steps_out, steps_in = sem("steps_out"), sem("steps_in")
        items_out, edges_out = sem("items_out"), sem("edges_out")
        spans, listed, items, iotas = sem("spans"), sem("listed"), sem("items"), sem("iotas")
        squared, summed, rooted, unit = sem("squared"), sem("summed"), sem("rooted"), sem("unit")
        clipped, shifted, bell, masked = sem("clipped"), sem("shifted"), sem("bell"), sem("masked")
        emb_out = [sem("emb_out0"), sem("emb_out1")]
        chain, zeroed = sem("chain"), sem("zeroed")
        block = ctx.enter_context(nc.Block())

        @block.sync
        def _(sp):
            sp.dma_start(dst_rows[:], io["dst_flat"].rearrange("a (p q e) -> (a p) q e", p=PG, q=UNROLL)).then_inc(dst_in, 16)
            sp.dma_start(vec, io["edge_vec"]).then_inc(edges_in, 16)
            sp.dma_start(dist, io["edge_dist"]).then_inc(edges_in, 16)
            sp.dma_start(ident[:], io["ident"]).then_inc(const_in, 16)
            sp.wait_ge(spans, 1)
            sp.dma_start(dram["group_lo"].rearrange("a (p q) -> (a p) q", p=PG), lo4[:]).then_inc(spans_out, 16)
            sp.dma_start(dram["group_extra"].rearrange("a (p q) -> (a p) q", p=PG), extra4[:]).then_inc(spans_out, 16)
            sp.wait_ge(spans_out, 32)
            sp.dma_start(lo_row[:], dram["group_lo"]).then_inc(spans_in, 16)
            sp.dma_start(extra_row[:], dram["group_extra"]).then_inc(spans_in, 16)
            sp.dma_start(lo0[:], dram["group_lo"][:, 0:1].broadcast_to([P, 1])).then_inc(spans_in, 16)
            sp.wait_ge(listed, 1)
            sp.dma_start(dram["group_end"], end_row[:]).then_inc(steps_out, 16)
            sp.dma_start(dram["group_step"], step_row[:]).then_inc(steps_out, 16)
            sp.wait_ge(steps_out, 32)
            sp.dma_start(end_all[:], dram["group_end"].broadcast_to([P, NG])).then_inc(steps_in, 16)
            sp.dma_start(step_all[:], dram["group_step"].broadcast_to([P, NG])).then_inc(steps_in, 16)
            sp.wait_ge(items, 1)
            sp.wait_ge(iotas, 1)
            several = sp.value_load(ctl[0:1, 1:2], min_val=0, max_val=1)
            with sp.If(several == 1):
                sp.dma_start(dram["item_group"].rearrange("a (p j) -> (a p) j", p=P), group_int[:]).then_inc(items_out, 16)
                sp.dma_start(dram["item_base"].rearrange("a (p j) -> (a p) j", p=P), base_int[:]).then_inc(items_out, 16)
                sp.dma_start(dram["sum_base"][:, SUM_LAG:SUM_LAG + P * J].rearrange("a (p j) -> (a p) j", p=P),
                             base_int[:]).then_inc(items_out, 16)
                sp.dma_start(dram["item_base_f"].rearrange("a (p j) -> (a p) j", p=P), base_f[:]).then_inc(items_out, 16)
            with sp.Else():
                sp.dma_start(dram["item_group"][:, 0:NG], group_row[:]).then_inc(items_out, 16)
                sp.dma_start(dram["item_base"][:, 0:NG], lo_row[:]).then_inc(items_out, 16)
                sp.dma_start(dram["sum_base"][:, SUM_LAG:SUM_LAG + NG], lo_row[:]).then_inc(items_out, 16)
                sp.dma_start(dram["item_base_f"][:, 0:NG], lo_row_f[:]).then_inc(items_out, 16)
            sp.dma_start(dram["sum_base"][:, 0:SUM_LAG], first[:]).then_inc(items_out, 16)
            sp.wait_ge(unit, 1)
            sp.dma_start(dram["y_edges"], vec.rearrange("p c k -> p (c k)")).then_inc(edges_out, 16)
            for b in range(NB):
                sp.wait_ge(masked, b + 1)
                sp.dma_start(dram["emb_edges"][b:b + 1, :].rearrange("a (p c) -> (a p) c", p=P),
                             emb[:, b % 2, :]).then_inc(emb_out[b % 2], 16)
            sp.wait_ge(items_out, 16 * 5)
            sp.wait_ge(edges_out, 16)
            sp.wait_ge(steps_in, 32)
            sp.wait_ge(const_in, 16)
            for s in emb_out:
                sp.wait_ge(s, 16 * NB // 2)

        @block.gpsimd
        def _(pool):
            nc.gpsimd.iota(group_row[:], [[1, NG]], base=0, channel_multiplier=0)
            nc.gpsimd.iota(slot[:], [[1, J]], base=0, channel_multiplier=J, allow_small_or_imprecise_dtypes=True)
            nc.gpsimd.iota(centers[:], [[-1, NB]], base=0, channel_multiplier=0, allow_small_or_imprecise_dtypes=True)
            nc.gpsimd.iota(iota[:], [[1, P]], base=0, channel_multiplier=0,
                           allow_small_or_imprecise_dtypes=True).then_inc(iotas, 1)
            nc.gpsimd.memset(agg[:, 0, :], 0.0).then_inc(zeroed, 1)
            pool.wait_ge(zeroed, 1)

        @block.vector
        def _(dve):
            done = [0]

            def then(instruction):
                done[0] += 1
                instruction.then_inc(chain, 1)
                dve.wait_ge(chain, done[0])

            nc.vector.memset(eps[:], EPS)
            nc.vector.memset(first[:], 0)
            nc.vector.memset(ones[:], 1.0)
            dve.wait_ge(dst_in, 16)
            nc.vector.tensor_reduce(lo4[:], dst_rows[:], AX.X, ALU.min)
            then(nc.vector.tensor_reduce(hi4[:], dst_rows[:], AX.X, ALU.max))
            then(nc.vector.tensor_tensor(span4[:], hi4[:], lo4[:], ALU.subtract))
            nc.vector.tensor_scalar(extra4[:], span4[:], P.bit_length() - 1, None, ALU.arith_shift_right).then_inc(spans, 1)
            dve.wait_ge(spans_in, 48)
            nc.vector.tensor_copy(lo_row_f[:], lo_row[:])
            then(nc.vector.tensor_scalar(count[:], extra_row[:], 1.0, None, ALU.add))
            then(nc.vector.tensor_tensor_scan(end_row[:], ones[:], count[:], 0.0, ALU.mult, ALU.add))
            then(nc.vector.tensor_tensor(start_row[:], end_row[:], count[:], ALU.subtract))
            then(nc.vector.scalar_tensor_tensor(out=shift_row[:], in0=start_row[:], scalar=-float(P), in1=lo_row[:],
                                                op0=ALU.mult, op1=ALU.add))
            nc.vector.memset(step_row[0:1, NG - 1:NG], 0.0)
            nc.vector.tensor_tensor(step_row[0:1, 0:NG - 1], shift_row[0:1, 1:NG], shift_row[0:1, 0:NG - 1], ALU.subtract)
            then(nc.vector.tensor_scalar(total[0:1, 0:1], end_row[0:1, NG - 1:NG], -1.0, None, ALU.add))
            nc.vector.tensor_scalar(ctl[0:1, 0:1], total[0:1, 0:1], UNROLL.bit_length() - 1, None, ALU.arith_shift_right)
            then(nc.vector.tensor_scalar(ctl[0:1, 1:2], end_row[0:1, NG - 1:NG], float(NG), None, ALU.is_gt))
            nc.vector.memset(ctl[0:1, 2:4], 0).then_inc(listed, 1)
            several = dve.value_load(ctl[0:1, 1:2], min_val=0, max_val=1)
            dve.wait_ge(steps_in, 32)
            dve.wait_ge(iotas, 1)
            with dve.If(several == 1):
                nc.vector.memset(group_of[:], 0.0)
                nc.vector.tensor_scalar(base_of[:], slot[:], float(P), lo0[:, 0:1], ALU.mult, ALU.add).then_inc(chain, 1)
                dve.wait_ge(chain, done[0] + 1)
                with dve.Fori(0, NG) as g:
                    nc.vector.tensor_scalar(passed[:], slot[:], end_all[:, bass.ds(g, 1)], step_all[:, bass.ds(g, 1)],
                                            ALU.is_ge, ALU.mult)
                    nc.vector.scalar_tensor_tensor(out=group_of[:], in0=slot[:], scalar=end_all[:, bass.ds(g, 1)],
                                                   in1=group_of[:], op0=ALU.is_ge, op1=ALU.add).then_inc(chain, 1)
                    dve.wait_ge(chain, 2 * g + done[0] + 2)
                    nc.vector.tensor_tensor(base_of[:], base_of[:], passed[:], ALU.add).then_inc(chain, 1)
                    dve.wait_ge(chain, 2 * g + done[0] + 3)
                after = done[0] + 1 + 2 * NG
                nc.vector.tensor_scalar(live[:], slot[:], end_all[:, NG - 1:NG], None, ALU.is_lt)
                nc.vector.tensor_scalar(base_of[:], base_of[:], -float(NP - P), None, ALU.add).then_inc(chain, 1)
                dve.wait_ge(chain, after + 1)
                nc.vector.tensor_tensor(group_int[:], group_of[:], live[:], ALU.mult)
                nc.vector.tensor_tensor(base_of[:], base_of[:], live[:], ALU.mult).then_inc(chain, 1)
                dve.wait_ge(chain, after + 2)
                nc.vector.tensor_scalar(base_int[:], base_of[:], float(NP - P), None, ALU.add)
                nc.vector.tensor_scalar(base_f[:], base_of[:], float(NP - P), None, ALU.add).then_inc(chain, 1)
                dve.wait_ge(chain, after + 3)
            nc.vector.memset(ones[0:1, 0:1], 1.0).then_inc(items, 1)
            dve.wait_ge(edges_in, 32)
            nc.vector.tensor_scalar(inside, dist, 1.0, float(NB) ** 0.5, ALU.is_le, ALU.mult).then_inc(clipped, 1)
            dve.wait_ge(clipped, 1)
            nc.vector.tensor_scalar(dist, dist, 0.0, 1.0, ALU.max, ALU.min).then_inc(clipped, 1)
            sq = emb[:, 0, :]
            for k in range(3):
                if k:
                    nc.vector.tensor_tensor(emb[:, 1, :], vec[:, :, k], vec[:, :, k], ALU.mult).then_inc(squared, 1)
                    dve.wait_ge(squared, 2 * k)
                    nc.vector.tensor_tensor(sq, sq, emb[:, 1, :], ALU.add).then_inc(squared, 1)
                else:
                    nc.vector.tensor_tensor(sq, vec[:, :, k], vec[:, :, k], ALU.mult).then_inc(squared, 1)
                dve.wait_ge(squared, 2 * k + 1)
            dve.wait_ge(rooted, 1)
            nc.vector.tensor_scalar(norm, norm, 1e-12, None, ALU.add).then_inc(summed, 1)
            dve.wait_ge(summed, 1)
            nc.vector.reciprocal(norm, norm).then_inc(summed, 1)
            dve.wait_ge(summed, 2)
            nc.vector.tensor_scalar(norm, norm, SQ3, None, ALU.mult).then_inc(summed, 1)
            dve.wait_ge(summed, 3)
            nc.vector.tensor_tensor(vec, vec, norm.unsqueeze(2).broadcast_to([P, C, 3]), ALU.mult).then_inc(unit, 1)
            for b in range(NB):
                dve.wait_ge(bell, b + 1)
                nc.vector.tensor_tensor(emb[:, b % 2, :], emb[:, b % 2, :], inside, ALU.mult).then_inc(masked, 1)

        @block.scalar
        def _(act):
            act.wait_ge(squared, 5)
            nc.scalar.activation(norm, emb[:, 0, :], ACT.Sqrt).then_inc(rooted, 1)
            act.wait_ge(rooted, 1)
            act.wait_ge(clipped, 2)
            act.wait_ge(iotas, 1)
            for b in range(NB):
                if b >= 2:
                    act.wait_ge(emb_out[b % 2], 16 * (b // 2))
                nc.scalar.activation(emb[:, b % 2, :], dist, ACT.Square, bias=centers[:, b:b + 1],
                                     scale=float(NB - 1)).then_inc(shifted, 1)
                act.wait_ge(shifted, b + 1)
                nc.scalar.activation(emb[:, b % 2, :], emb[:, b % 2, :], ACT.Exp, scale=-0.5).then_inc(bell, 1)


def node_tables(nc, io, dram, keep, NP):
    ident, nodes, agg = keep["ident"], keep["nodes"], keep["agg"]
    NQ = NP // QUAD
    LAG, PEEL = 6, 8
    with ExitStack() as ctx:
        def sb(name, shape, dt):
            return ctx.enter_context(nc.sbuf_tensor("tables_" + name, shape, dt))

        def pb(name):
            return ctx.enter_context(nc.psum_tensor("tables_" + name, [P, 4, D], F32))

        def sem(name):
            return ctx.enter_context(nc.semaphore("tables_" + name))

        wab = sb("wab", [P, 2, D], F32)
        b1 = sb("b1", [P, 1, D], F32)
        gate_b = sb("gate_b", [P, 1], F32)
        means = sb("means", [P, 3], F32)
        x = sb("x", [P, SLOTS, 4, D], F32)
        stats = sb("stats", [P, 2, 4, 6], F32)
        mv = sb("mv", [P, 2, 4, 2], F32)
        rstd = sb("rstd", [P, 2, 4], F32)
        normed = sb("normed", [P, 2, 4, D], F32)
        hT = sb("hT", [P, 2, QUAD], F32)
        a_out = sb("a_out", [P, SLOTS, 4, D + 1], F32)
        rest = sb("rest", [P, 2, 4, D], F32)
        b_out = sb("b_out", [P, SLOTS, 4, SPLITS, D], BF16)
        hT_ps = [pb(f"hT_ps{i}") for i in range(2)]
        a_ps = [pb(f"a_ps{i}") for i in range(2)]
        b_ps = [pb(f"b_ps{i}") for i in range(2)]

        w_in, centred, chain, zeroed = sem("w_in"), sem("centred"), sem("chain"), sem("zeroed")
        x_in = [sem(f"x_in{s}") for s in range(SLOTS)]
        stored = [sem(f"stored{s}") for s in range(SLOTS)]
        joining = sem("joining")
        measured, moments, scaled, normed_s, turned, hT_ready = (sem(n) for n in (
            "measured", "moments", "scaled", "normed", "turned", "hT_ready"))
        kept, multiplied, a_ready = sem("kept"), sem("multiplied"), sem("a_ready")
        part0, rest0, part1, part2 = (sem(n) for n in ("part0", "rest0", "part1", "part2"))
        block = ctx.enter_context(nc.Block())

        @block.sync
        def _(sp):
            sp.dma_start(wab[:], io["w1_nodes"]).then_inc(w_in, 16)
            sp.dma_start(b1[:, 0, :], io["b1"].broadcast_to([P, D])).then_inc(w_in, 16)
            sp.dma_start(gate_b[:], io["gate_b"].broadcast_to([P, 1])).then_inc(w_in, 16)

            def step(q, s):
                if has_quad(q, NQ):
                    if reached(q, SLOTS):
                        sp.wait_ge(normed_s, q - SLOTS + 1)
                    sp.dma_start(x[:, s], quad_rows(io["x"], q)).then_inc(x_in[s], 16)
                if has_quad(q - LAG, NQ):
                    r, z = q - LAG, (s - LAG) % SLOTS
                    sp.wait_ge(a_ready, r + 1)
                    sp.dma_start(quad_rows(dram["a_table"], r), a_out[:, z]).then_inc(stored[z], 16)
                    sp.wait_ge(part2, r + 1)
                    sp.dma_start(quad_rows(dram["b_table"], r), b_out[:, z].rearrange("p t k d -> p t (k d)")).then_inc(stored[z], 16)

            over_quads(sp, step, NQ, LAG, PEEL)
            for s in range(SLOTS):
                if NQ > s:
                    sp.wait_ge(stored[s], 32 * ((NQ - s - 1) // SLOTS + 1))

        @block.vector
        def _(dve):
            dve.wait_ge(w_in, 48)
            nc.vector.tensor_reduce(means[:, 0:2], wab[:], AX.X, ALU.add)
            nc.vector.tensor_reduce(means[:, 2:3], b1[:], AX.X, ALU.add).then_inc(chain, 1)
            dve.wait_ge(chain, 1)
            nc.vector.tensor_scalar(means[:], means[:], 1.0 / D, None, ALU.mult).then_inc(chain, 1)
            dve.wait_ge(chain, 2)
            for k in range(2):
                nc.vector.tensor_scalar(wab[:, k, :], wab[:, k, :], means[:, k:k + 1], None, ALU.subtract)
            nc.vector.tensor_scalar(b1[:, 0, :], b1[:, 0, :], means[:, 2:3], None, ALU.subtract)
            for s in range(SLOTS):
                for t in range(4):
                    last = nc.vector.tensor_copy(a_out[:, s, t, D:D + 1], gate_b[:])
            last.then_inc(centred, 1)
            dve.wait_ge(centred, 1)

            def step(q, s):
                if has_quad(q - 4, NQ):
                    r, z, v = q - 4, s, s % 2
                    dve.wait_ge(part0, r + 1)
                    if reached(r, 2):
                        dve.wait_ge(part2, r - 1)
                    nc.vector.tensor_tensor(rest[:, v], b_ps[v][:], b_out[:, z, :, 0, :], ALU.subtract).then_inc(rest0, 1)
                if has_quad(q - 3, NQ):
                    r, z, v = q - 3, (s - 3) % SLOTS, (s - 3) % 2
                    dve.wait_ge(multiplied, r + 1)
                    if reached(r, SLOTS):
                        dve.wait_ge(stored[z], 32 * (quad_use(r, z) - 1))
                    nc.vector.tensor_tensor(a_out[:, z, :, 0:D], a_ps[v][:], b1[:].broadcast_to([P, 4, D]),
                                            ALU.add).then_inc(a_ready, 1)
                if has_quad(q, NQ):
                    v = s % 2
                    dve.wait_ge(x_in[s], 16 * quad_use(q, s))
                    if reached(q, 2):
                        dve.wait_ge(moments, q - 1)
                    for t in range(4):
                        last = nc.vector.bn_stats(stats[:, v, t, :], x[:, s, t, :])
                    last.then_inc(measured, 1)
                    dve.wait_ge(measured, q + 1)
                    if reached(q, 2):
                        dve.wait_ge(normed_s, q - 1)
                    dve.sem_inc(joining, 1)
                    for t in range(4):
                        last = nc.vector.bn_aggr(mv[:, v, t, :], stats[:, v, t, :])
                    last.then_inc(moments, 1)
                if has_quad(q - 1, NQ):
                    r, z, v = q - 1, (s - 1) % SLOTS, (s - 1) % 2
                    dve.wait_ge(scaled, 2 * r + 2)
                    if reached(r, 2):
                        dve.wait_ge(turned, r - 1)
                    for t in range(4):
                        last = nc.vector.tensor_scalar(normed[:, v, t, :], x[:, z, t, :], mv[:, v, t, 0:1], rstd[:, v, t:t + 1],
                                                       ALU.subtract, ALU.mult)
                    last.then_inc(normed_s, 1)

            over_quads(dve, step, NQ, LAG, PEEL)

        @block.scalar
        def _(act):
            nc.scalar.preload_act_table_set("natural_log_exp_and_others")

            def step(q, s):
                if has_quad(q - 3, NQ):
                    r, z, v = q - 3, (s - 3) % SLOTS, (s - 3) % 2
                    act.wait_ge(multiplied, r + 1)
                    if reached(r, SLOTS):
                        act.wait_ge(stored[z], 32 * (quad_use(r, z) - 1))
                    nc.scalar.copy(b_out[:, z, :, 0, :], b_ps[v][:]).then_inc(part0, 1)
                if has_quad(q - 5, NQ):
                    r, z, v = q - 5, (s - 5) % SLOTS, (s - 5) % 2
                    act.wait_ge(rest0, r + 1)
                    nc.scalar.copy(b_out[:, z, :, 1, :], rest[:, v]).then_inc(part1, 1)
                if has_quad(q, NQ):
                    v = s % 2
                    act.wait_ge(moments, q + 1)
                    nc.scalar.activation(rstd[:, v], mv[:, v, :, 1], ACT.Ln, bias=keep["eps"][:]).then_inc(scaled, 1)
                    act.wait_ge(scaled, 2 * q + 1)
                    nc.scalar.activation(rstd[:, v], rstd[:, v], ACT.Exp, scale=-0.5).then_inc(scaled, 1)
                if has_quad(q - 1, NQ):
                    r, v = q - 1, (s - 1) % 2
                    act.wait_ge(turned, r + 1)
                    if reached(r, 2):
                        act.wait_ge(multiplied, r - 1)
                        act.wait_ge(kept, r - 1)
                    nc.scalar.activation(hT[:, v], hT_ps[v][:].rearrange("p t d -> p (t d)"), ACT.Relu).then_inc(hT_ready, 1)

            over_quads(act, step, NQ, LAG, PEEL)

        @block.gpsimd
        def _(pool):
            nc.gpsimd.memset(agg[0:1, 1, :], 0.0).then_inc(zeroed, 1)

            def step(q, s):
                if has_quad(q - 2, NQ):
                    r, v = q - 2, s % 2
                    pool.wait_ge(hT_ready, r + 1)
                    pool.sem_inc(joining, 1)
                    nc.gpsimd.tensor_copy(nodes[:, bass.ds(r * QUAD, QUAD)], hT[:, v]).then_inc(kept, 1)
                if has_quad(q - 5, NQ):
                    r, z, v = q - 5, (s - 5) % SLOTS, (s - 5) % 2
                    pool.wait_ge(part1, r + 1)
                    nc.gpsimd.tensor_tensor(b_out[:, z, :, 2, :], rest[:, v], b_out[:, z, :, 1, :], ALU.subtract).then_inc(part2, 1)

            over_quads(pool, step, NQ, LAG, PEEL)
            pool.wait_ge(zeroed, 1)

        @block.tensor
        def _(pe):
            def step(q, s):
                if has_quad(q - 2, NQ):
                    r, v = q - 2, s % 2
                    pe.wait_ge(hT_ready, r + 1)
                    if reached(r, 2):
                        pe.wait_ge(a_ready, r - 1)
                        pe.wait_ge(rest0, r - 1)
                    for k, out in enumerate((a_ps[v], b_ps[v])):
                        for t in range(4):
                            last = nc.tensor.matmul(out[:, t, :], hT[:, v, t * P:(t + 1) * P], wab[:, k, :], start=True, stop=True)
                    last.then_inc(multiplied, 1)
                if has_quad(q - 1, NQ):
                    r, v = q - 1, (s - 1) % 2
                    pe.wait_ge(normed_s, r + 1)
                    if reached(r, 2):
                        pe.wait_ge(hT_ready, r - 1)
                    for t in range(4):
                        last = nc.tensor.transpose(hT_ps[v][:, t, :], normed[:, v, t, :], ident[:])
                    last.then_inc(turned, 1)

            pe.wait_ge(centred, 1)
            over_quads(pe, step, NQ, LAG, PEEL)


def over_items(eng, step, passes, lag):
    for u in range(UNROLL):
        step(u, u, -1)
    with eng.Fori(1, passes) as k:
        for u in range(UNROLL):
            step(k * UNROLL + u, u, -1)
    for u in range(lag):
        step(passes * UNROLL + u, u % UNROLL, u)


def load_pass(nc, engine, table, item, count, highest):
    return nc.values_load_multi_w_load_instructions(
        table[0:1, bass.ds(item, count)], engines=(engine,), min_val=0, max_val=highest,
        skip_runtime_bounds_check_because="prepare() keeps the list of items within these bounds")[1]


def over_quads(eng, step, NQ, lag, peel):
    first, end = peel // SLOTS, NQ // SLOTS
    for q in range(min(peel, NQ + lag)):
        step(q, q % SLOTS)
    if end > first:
        with eng.Fori(first, end) as k:
            for s in range(SLOTS):
                step(k * SLOTS + s, s)
    for q in range(max(peel, end * SLOTS), NQ + lag):
        step(q, q % SLOTS)


def quad_use(q, s):
    return q // SLOTS + 1 if isinstance(q, int) else (q - s) // SLOTS + 1


def has_quad(q, NQ):
    return not isinstance(q, int) or 0 <= q < NQ


def quad_rows(table, q):
    return table[bass.ds(q * QUAD, QUAD), :].rearrange("(t p) d -> p t d", p=P)


def stage(item, drained, lag):
    return drained < lag and reached(item, lag)


def gated_edges(nc, io, dram, keep, NP, NG, J):
    agg, iota, ident, ctl = keep["agg"], keep["iota"], keep["ident"], keep["ctl"]
    PRE = D + 1
    MIN_PASSES, MAX_PASSES = NG // UNROLL, P * J // UNROLL
    with ExitStack() as ctx:
        def sb(name, shape, dt):
            return ctx.enter_context(nc.sbuf_tensor("gated_" + name, shape, dt))

        def pb(name, shape):
            return ctx.enter_context(nc.psum_tensor("gated_" + name, shape, F32))

        def sem(name):
            return ctx.enter_context(nc.semaphore("gated_" + name))

        w_edge = sb("w_edge", [P, 2, PRE], F32)
        w_mean = sb("w_mean", [P, 2], F32)
        ln_g = sb("ln_g", [P, D], F32)
        ln_b = sb("ln_b", [P, 1, D], F32)
        meta = sb("meta", [P, UNROLL, 2 * TILES], I32)
        base = sb("base", [P, UNROLL], F32)
        feat = sb("feat", [P, UNROLL, GROUP // 2], F32)
        b_win = sb("b_win", [P, BATCH, SPLITS * D], BF16)
        gath = sb("gath", [P, UNROLL, TILES, PRE], F32)
        by_node = sb("by_node", [P, 2, GROUP], BF16)
        by_edge = sb("by_edge", [P, UNROLL, TILES, P], F32)
        pre = sb("pre", [P, 2, TILES, PRE], F32)
        junk = sb("junk", [P, D], F32)
        ss = sb("ss", [P, TILES], F32)
        rstd = sb("rstd", [P, 2, TILES], F32)
        gexp = sb("gexp", [P, 2, TILES], F32)
        gate = sb("gate", [P, 2, TILES], F32)
        msg = sb("msg", [P, 2, TILES, D], F32)
        turned_ps = [pb(f"turned_ps{i}", [P, GROUP]) for i in range(2)]
        pre_ps = [pb(f"pre_ps{i}", [P, 2, 512]) for i in range(2)]
        agg_ps = [pb(f"agg_ps{i}", [P, 512]) for i in range(2)]

        w_in, centred, chain = sem("w_in"), sem("centred"), sem("chain")
        meta_in, edge_in, gathered, base_in, started = (keep[k] for k in ("meta_in", "edge_in", "gathered", "base_in", "started"))
        by_edge_built, turned, by_node_built = sem("by_edge_built"), sem("turned"), sem("by_node_built")
        pre_mm, pre_summed, squares, logs, measured = (sem(n) for n in ("pre_mm", "pre_summed", "squares", "logs", "measured"))
        scaled, normed_s, gated, msg_ready, agg_mm, acc_done = (sem(n) for n in ("scaled", "normed", "gated", "msg_ready", "agg_mm", "acc_done"))
        block = ctx.enter_context(nc.Block())

        def use(item, u):
            return item // UNROLL + 1 if isinstance(item, int) else (item - u) // UNROLL + 1

        @block.sync
        def _(sp):
            sp.dma_start(w_edge[:], io["w1_edges"]).then_inc(w_in, 16)
            sp.dma_start(ln_g[:], io["ln_g"].broadcast_to([P, D])).then_inc(w_in, 16)
            sp.dma_start(ln_b[:, 0, :], io["ln_b"].broadcast_to([P, D])).then_inc(w_in, 16)
            passes = sp.value_load(ctl[0:1, 0:1], min_val=MIN_PASSES - 1, max_val=MAX_PASSES - 1) + 1

            loaded = {}

            def step(w, u, drained):
                if u == 0:
                    loaded["group"] = load_pass(nc, mybir.EngineType.SP, dram["item_group"], w, UNROLL, NG - 1)
                    loaded["base"] = load_pass(nc, mybir.EngineType.SP, dram["item_base"], w, UNROLL, NP - P)
                g, first = loaded["group"][u], loaded["base"][u]
                if u % BATCH == 0:
                    if reached(w, UNROLL):
                        sp.wait_ge(by_edge_built, w - UNROLL + BATCH)
                    sp.dma_start(base[:, u:u + BATCH],
                                 dram["item_base_f"][0:1, bass.ds(w, BATCH)].broadcast_to([P, BATCH])).then_inc(base_in[u // BATCH], 16)
                if reached(w, UNROLL):
                    sp.wait_ge(pre_summed, w - UNROLL + 1)
                sp.dma_start(meta[:, u], io["meta"][bass.ds(g, 1)].rearrange("a p k -> (a p) k")).then_inc(meta_in[u], 16)
                sp.dma_start(feat[:, u], io["edge_feat"][bass.ds(g, 1)].rearrange("a p k -> (a p) k")).then_inc(edge_in[u], 16)
                if reached(w, BATCH):
                    sp.wait_ge(pre_mm, w - BATCH + 1)
                sp.dma_start(b_win[:, u % BATCH], dram["b_table"][bass.ds(first, P), :]).then_inc(edge_in[u], 16)

            over_items(sp, step, passes, 0)

        @block.gpsimd
        def _(pool):
            passes = pool.value_load(ctl[0:1, 0:1], min_val=MIN_PASSES - 1, max_val=MAX_PASSES - 1) + 1

            def step(w, u, drained):
                pool.wait_ge(meta_in[u], 16 * use(w, u))
                if reached(w, UNROLL):
                    pool.wait_ge(pre_summed, w - UNROLL + 1)
                pool.sem_inc(started, 1)
                for i in range(TILES):
                    nc.gpsimd.indirect_dma_start(
                        gath[:, u, i, :], None, dram["a_table"],
                        bass.IndirectOffsetOnAxis(ap=meta[:, u, i:i + 1], axis=0)).then_inc(gathered[u], 16)

            over_items(pool, step, passes, 0)

        @block.tensor
        def _(pe):
            passes = pe.value_load(ctl[0:1, 0:1], min_val=MIN_PASSES - 1, max_val=MAX_PASSES - 1) + 1
            pe.wait_ge(centred, 1)

            def step(w, u, drained):
                if stage(w, drained, 1):
                    r, v, z = w - 1, (u - 1) % 2, (u - 1) % UNROLL
                    pe.wait_ge(by_edge_built, r + 1)
                    if reached(r, 2):
                        pe.wait_ge(by_node_built, r - 1)
                    for i in range(TILES):
                        last = nc.tensor.transpose(turned_ps[v][:, i * P:(i + 1) * P], by_edge[:, z, i, :], ident[:])
                    last.then_inc(turned, 1)
                if stage(w, drained, 5):
                    r, v, z = w - 5, (u - 5) % 2, (u - 5) % UNROLL
                    pe.wait_ge(msg_ready, r + 1)
                    if reached(r, 2):
                        pe.wait_ge(acc_done, r - 1)
                    for i in range(TILES):
                        nc.tensor.matmul(agg_ps[v][:, 0:P], msg[:, v, i, :], by_edge[:, z, i, :],
                                         start=(i == 0), stop=(i == TILES - 1))
                    for i in range(TILES):
                        last = nc.tensor.matmul(agg_ps[v][0:1, P:2 * P], gate[:, v, i:i + 1], by_edge[:, z, i, :],
                                                start=(i == 0), stop=(i == TILES - 1))
                    last.then_inc(agg_mm, 1)
                if stage(w, drained, 2):
                    r, v, z = w - 2, u % 2, (u - 2) % UNROLL
                    pe.wait_ge(edge_in[z], 32 * use(r, z))
                    if reached(r, 2):
                        pe.wait_ge(pre_summed, r - 1)
                    for t in range(2):
                        nc.tensor.matmul(pre_ps[v][:, t, 0:2 * PRE], feat[:, z, t * P:(t + 1) * P],
                                         w_edge[:].rearrange("p h d -> p (h d)"), start=True, stop=False)
                        if t == 0:
                            pe.wait_ge(by_node_built, r + 1)
                        for half in range(2):
                            i = 2 * t + half
                            for k in range(SPLITS):
                                last = nc.tensor.matmul(pre_ps[v][:, t, half * PRE:half * PRE + D],
                                                        by_node[:, v, i * P:(i + 1) * P], b_win[:, z % BATCH, k * D:(k + 1) * D],
                                                        start=False, stop=(half == 1 and k == SPLITS - 1))
                    last.then_inc(pre_mm, 1)

            over_items(pe, step, passes, SUM_LAG)

        @block.vector
        def _(dve):
            passes = dve.value_load(ctl[0:1, 0:1], min_val=MIN_PASSES - 1, max_val=MAX_PASSES - 1) + 1
            dve.wait_ge(w_in, 48)
            nc.vector.tensor_reduce(w_mean[:], w_edge[:, :, 0:D], AX.X, ALU.add).then_inc(chain, 1)
            dve.wait_ge(chain, 1)
            nc.vector.tensor_scalar(w_mean[:], w_mean[:], 1.0 / D, None, ALU.mult).then_inc(chain, 1)
            dve.wait_ge(chain, 2)
            for half in range(2):
                last = nc.vector.tensor_scalar(w_edge[:, half, 0:D], w_edge[:, half, 0:D], w_mean[:, half:half + 1],
                                               None, ALU.subtract)
            last.then_inc(centred, 1)
            loaded = {}

            def step(w, u, drained):
                if u == 0:
                    loaded["first"] = load_pass(nc, mybir.EngineType.DVE, dram["sum_base"], w,
                                                UNROLL if drained < 0 else SUM_LAG, NP - P)
                if stage(w, drained, 3):
                    r, v, z = w - 3, (u - 3) % 2, (u - 3) % UNROLL
                    dve.wait_ge(pre_mm, r + 1)
                    dve.wait_ge(gathered[z], 16 * TILES * use(r, z))
                    if reached(r, 2):
                        dve.wait_ge(normed_s, r - 1)
                    nc.vector.tensor_tensor(
                        pre[:, v].rearrange("p (t h) d -> p t h d", h=2),
                        pre_ps[v][:, :, 0:2 * PRE].rearrange("p t (h d) -> p t h d", h=2),
                        gath[:, z].rearrange("p (t h) d -> p t h d", h=2), ALU.add).then_inc(pre_summed, 1)
                if stage(w, drained, 4):
                    r, v = w - 4, u % 2
                    dve.wait_ge(measured, r + 1)
                    if reached(r, 2):
                        dve.wait_ge(agg_mm, r - 1)
                    nc.vector.tensor_scalar(gate[:, v], gexp[:, v], 1.0, None, ALU.add).then_inc(gated, 1)
                    for i in range(TILES):
                        last = nc.vector.scalar_tensor_tensor(out=msg[:, v, i, :], in0=pre[:, v, i, 0:D],
                                                              scalar=rstd[:, v, i:i + 1], in1=ln_g[:],
                                                              op0=ALU.mult, op1=ALU.mult)
                    last.then_inc(scaled, 1)
                    dve.wait_ge(gated, 2 * r + 1)
                    nc.vector.reciprocal(gate[:, v], gate[:, v]).then_inc(gated, 1)
                    dve.wait_ge(scaled, r + 1)
                    nc.vector.tensor_tensor(msg[:, v], msg[:, v], ln_b[:].broadcast_to([P, TILES, D]),
                                            ALU.add).then_inc(normed_s, 1)
                if stage(w, drained, 0):
                    dve.wait_ge(meta_in[u], 16 * use(w, u))
                    dve.wait_ge(base_in[u // BATCH], 16 * use(w, u))
                    if reached(w, UNROLL):
                        dve.wait_ge(agg_mm, w - UNROLL + 1)
                    nc.vector.scalar_tensor_tensor(
                        out=by_edge[:, u], in0=iota[:].unsqueeze(1).broadcast_to([P, TILES, P]), scalar=base[:, u:u + 1],
                        in1=meta[:, u, TILES:2 * TILES].unsqueeze(2).broadcast_to([P, TILES, P]),
                        op0=ALU.add, op1=ALU.is_equal).then_inc(by_edge_built, 1)
                if stage(w, drained, SUM_LAG):
                    r, v, first = w - SUM_LAG, u % 2, loaded["first"][u]
                    dve.wait_ge(agg_mm, r + 1)
                    if reached(r, 1):
                        dve.wait_ge(acc_done, r)
                    nc.vector.tensor_tensor(agg[0:1, 1, bass.ds(first, P)], agg[0:1, 1, bass.ds(first, P)],
                                            agg_ps[v][0:1, P:2 * P], ALU.add)
                    nc.vector.tensor_tensor(agg[:, 0, bass.ds(first, P)], agg[:, 0, bass.ds(first, P)],
                                            agg_ps[v][:, 0:P], ALU.add).then_inc(acc_done, 1)

            over_items(dve, step, passes, SUM_LAG)

        @block.scalar
        def _(act):
            nc.scalar.preload_act_table_set("natural_log_exp_and_others")
            passes = act.value_load(ctl[0:1, 0:1], min_val=MIN_PASSES - 1, max_val=MAX_PASSES - 1) + 1

            def step(w, u, drained):
                if stage(w, drained, 1):
                    r, v = w - 1, (u - 1) % 2
                    act.wait_ge(turned, r + 1)
                    if reached(r, 2):
                        act.wait_ge(pre_mm, r - 1)
                    nc.scalar.copy(by_node[:, v], turned_ps[v][:]).then_inc(by_node_built, 1)
                if stage(w, drained, 3):
                    r, v = w - 3, (u - 3) % 2
                    act.wait_ge(pre_summed, r + 1)
                    if reached(r, 2):
                        act.wait_ge(normed_s, r - 1)
                        act.wait_ge(gated, 2 * r - 2)
                    if reached(r, 1):
                        act.wait_ge(measured, r)
                    for i in range(TILES):
                        if i or reached(r, 1):
                            act.wait_ge(squares, TILES * r + i)
                        nc.scalar.activation(junk[:], pre[:, v, i, 0:D], ACT.Square,
                                             accum_out=ss[:, i:i + 1]).then_inc(squares, 1)
                    nc.scalar.activation(gexp[:, v], pre[:, v, :, D], ACT.Exp, scale=-1.0)
                    act.wait_ge(squares, TILES * (r + 1))
                    nc.scalar.activation(rstd[:, v], ss[:], ACT.Ln, bias=keep["eps"][:], scale=1.0 / D).then_inc(logs, 1)
                    act.wait_ge(logs, r + 1)
                    nc.scalar.activation(rstd[:, v], rstd[:, v], ACT.Exp, scale=-0.5).then_inc(measured, 1)
                if stage(w, drained, 4):
                    r, v = w - 4, u % 2
                    act.wait_ge(normed_s, r + 1)
                    act.wait_ge(gated, 2 * r + 2)
                    for i in range(TILES):
                        last = nc.scalar.activation(msg[:, v, i, :], msg[:, v, i, :], ACT.Relu,
                                                    scale=gate[:, v, i:i + 1])
                    last.then_inc(msg_ready, 1)

            over_items(act, step, passes, SUM_LAG)


def gru_nodes(nc, io, dram, keep, NP):
    agg, ident, nodes = keep["agg"], keep["ident"], keep["nodes"]
    NQ = NP // QUAD
    UP = 1.0 / float(MUL) ** 0.5
    GRU_LAG, GRU_PEEL, UP_LAG, UP_PEEL = 4, 8, 2, 4
    with ExitStack() as ctx:
        def sb(name, shape, dt):
            return ctx.enter_context(nc.sbuf_tensor("gru_" + name, shape, dt))

        def pb(name):
            return ctx.enter_context(nc.psum_tensor("gru_" + name, [P, QUAD], F32))

        def sem(name):
            return ctx.enter_context(nc.semaphore("gru_" + name))

        w2 = sb("w2", [P, D], F32)
        b2 = sb("b2", [1, D], F32)
        w_ih = sb("w_ih", [P, 3 * D], F32)
        w_hh = sb("w_hh", [P, 3 * D], F32)
        b_ih = sb("b_ih", [P, 3], F32)
        b_hh = sb("b_hh", [P, 3], F32)
        b_sum = sb("b_sum", [P, 3], F32)
        w_up = sb("w_up", [P, D], F32)
        x = sb("x", [P, SLOTS, 4, D], F32)
        mT = sb("mT", [P, 2, QUAD], F32)
        rT = sb("rT", [P, QUAD], F32)
        zT = sb("zT", [P, 2, QUAD], F32)
        nT = sb("nT", [P, 2, QUAD], F32)
        oT = sb("oT", [P, 2, QUAD], F32)
        x1 = sb("x1", [P, 2, 4, D], F32)
        stats = sb("stats", [P, 2, 4, 6], F32)
        mv = sb("mv", [P, 2, 4, 2], F32)
        mv_all = sb("mv_all", [P, 4 * NQ, 2], F32)
        rstd = sb("rstd", [P, 4 * NQ], F32)
        h2 = sb("h2", [P, 2, 4, D], F32)
        h2T = sb("h2T", [P, 2, QUAD], F32)
        up = sb("up", [P, SLOTS, 4, D], F32)
        m_ps, r_ps, z_ps, i_ps, n_ps, o_ps, h_ps, u_ps = (pb(n) for n in (
            "m_ps", "r_ps", "z_ps", "i_ps", "n_ps", "o_ps", "h_ps", "u_ps"))
        h_pair, u_pair = [h_ps, r_ps], [u_ps, z_ps]

        w_in, biases = sem("w_in"), sem("biases")
        x_in = [sem(f"x_in{s}") for s in range(SLOTS)]
        m_mm, m_copied, rz_mm, in_mm, rz_ready = (sem(n) for n in ("m_mm", "m_copied", "rz_mm", "in_mm", "rz_ready"))
        n_in, n_ready, diff, mixed, o_turned = (sem(n) for n in ("n_in", "n_ready", "diff", "mixed", "o_turned"))
        joining = sem("joining")
        x1_ready, measured, moments, noted, kept, rooted, inverted = (sem(n) for n in (
            "x1_ready", "measured", "moments", "noted", "kept", "rooted", "inverted"))
        normed, h_turned, h2T_ready, u_mm, u_ready = (sem(n) for n in ("normed", "h_turned", "h2T_ready", "u_mm", "u_ready"))
        u_stored = [sem(f"u_stored{s}") for s in range(SLOTS)]
        cleared = sem("cleared")
        block = ctx.enter_context(nc.Block())

        def flat(t):
            return t.rearrange("p t d -> p (t d)")

        @block.sync
        def _(sp):
            for tile, name in ((w2, "w2"), (b2, "b2"), (w_ih, "w_ih"), (w_hh, "w_hh"), (b_ih, "b_ih"), (b_hh, "b_hh"), (w_up, "w_up")):
                sp.dma_start(tile[:], io[name]).then_inc(w_in, 16)

            def gru_step(q, s):
                if has_quad(q, NQ):
                    if reached(q, SLOTS):
                        sp.wait_ge(x1_ready, q - SLOTS + 1)
                    sp.dma_start(x[:, s], quad_rows(io["x"], q)).then_inc(x_in[s], 16)

            def up_step(q, s):
                if has_quad(q - 2, NQ):
                    r, z = q - 2, (s - 2) % SLOTS
                    sp.wait_ge(u_ready, r + 1)
                    sp.dma_start(quad_rows(dram["u_table"], r), up[:, z]).then_inc(u_stored[z], 16)

            over_quads(sp, gru_step, NQ, 0, GRU_PEEL)
            over_quads(sp, up_step, NQ, UP_LAG, UP_PEEL)
            for s in range(SLOTS):
                if NQ > s:
                    sp.wait_ge(u_stored[s], 16 * ((NQ - s - 1) // SLOTS + 1))

        @block.tensor
        def _(pe):
            pe.wait_ge(w_in, 16 * 7)

            def gru_step(q, s):
                if has_quad(q, NQ):
                    cols = bass.ds(q * QUAD, QUAD)
                    if reached(q, 1):
                        pe.wait_ge(m_copied, q)
                    nc.tensor.matmul(m_ps[:], w2[:], agg[:, 0, cols], start=True, stop=False)
                    nc.tensor.matmul(m_ps[:], b2[:], agg[0:1, 1, cols], start=False, stop=True).then_inc(m_mm, 1)
                if has_quad(q - 1, NQ):
                    r, v = q - 1, (s - 1) % 2
                    cols = bass.ds(r * QUAD, QUAD)
                    if reached(r, 1):
                        pe.wait_ge(rz_ready, 2 * r)
                    pe.wait_ge(m_copied, r + 1)
                    for k, out in enumerate((r_ps, z_ps)):
                        nc.tensor.matmul(out[:], w_hh[:, k * D:(k + 1) * D], nodes[:, cols], start=True, stop=False)
                        nc.tensor.matmul(out[:], w_ih[:, k * D:(k + 1) * D], mT[:, v], start=False, stop=True).then_inc(rz_mm, 1)
                    if reached(r, 1):
                        pe.wait_ge(n_in, 2 * r)
                    nc.tensor.matmul(n_ps[:], w_hh[:, 2 * D:3 * D], nodes[:, cols], start=True, stop=True)
                    nc.tensor.matmul(i_ps[:], w_ih[:, 2 * D:3 * D], mT[:, v], start=True, stop=True).then_inc(in_mm, 1)
                if has_quad(q - 3, NQ):
                    r, v = q - 3, (s - 3) % 2
                    pe.wait_ge(mixed, 2 * r + 2)
                    if reached(r, 1):
                        pe.wait_ge(x1_ready, r)
                    for t in range(4):
                        last = nc.tensor.transpose(o_ps[:, t * P:(t + 1) * P], oT[:, v, t * P:(t + 1) * P], ident[:])
                    last.then_inc(o_turned, 1)

            def up_step(q, s):
                if has_quad(q - 1, NQ):
                    r, v = q - 1, (s - 1) % 2
                    pe.wait_ge(normed, r + 1)
                    if reached(r, 2):
                        pe.wait_ge(h2T_ready, r - 1)
                    for t in range(4):
                        last = nc.tensor.transpose(h_pair[v][:, t * P:(t + 1) * P], h2[:, v, t, :], ident[:])
                    last.then_inc(h_turned, 1)
                if has_quad(q - 2, NQ):
                    r, v = q - 2, s % 2
                    pe.wait_ge(h2T_ready, r + 1)
                    if reached(r, 2):
                        pe.wait_ge(u_ready, r - 1)
                    for t in range(4):
                        last = nc.tensor.matmul(u_pair[v][:, t * P:(t + 1) * P], h2T[:, v, t * P:(t + 1) * P], w_up[:], start=True, stop=True)
                    last.then_inc(u_mm, 1)

            over_quads(pe, gru_step, NQ, GRU_LAG, GRU_PEEL)
            over_quads(pe, up_step, NQ, UP_LAG, UP_PEEL)

        @block.scalar
        def _(act):
            act.wait_ge(biases, 1)

            def gru_step(q, s):
                if has_quad(q - 2, NQ):
                    r, v = q - 2, s % 2
                    act.wait_ge(n_in, 2 * r + 2)
                    nc.scalar.activation(nT[:, v], nT[:, v], ACT.Tanh, bias=b_ih[:, 2:3]).then_inc(n_ready, 1)
                if has_quad(q, NQ):
                    v = s % 2
                    act.wait_ge(m_mm, q + 1)
                    if reached(q, 2):
                        act.wait_ge(in_mm, q - 1)
                    nc.scalar.copy(mT[:, v], m_ps[:]).then_inc(m_copied, 1)
                if has_quad(q - 1, NQ):
                    r, v = q - 1, (s - 1) % 2
                    act.wait_ge(rz_mm, 2 * r + 1)
                    if reached(r, 1):
                        act.wait_ge(n_in, 2 * r)
                    nc.scalar.activation(rT[:], r_ps[:], ACT.Sigmoid, bias=b_sum[:, 0:1]).then_inc(rz_ready, 1)
                    act.wait_ge(rz_mm, 2 * r + 2)
                    if reached(r, 2):
                        act.wait_ge(mixed, 2 * r - 3)
                    nc.scalar.activation(zT[:, v], z_ps[:], ACT.Sigmoid, bias=b_sum[:, 1:2]).then_inc(rz_ready, 1)

            def up_step(q, s):
                if has_quad(q - 1, NQ):
                    r, v = q - 1, (s - 1) % 2
                    act.wait_ge(h_turned, r + 1)
                    if reached(r, 2):
                        act.wait_ge(u_mm, r - 1)
                    nc.scalar.activation(h2T[:, v], h_pair[v][:], ACT.Relu).then_inc(h2T_ready, 1)
                if has_quad(q - 2, NQ):
                    r, v, z = q - 2, s % 2, (s - 2) % SLOTS
                    act.wait_ge(u_mm, r + 1)
                    if reached(r, SLOTS):
                        act.wait_ge(u_stored[z], 16 * (quad_use(r, z) - 1))
                    nc.scalar.activation(flat(up[:, z]), u_pair[v][:], ACT.Copy, scale=UP).then_inc(u_ready, 1)

            over_quads(act, gru_step, NQ, GRU_LAG, GRU_PEEL)
            act.wait_ge(noted, NQ)
            nc.scalar.activation(rstd[:], mv_all[:, :, 1], ACT.Sqrt, bias=keep["eps"][:]).then_inc(rooted, 1)
            over_quads(act, up_step, NQ, UP_LAG, UP_PEEL)

        @block.gpsimd
        def _(pool):
            def gru_step(q, s):
                if has_quad(q - 2, NQ):
                    r, v = q - 2, s % 2
                    pool.wait_ge(diff, r + 1)
                    nc.gpsimd.tensor_tensor(oT[:, v], oT[:, v], zT[:, v], ALU.mult).then_inc(mixed, 1)
                    pool.wait_ge(mixed, 2 * r + 1)
                    nc.gpsimd.tensor_tensor(oT[:, v], oT[:, v], nT[:, v], ALU.add).then_inc(mixed, 1)

            over_quads(pool, gru_step, NQ, GRU_LAG, GRU_PEEL)
            pool.wait_ge(m_mm, NQ)
            nc.gpsimd.memset(agg[:], 0.0).then_inc(cleared, 1)
            pool.wait_ge(cleared, 1)

        @block.vector
        def _(dve):
            dve.wait_ge(w_in, 16 * 7)
            nc.vector.tensor_tensor(b_sum[:], b_ih[:], b_hh[:], ALU.add).then_inc(biases, 1)

            def gru_step(q, s):
                if has_quad(q - 4, NQ):
                    r, z, v = q - 4, s, s % 2
                    dve.wait_ge(o_turned, r + 1)
                    dve.wait_ge(x_in[z], 16 * quad_use(r, z))
                    if reached(r, 2):
                        dve.wait_ge(kept, r - 1)
                    nc.vector.tensor_tensor(flat(x1[:, v]), flat(x[:, z]), o_ps[:], ALU.add).then_inc(x1_ready, 1)
                    dve.wait_ge(x1_ready, r + 1)
                    if reached(r, 2):
                        dve.wait_ge(moments, r - 1)
                    dve.sem_inc(joining, 1)
                    for t in range(4):
                        last = nc.vector.bn_stats(stats[:, v, t, :], x1[:, v, t, :])
                    last.then_inc(measured, 1)
                    nc.vector.tensor_copy(nodes[:, bass.ds(r * QUAD, QUAD)], flat(x1[:, v])).then_inc(kept, 1)
                    dve.wait_ge(measured, r + 1)
                    if reached(r, 2):
                        dve.wait_ge(noted, r - 1)
                    dve.sem_inc(joining, 1)
                    for t in range(4):
                        last = nc.vector.bn_aggr(mv[:, v, t, :], stats[:, v, t, :])
                    last.then_inc(moments, 1)
                if has_quad(q - 2, NQ):
                    r, v = q - 2, s % 2
                    dve.wait_ge(n_ready, r + 1)
                    if reached(r, 2):
                        dve.wait_ge(o_turned, r - 1)
                    nc.vector.tensor_tensor(oT[:, v], nodes[:, bass.ds(r * QUAD, QUAD)], nT[:, v], ALU.subtract).then_inc(diff, 1)
                if has_quad(q - 4, NQ):
                    r, v = q - 4, s % 2
                    dve.wait_ge(moments, r + 1)
                    nc.vector.tensor_copy(mv_all[:, bass.ds(4 * r, 4), :], mv[:, v]).then_inc(noted, 1)
                if has_quad(q - 1, NQ):
                    r, v = q - 1, (s - 1) % 2
                    dve.wait_ge(in_mm, r + 1)
                    dve.wait_ge(rz_ready, 2 * r + 1)
                    if reached(r, 2):
                        dve.wait_ge(mixed, 2 * r - 2)
                    nc.vector.scalar_tensor_tensor(out=nT[:, v], in0=n_ps[:], scalar=b_hh[:, 2:3], in1=rT[:],
                                                   op0=ALU.add, op1=ALU.mult).then_inc(n_in, 1)
                    dve.wait_ge(n_in, 2 * r + 1)
                    nc.vector.tensor_tensor(nT[:, v], nT[:, v], i_ps[:], ALU.add).then_inc(n_in, 1)

            def up_step(q, s):
                if has_quad(q, NQ):
                    v = s % 2
                    if reached(q, 2):
                        dve.wait_ge(h_turned, q - 1)
                    for t in range(4):
                        last = nc.vector.tensor_scalar(h2[:, v, t, :], nodes[:, bass.ds(q * QUAD + t * P, P)],
                                                       mv_all[:, bass.ds(4 * q + t, 1), 0], rstd[:, bass.ds(4 * q + t, 1)],
                                                       ALU.subtract, ALU.mult)
                    last.then_inc(normed, 1)

            over_quads(dve, gru_step, NQ, GRU_LAG, GRU_PEEL)
            dve.wait_ge(kept, NQ)
            dve.wait_ge(rooted, 1)
            nc.vector.reciprocal(rstd[:], rstd[:]).then_inc(inverted, 1)
            dve.wait_ge(inverted, 1)
            over_quads(dve, up_step, NQ, UP_LAG, UP_PEEL)


def tensor_edges(nc, io, dram, keep, NP, NG, J):
    agg, iota, ctl = keep["agg"], keep["iota"], keep["ctl"]
    MIN_PASSES, MAX_PASSES = NG // UNROLL, P * J // UNROLL
    HALF = GROUP // 2
    KIN = 2 * NB
    VEC = slice(MUL, 4 * MUL)
    with ExitStack() as ctx:
        def sb(name, shape, dt):
            return ctx.enter_context(nc.sbuf_tensor("tensor_" + name, shape, dt))

        def pb(name, shape):
            return ctx.enter_context(nc.psum_tensor("tensor_" + name, shape, F32))

        def sem(name):
            return ctx.enter_context(nc.semaphore("tensor_" + name))

        mlp0 = sb("mlp0", [P, P], F32)
        mlp1 = sb("mlp1", [P, P], F32)
        mlp2 = sb("mlp2", [P, 2 * D], F32)
        bias0 = sb("bias0", [P, 1], F32)
        bias1 = sb("bias1", [P, 1], F32)
        bias2 = sb("bias2", [1, 2 * D], F32)
        bias2_rest = sb("bias2_rest", [1, 2 * D], F32)
        bias2_part = sb("bias2_part", [1, SPLITS, 2 * D], BF16)
        ones = sb("ones", [1, P], BF16)
        meta = sb("meta", [P, UNROLL, 2 * TILES], I32)
        base = sb("base", [P, UNROLL], F32)
        y = sb("y", [P, UNROLL, TILES, 3], F32)
        emb = sb("emb", [P, UNROLL, HALF], F32)
        gath = sb("gath", [P, UNROLL, TILES, D], F32)
        h0 = sb("h0", [P, 2, HALF], F32)
        h1 = sb("h1", [P, 2, HALF], F32)
        by_edge = sb("by_edge", [P, 2, TILES, P], F32)
        msg = sb("msg", [P, 2, TILES, MSG], F32)
        prod = sb("prod", [P, TILES, 3, MUL], F32)
        dot = sb("dot", [P, TILES, MUL], F32)
        h0_ps = pb("h0_ps", [P, 512])
        h1_ps = pb("h1_ps", [P, 512])
        w_ps = [pb(f"w_ps{i}", [P, TILES, D]) for i in range(2)]
        agg_ps = [pb(f"agg_ps{i}", [P, 512]) for i in range(4)]

        w_in, cleared, split, ready = sem("w_in"), sem("cleared"), sem("split"), sem("ready")
        meta_in, edge_in, gathered, base_in, started = (keep[k] for k in ("meta_in", "edge_in", "gathered", "base_in", "started"))
        h0_mm, h0_ready, h1_mm, h1_ready, w_mm = (sem(n) for n in ("h0_mm", "h0_ready", "h1_mm", "h1_ready", "w_mm"))
        built, scal, prods, dots, msg_ready, agg_mm, acc_done = (sem(n) for n in ("built", "scal", "prods", "dots", "msg_ready", "agg_mm", "acc_done"))
        block = ctx.enter_context(nc.Block())

        def use(item, u):
            return item // UNROLL + 1 if isinstance(item, int) else (item - u) // UNROLL + 1

        @block.sync
        def _(sp):
            for tile, name in ((mlp0, "mlp0"), (mlp1, "mlp1"), (mlp2, "mlp2"), (bias0, "mlp_b0"), (bias1, "mlp_b1"), (bias2, "mlp_b2")):
                sp.dma_start(tile[:], io[name]).then_inc(w_in, 16)
            passes = sp.value_load(ctl[0:1, 0:1], min_val=MIN_PASSES - 1, max_val=MAX_PASSES - 1) + 1
            sp.wait_ge(cleared, 1)

            loaded = {}

            def step(w, u, drained):
                if u == 0:
                    loaded["group"] = load_pass(nc, mybir.EngineType.SP, dram["item_group"], w, UNROLL, NG - 1)
                g = loaded["group"][u]
                if u % BATCH == 0:
                    if reached(w, UNROLL):
                        sp.wait_ge(built, w - UNROLL + BATCH)
                    sp.dma_start(base[:, u:u + BATCH],
                                 dram["item_base_f"][0:1, bass.ds(w, BATCH)].broadcast_to([P, BATCH])).then_inc(base_in[u // BATCH], 16)
                if reached(w, UNROLL):
                    sp.wait_ge(msg_ready, w - UNROLL + 1)
                sp.dma_start(meta[:, u], io["meta"][bass.ds(g, 1)].rearrange("a p k -> (a p) k")).then_inc(meta_in[u], 16)
                sp.dma_start(y[:, u].rearrange("p i k -> p (i k)"),
                             dram["y_edges"][:, bass.ds(g * (TILES * 3), TILES * 3)]).then_inc(edge_in[u], 16)
                for half in range(2):
                    sp.dma_start(emb[half * NB:(half + 1) * NB, u],
                                 dram["emb_edges"][:, bass.ds(g * GROUP + half * HALF, HALF)]).then_inc(edge_in[u], 16)

            over_items(sp, step, passes, 0)

        @block.gpsimd
        def _(pool):
            passes = pool.value_load(ctl[0:1, 0:1], min_val=MIN_PASSES - 1, max_val=MAX_PASSES - 1) + 1
            meta_before = pool.snap(16 * passes)

            def step(w, u, drained):
                pool.wait_ge(meta_in[u], 16 * use(w, u) + meta_before)
                if reached(w, UNROLL):
                    pool.wait_ge(msg_ready, w - UNROLL + 1)
                pool.sem_inc(started, 1)
                for i in range(TILES):
                    nc.gpsimd.indirect_dma_start(
                        gath[:, u, i, :], None, dram["u_table"],
                        bass.IndirectOffsetOnAxis(ap=meta[:, u, i:i + 1], axis=0)).then_inc(gathered[u], 16)

            over_items(pool, step, passes, 0)

        @block.tensor
        def _(pe):
            passes = pe.value_load(ctl[0:1, 0:1], min_val=MIN_PASSES - 1, max_val=MAX_PASSES - 1) + 1
            edges_before = pe.snap(32 * passes)
            pe.wait_ge(ready, 1)
            pe.wait_ge(w_in, 16 * 6)

            def step(w, u, drained):
                if stage(w, drained, 2):
                    r, v = w - 2, u % 2
                    pe.wait_ge(h1_ready, r + 1)
                    if reached(r, 2):
                        pe.wait_ge(msg_ready, r - 1)
                    for t in range(2):
                        out = w_ps[v][:, 2 * t:2 * t + 2, :].rearrange("p h d -> p (h d)")
                        for k in range(SPLITS):
                            nc.tensor.matmul(out, ones[:], bias2_part[:, k, :], start=(k == 0), stop=False)
                        last = nc.tensor.matmul(out, h1[:, v, t * P:(t + 1) * P], mlp2[:], start=False, stop=True)
                    last.then_inc(w_mm, 1)
                if stage(w, drained, 0):
                    pe.wait_ge(edge_in[u], 48 * use(w, u) + edges_before)
                    if reached(w, 1):
                        pe.wait_ge(h0_ready, w)
                    nc.tensor.matmul(h0_ps[:, 0:HALF], mlp0[:], emb[:, u], start=True, stop=True).then_inc(h0_mm, 1)
                if stage(w, drained, 1):
                    r, v = w - 1, (u + 1) % 2
                    pe.wait_ge(h0_ready, r + 1)
                    if reached(r, 1):
                        pe.wait_ge(h1_ready, r)
                    nc.tensor.matmul(h1_ps[:, 0:HALF], mlp1[:], h0[:, v], start=True, stop=True).then_inc(h1_mm, 1)
                if stage(w, drained, 4):
                    r, v, a = w - 4, u % 2, u % 4
                    pe.wait_ge(msg_ready, r + 1)
                    if reached(r, 4):
                        pe.wait_ge(acc_done, r - 3)
                    for c in range(2):
                        for i in range(TILES):
                            last = nc.tensor.matmul(agg_ps[a][:, c * P:(c + 1) * P],
                                                    msg[:, v, i, MUL + c * P:MUL + (c + 1) * P], by_edge[:, v, i, :],
                                                    start=(i == 0), stop=(i == TILES - 1))
                    last.then_inc(agg_mm, 1)

            over_items(pe, step, passes, SUM_LAG)

        @block.scalar
        def _(act):
            passes = act.value_load(ctl[0:1, 0:1], min_val=MIN_PASSES - 1, max_val=MAX_PASSES - 1) + 1
            act.wait_ge(w_in, 16 * 6)

            def step(w, u, drained):
                if stage(w, drained, 0):
                    v = u % 2
                    act.wait_ge(h0_mm, w + 1)
                    if reached(w, 2):
                        act.wait_ge(h1_mm, w - 1)
                    nc.scalar.activation(h0[:, v], h0_ps[:, 0:HALF], ACT.Silu, bias=bias0[:]).then_inc(h0_ready, 1)
                if stage(w, drained, 1):
                    r, v = w - 1, (u + 1) % 2
                    act.wait_ge(h1_mm, r + 1)
                    if reached(r, 2):
                        act.wait_ge(w_mm, r - 1)
                    nc.scalar.activation(h1[:, v], h1_ps[:, 0:HALF], ACT.Silu, bias=bias1[:]).then_inc(h1_ready, 1)

            over_items(act, step, passes, 1)

        @block.vector
        def _(dve):
            passes = dve.value_load(ctl[0:1, 0:1], min_val=MIN_PASSES - 1, max_val=MAX_PASSES - 1) + 1
            meta_before = dve.snap(16 * passes)
            edges_before = dve.snap(32 * passes)
            gathers_before = dve.snap(16 * TILES * passes)
            nc.vector.memset(emb[:], 0.0).then_inc(cleared, 1)
            nc.vector.memset(ones[:], 1.0)
            dve.wait_ge(w_in, 16 * 6)
            nc.vector.tensor_copy(bias2_part[:, 0, :], bias2[:]).then_inc(split, 1)
            dve.wait_ge(split, 1)
            nc.vector.tensor_tensor(bias2_rest[:], bias2[:], bias2_part[:, 0, :], ALU.subtract).then_inc(split, 1)
            dve.wait_ge(split, 2)
            nc.vector.tensor_copy(bias2_part[:, 1, :], bias2_rest[:]).then_inc(split, 1)
            dve.wait_ge(split, 3)
            nc.vector.tensor_tensor(bias2_rest[:], bias2_rest[:], bias2_part[:, 1, :], ALU.subtract).then_inc(split, 1)
            dve.wait_ge(split, 4)
            nc.vector.tensor_copy(bias2_part[:, 2, :], bias2_rest[:]).then_inc(ready, 1)

            loaded = {}

            def step(w, u, drained):
                if u == 0:
                    loaded["first"] = load_pass(nc, mybir.EngineType.DVE, dram["sum_base"], w,
                                                UNROLL if drained < 0 else SUM_LAG, NP - P)
                if stage(w, drained, SUM_LAG):
                    r, a, first = w - SUM_LAG, (u - SUM_LAG) % 4, loaded["first"][u]
                    dve.wait_ge(agg_mm, r + 1)
                    if reached(r, 1):
                        dve.wait_ge(acc_done, r)
                    nc.vector.tensor_tensor(agg[:, :, bass.ds(first, P)], agg[:, :, bass.ds(first, P)],
                                            agg_ps[a][:, 0:2 * P].rearrange("p (c n) -> p c n", c=2), ALU.add).then_inc(acc_done, 1)
                if stage(w, drained, 3):
                    r, v, z = w - 3, (u - 3) % 2, (u - 3) % UNROLL
                    dve.wait_ge(meta_in[z], 16 * use(r, z) + meta_before)
                    if reached(r, 2):
                        dve.wait_ge(agg_mm, r - 1)
                    dve.wait_ge(base_in[z // BATCH], 16 * use(r, z) + meta_before)
                    nc.vector.scalar_tensor_tensor(
                        out=by_edge[:, v], in0=iota[:].unsqueeze(1).broadcast_to([P, TILES, P]), scalar=base[:, z:z + 1],
                        in1=meta[:, z, TILES:2 * TILES].unsqueeze(2).broadcast_to([P, TILES, P]),
                        op0=ALU.add, op1=ALU.is_equal).then_inc(built, 1)
                    dve.wait_ge(gathered[z], 16 * TILES * use(r, z) + gathers_before)
                    dve.wait_ge(edge_in[z], 48 * use(r, z) + edges_before)
                    m, g, wt = msg[:, v], gath[:, z], w_ps[v]
                    vec = g[:, :, VEC].rearrange("p i (c k) -> p i c k", c=3)
                    if reached(r, 1):
                        dve.wait_ge(dots, r)
                    nc.vector.tensor_tensor(prod[:], vec, y[:, z].unsqueeze(3).broadcast_to([P, TILES, 3, MUL]),
                                            ALU.mult).then_inc(prods, 1)
                    dve.wait_ge(w_mm, r + 1)
                    nc.vector.tensor_tensor(m[:, :, 0:2 * MUL].rearrange("p i (j k) -> p i j k", j=2),
                                            wt[:, :, 0:2 * MUL].rearrange("p i (j k) -> p i j k", j=2),
                                            g[:, :, 0:MUL].unsqueeze(2).broadcast_to([P, TILES, 2, MUL]), ALU.mult).then_inc(scal, 1)
                    dve.wait_ge(prods, r + 1)
                    if reached(r, 1):
                        dve.wait_ge(msg_ready, r)
                    nc.vector.tensor_reduce(dot[:], prod[:].rearrange("p i c k -> p i k c"), AX.X, ALU.add).then_inc(dots, 1)
                    nc.vector.tensor_tensor(m[:, :, 3 * MUL:6 * MUL].rearrange("p i (c k) -> p i c k", c=3), vec,
                                            wt[:, :, 3 * MUL:4 * MUL].unsqueeze(2).broadcast_to([P, TILES, 3, MUL]), ALU.mult)
                    dve.wait_ge(scal, r + 1)
                    nc.vector.tensor_tensor(m[:, :, 6 * MUL:9 * MUL].rearrange("p i (c k) -> p i c k", c=3),
                                            m[:, :, 0:MUL].unsqueeze(2).broadcast_to([P, TILES, 3, MUL]),
                                            y[:, z].unsqueeze(3).broadcast_to([P, TILES, 3, MUL]), ALU.mult)
                    dve.wait_ge(dots, r + 1)
                    nc.vector.scalar_tensor_tensor(out=m[:, :, 2 * MUL:3 * MUL], in0=dot[:], scalar=1.0 / SQ3,
                                                   in1=wt[:, :, 2 * MUL:3 * MUL], op0=ALU.mult, op1=ALU.mult).then_inc(msg_ready, 1)

            over_items(dve, step, passes, SUM_LAG)


def output_nodes(nc, io, dram, keep, NP):
    agg, nodes = keep["agg"], keep["nodes"]
    NQ = NP // QUAD
    LAG, PEEL = 3, 4
    SCALE = 1.0 / (float(2 * MUL) ** 0.5 * 16.0)
    with ExitStack() as ctx:
        def sb(name, shape, dt):
            return ctx.enter_context(nc.sbuf_tensor("final_" + name, shape, dt))

        def sem(name):
            return ctx.enter_context(nc.semaphore("final_" + name))

        w_out = sb("w_out", [P, 2, D], F32)
        sums = sb("sums", [P, SLOTS, 2, QUAD], F32)
        out = sb("out", [P, SLOTS, QUAD], F32)
        out_ps = [ctx.enter_context(nc.psum_tensor(f"final_out_ps{i}", [P, QUAD], F32)) for i in range(SLOTS)]
        w_in = sem("w_in")
        stored = [sem(f"stored{s}") for s in range(SLOTS)]
        copied = [sem("copied0"), sem("copied1")]
        out_mm, out_ready = sem("out_mm"), sem("out_ready")
        block = ctx.enter_context(nc.Block())

        @block.sync
        def _(sp):
            sp.dma_start(w_out[:], io["w_out"]).then_inc(w_in, 16)

            def step(q, s):
                if has_quad(q - 3, NQ):
                    r, z = q - 3, (s - 3) % SLOTS
                    sp.wait_ge(out_ready, r + 1)
                    sp.dma_start(quad_rows(io["out"], r), out[:, z].rearrange("p (t d) -> p t d", d=D)).then_inc(stored[z], 16)

            over_quads(sp, step, NQ, LAG, PEEL)
            for s in range(SLOTS):
                if NQ > s:
                    sp.wait_ge(stored[s], 16 * ((NQ - s - 1) // SLOTS + 1))

        @block.scalar
        def _(act):
            def step(q, s):
                if has_quad(q, NQ):
                    if reached(q, SLOTS):
                        act.wait_ge(out_mm, q - SLOTS + 1)
                    nc.scalar.copy(sums[:, s, 0], agg[:, 0, bass.ds(q * QUAD, QUAD)]).then_inc(copied[0], 1)

            over_quads(act, step, NQ, LAG, PEEL)

        @block.tensor
        def _(pe):
            pe.wait_ge(w_in, 16)

            def step(q, s):
                if has_quad(q - 1, NQ):
                    r, z = q - 1, (s - 1) % SLOTS
                    for c in range(2):
                        pe.wait_ge(copied[c], r + 1)
                    if reached(r, SLOTS):
                        pe.wait_ge(out_ready, r - SLOTS + 1)
                    for t in range(4):
                        for c in range(2):
                            last = nc.tensor.matmul(out_ps[z][:, t * P:(t + 1) * P], sums[:, z, c, t * P:(t + 1) * P], w_out[:, c, :],
                                                    start=(c == 0), stop=(c == 1))
                    last.then_inc(out_mm, 1)

            over_quads(pe, step, NQ, LAG, PEEL)

        @block.vector
        def _(dve):
            def step(q, s):
                if has_quad(q, NQ):
                    if reached(q, SLOTS):
                        dve.wait_ge(out_mm, q - SLOTS + 1)
                    nc.vector.tensor_copy(sums[:, s, 1], agg[:, 1, bass.ds(q * QUAD, QUAD)]).then_inc(copied[1], 1)
                if has_quad(q - 2, NQ):
                    r, z = q - 2, (s - 2) % SLOTS
                    dve.wait_ge(out_mm, r + 1)
                    if reached(r, SLOTS):
                        dve.wait_ge(stored[z], 16 * (quad_use(r, z) - 1))
                    nc.vector.scalar_tensor_tensor(out=out[:, z], in0=out_ps[z][:], scalar=SCALE, in1=nodes[:, bass.ds(r * QUAD, QUAD)],
                                                   op0=ALU.mult, op1=ALU.add).then_inc(out_ready, 1)

            over_quads(dve, step, NQ, LAG, PEEL)


def kernel(**inputs):
    import numpy as np
    import concourse.bacc as bacc
    from concourse.bass_utils import run_bass_kernel_spmd

    a = {k: np.asarray(v) for k, v in inputs.items()}
    N, E = a["x"].shape[0], a["src"].shape[0]
    NP, NG, J = layout(N, E)
    EP = NG * GROUP

    def padded(rows, n, value=0):
        out = np.full((n,) + rows.shape[1:], value, rows.dtype)
        out[:rows.shape[0]] = rows
        return out

    def by_tile(edges):
        v = edges.reshape(NG, 2, 2, P, -1)
        return np.ascontiguousarray(v.transpose(0, 3, 2, 1, 4)).reshape(NG, P, TILES, -1)

    src, dst = padded(a["src"], EP), padded(a["dst"], EP, N)
    feat = padded(a["edge_attr_64"], EP).reshape(NG, 2, GROUP // 2, ED)
    vec = by_tile(padded(a["edge_attr_3"], EP))
    w1 = a["L0_gnn_W1"]
    f32 = np.float32
    w1_edges = np.zeros((2, ED, 2, D + 1), f32)
    mlp0, mlp1 = np.zeros((P, 2, HID), f32), np.zeros((2, HID, 2, HID), f32)
    mlp2 = np.zeros((2, HID, 2, D), f32)
    order = [1, 0, 3, 2]
    w3 = a["L1_gnn_mlp_w2"].reshape(HID, 4, MUL)[:, order].reshape(HID, D)
    b3 = a["L1_gnn_mlp_b2"].reshape(4, MUL)[order].reshape(D)
    for half in range(2):
        w1_edges[half, :, half, 0:D] = w1[2 * D:]
        w1_edges[half, :, half, D] = a["L0_gnn_gate_w"][:, 0]
        mlp0[half * NB:(half + 1) * NB, half] = a["L1_gnn_mlp_w0"]
        mlp1[half, :, half] = a["L1_gnn_mlp_w1"]
        mlp2[half, :, half] = w3
    w_up = np.zeros((D, 4, MUL), f32)
    w_up[0:MUL, 0] = a["L1_gnn_W_up0"]
    w_out = np.zeros((8, MUL, D), f32)
    w_out[0, :, 0:MUL] = a["L1_gnn_W_out0"][0:MUL]
    w_out[1, :, 0:MUL] = a["L1_gnn_W_out0"][MUL:]
    for c in range(3):
        w_up[MUL + c::3, 1 + c] = a["L1_gnn_W_up1"]
        w_out[2 + c, :, MUL + c::3] = a["L1_gnn_W_out1"][MUL:]
        w_out[5 + c, :, MUL + c::3] = a["L1_gnn_W_out1"][0:MUL]

    arrays = {
        "x": padded(a["x"], NP),
        "meta": np.concatenate([by_tile(src), by_tile(dst)], axis=2)[..., 0],
        "dst_flat": dst.reshape(1, EP),
        "edge_feat": feat.transpose(0, 1, 3, 2).reshape(NG, P, GROUP // 2),
        "edge_vec": vec.transpose(1, 0, 2, 3).reshape(P, NG * TILES, 3),
        "edge_dist": padded(a["edge_weight"], EP).reshape(P, EP // P),
        "ident": np.eye(P, dtype=f32),
        "w1_nodes": w1[:2 * D].reshape(2, D, D).transpose(1, 0, 2),
        "b1": a["L0_gnn_b1"].reshape(1, D),
        "w1_edges": w1_edges.reshape(P, 2, D + 1),
        "gate_b": a["L0_gnn_gate_b"].reshape(1, 1),
        "ln_g": a["L0_gnn_ln_g"].reshape(1, D),
        "ln_b": a["L0_gnn_ln_b"].reshape(1, D),
        "w2": a["L0_gnn_W2"],
        "b2": a["L0_gnn_b2"].reshape(1, D),
        "w_ih": a["L0_gnn_W_ih"].T,
        "w_hh": a["L0_gnn_W_hh"].T,
        "b_ih": a["L0_gnn_b_ih"].reshape(3, D).T,
        "b_hh": a["L0_gnn_b_hh"].reshape(3, D).T,
        "w_up": w_up.reshape(D, D),
        "mlp0": mlp0.reshape(P, P),
        "mlp1": mlp1.reshape(P, P),
        "mlp2": mlp2.reshape(P, 2 * D),
        "mlp_b0": np.concatenate([a["L1_gnn_mlp_b0"]] * 2).reshape(P, 1),
        "mlp_b1": np.concatenate([a["L1_gnn_mlp_b1"]] * 2).reshape(P, 1),
        "mlp_b2": np.concatenate([b3, b3]).reshape(1, 2 * D),
        "w_out": w_out.reshape(2, P, D).transpose(1, 0, 2),
    }
    arrays = {k: np.ascontiguousarray(v) for k, v in arrays.items()}
    nc = bacc.Bacc("TRN2", target_bir_lowering=False, num_devices=1)
    io = {k: nc.dram_tensor(f"in_{k}", v.shape, mybir.dt.from_np(v.dtype), kind="ExternalInput").ap() for k, v in arrays.items()}
    io["out"] = nc.dram_tensor("out_nodes", (NP, D), F32, kind="ExternalOutput").ap()
    program(nc, io, N, E)
    result = run_bass_kernel_spmd(nc, [{f"in_{k}": v for k, v in arrays.items()}], core_ids=[0])
    return result.results[0]["out_nodes"][:N]
```

```python
import concourse.bass as bass
from concourse import mybir
from contextlib import ExitStack
import math

F32 = mybir.dt.float32
BF16 = mybir.dt.bfloat16
I32 = mybir.dt.int32
ALU = mybir.AluOpType
ACT = mybir.ActivationFunctionType
AX = mybir.AxisListType

P = 128
D = 128
ED = 64
TILES = 4
GROUP = TILES * P
QUAD = 4 * P
SLOTS = 4
UNROLL = 8
BATCH = 4
SUM_LAG = 6
MUL = 32
NB = 8
HID = 64
MSG = 9 * MUL
EPS = 1e-5
SQ3 = 3.0 ** 0.5
SPLITS = 3


def tile_offset(i):
    return (i % 2) * (GROUP // 2) + (i // 2) * P


def reached(step, n):
    return not isinstance(step, int) or step >= n


def layout(N, E):
    NP = -(-(N + 1 + P) // QUAD) * QUAD
    NG = -(-E // GROUP)
    NG = -(-NG // UNROLL) * UNROLL
    windows = N // P + 1
    J = -(-(NG * windows + UNROLL) // P)
    return NP, NG, J


def program(nc, io, N, E):
    NP, NG, J = layout(N, E)
    dram = {}

    def scratch(name, shape, dt):
        dram[name] = nc.dram_tensor(name, shape, dt).ap()

    scratch("a_table", (NP, D + 1), F32)
    scratch("b_table", (NP, SPLITS * D), BF16)
    scratch("u_table", (NP, D), F32)
    scratch("y_edges", (P, NG * TILES * 3), F32)
    scratch("emb_edges", (NB, NG * GROUP), F32)
    scratch("group_lo", (1, NG), I32)
    scratch("group_extra", (1, NG), I32)
    scratch("group_end", (1, NG), F32)
    scratch("group_step", (1, NG), F32)
    scratch("item_group", (1, P * J), I32)
    scratch("item_base", (1, P * J), I32)
    scratch("item_base_f", (1, P * J), F32)
    scratch("sum_base", (1, P * J + UNROLL), I32)

    with ExitStack() as ctx:
        def sb(name, shape, dt):
            return ctx.enter_context(nc.sbuf_tensor(name, shape, dt))

        keep = {
            "agg": sb("agg", [P, 2, NP], F32),
            "nodes": sb("nodes", [P, NP], F32),
            "iota": sb("iota", [P, P], F32),
            "ident": sb("ident", [P, P], F32),
            "eps": sb("eps", [P, 1], F32),
            "meta_in": [ctx.enter_context(nc.semaphore(f"meta_in{u}")) for u in range(UNROLL)],
            "edge_in": [ctx.enter_context(nc.semaphore(f"edge_in{u}")) for u in range(UNROLL)],
            "gathered": [ctx.enter_context(nc.semaphore(f"gathered{u}")) for u in range(UNROLL)],
            "base_in": [ctx.enter_context(nc.semaphore(f"base_in{b}")) for b in range(UNROLL // BATCH)],
            "started": ctx.enter_context(nc.semaphore("started")),
            "ctl": sb("ctl", [1, 4], I32),
        }
        node_tables(nc, io, dram, keep, NP, NG, J)
        gated_edges(nc, io, dram, keep, NP, NG, J)
        gru_nodes(nc, io, dram, keep, NP)
        tensor_edges(nc, io, dram, keep, NP, NG, J)
        output_nodes(nc, io, dram, keep, NP)


def node_tables(nc, io, dram, keep, NP, NG, J):
    agg, nodes, iota, ident, eps, ctl = (keep[k] for k in ("agg", "nodes", "iota", "ident", "eps", "ctl"))
    PG = NG // BATCH
    C = NG * GROUP // P
    NQ = NP // QUAD
    LAG, PEEL = 6, 12
    with ExitStack() as ctx:
        def sb(name, shape, dt):
            return ctx.enter_context(nc.sbuf_tensor("tables_" + name, shape, dt))

        def pb(name):
            return ctx.enter_context(nc.psum_tensor("tables_" + name, [P, 4, D], F32))

        def sem(name):
            return ctx.enter_context(nc.semaphore("tables_" + name))

        wab = sb("wab", [P, 2, D], F32)
        b1 = sb("b1", [P, 1, D], F32)
        gate_b = sb("gate_b", [P, 1], F32)
        means = sb("means", [P, 3], F32)
        x = sb("x", [P, SLOTS, 4, D], F32)
        stats = sb("stats", [P, 2, 4, 6], F32)
        mv = sb("mv", [P, 2, 4, 2], F32)
        rstd = sb("rstd", [P, 2, 4], F32)
        normed = sb("normed", [P, 2, 4, D], F32)
        hT = sb("hT", [P, 2, QUAD], F32)
        a_out = sb("a_out", [P, SLOTS, 4, D + 1], F32)
        rest = sb("rest", [P, SLOTS, 4, D], F32)
        b_out = sb("b_out", [P, SLOTS, 4, SPLITS, D], BF16)
        assert BATCH * GROUP <= NP
        dst_rows = nodes[0:PG, NP - BATCH * GROUP:NP].bitcast(I32).rearrange("p (q e) -> p q e", q=BATCH)
        lo4 = sb("lo4", [PG, BATCH], I32)
        hi4 = sb("hi4", [PG, BATCH], I32)
        span4 = sb("span4", [PG, BATCH], I32)
        extra4 = sb("extra4", [PG, BATCH], I32)
        lo_row = sb("lo_row", [1, NG], I32)
        extra_row = sb("extra_row", [1, NG], I32)
        group_row = sb("group_row", [1, NG], I32)
        work_row = sb("work_row", [1, NG], F32)
        one = sb("one", [1, 1], F32)
        end_row = sb("end_row", [1, NG], F32)
        step_row = sb("step_row", [1, NG], F32)
        total = sb("total", [1, 2], I32)
        first = sb("first", [1, SUM_LAG], I32)
        lo0 = sb("lo0", [P, 1], I32)
        assert 6 * J <= SLOTS * QUAD and 2 * J + 2 * NG <= SLOTS * QUAD
        x_place, rest_place = (t[:].rearrange("p s t d -> p (s t d)") for t in (x, rest))
        slot, group_of, base_of, passed, live, base_f = (x_place[:, k * J:(k + 1) * J] for k in range(6))
        group_int, base_int = (rest_place[:, k * J:(k + 1) * J].bitcast(I32) for k in range(2))
        end_all, step_all = (rest_place[:, 2 * J + k * NG:2 * J + (k + 1) * NG] for k in range(2))
        assert 8 * C <= NP
        vec = agg[:, 1, 0:3 * C].rearrange("p (c k) -> p c k", k=3)
        norm, dist, far = (agg[:, 1, i * C:(i + 1) * C] for i in range(3, 6))
        emb = agg[:, 1, 6 * C:8 * C].rearrange("p (s c) -> p s c", s=2)
        centers = sb("centers", [P, NB], F32)
        log_height = sb("log_height", [P, 1], F32)
        hT_ps = [pb(f"hT_ps{i}") for i in range(2)]
        a_ps = [pb(f"a_ps{i}") for i in range(2)]
        b_ps = [pb(f"b_ps{i}") for i in range(2)]

        w_in, centred, chain, zeroed = sem("w_in"), sem("centred"), sem("chain"), sem("zeroed")
        x_in = [sem(f"x_in{s}") for s in range(SLOTS)]
        stored = [sem(f"stored{s}") for s in range(SLOTS)]
        joining = sem("joining")
        measured, moments, scaled, normed_s, turned, hT_ready = (sem(n) for n in (
            "measured", "moments", "scaled", "normed", "turned", "hT_ready"))
        kept, multiplied, a_ready = sem("kept"), sem("multiplied"), sem("a_ready")
        part0, rest0, part1, part2 = (sem(n) for n in ("part0", "rest0", "part1", "part2"))
        dst_in, edges_in = sem("dst_in"), sem("edges_in")
        spans_out, spans_in, steps_out, steps_in = (sem(n) for n in ("spans_out", "spans_in", "steps_out", "steps_in"))
        spans, listing, listed, items, iotas = (sem(n) for n in ("spans", "listing", "listed", "items", "iotas"))
        numbered, cleared = sem("numbered"), sem("cleared")
        squared, summed, rooted, inverted, unit = (sem(n) for n in ("squared", "summed", "rooted", "inverted", "unit"))
        clipped, shifted, bell = sem("clipped"), sem("shifted"), sem("bell")
        items_out, y_out = sem("items_out"), sem("y_out")
        emb_out = [sem("emb_out0"), sem("emb_out1")]
        block = ctx.enter_context(nc.Block())

        def after(q, n):
            return isinstance(q, int) and q == n

        @block.sync
        def _(sp):
            sp.dma_start(dst_rows, io["dst_flat"].rearrange("a (p q e) -> (a p) q e", p=PG, q=BATCH)).then_inc(dst_in, 16)
            sp.dma_start(wab[:], io["w1_nodes"]).then_inc(w_in, 16)
            sp.dma_start(b1[:, 0, :], io["b1"].broadcast_to([P, D])).then_inc(w_in, 16)
            sp.dma_start(gate_b[:], io["gate_b"].broadcast_to([P, 1])).then_inc(w_in, 16)
            sp.dma_start(ident[:], io["ident"]).then_inc(w_in, 16)

            def step(q, s):
                if has_quad(q, NQ):
                    if reached(q, SLOTS):
                        sp.wait_ge(normed_s, q - SLOTS + 1)
                    sp.dma_start(x[:, s], quad_rows(io["x"], q)).then_inc(x_in[s], 16)
                if has_quad(q - LAG, NQ):
                    r, z = q - LAG, (s - LAG) % SLOTS
                    sp.wait_ge(a_ready, r + 1)
                    sp.dma_start(quad_rows(dram["a_table"], r), a_out[:, z]).then_inc(stored[z], 16)
                    sp.wait_ge(part2, r + 1)
                    sp.dma_start(quad_rows(dram["b_table"], r), b_out[:, z].rearrange("p t k d -> p t (k d)")).then_inc(stored[z], 16)
                if after(q, 3):
                    sp.wait_ge(spans, 1)
                    sp.dma_start(dram["group_lo"].rearrange("a (p q) -> (a p) q", p=PG), lo4[:]).then_inc(spans_out, 16)
                    sp.dma_start(dram["group_extra"].rearrange("a (p q) -> (a p) q", p=PG), extra4[:]).then_inc(spans_out, 16)
                    sp.wait_ge(spans_out, 32)
                    sp.dma_start(lo_row[:], dram["group_lo"]).then_inc(spans_in, 16)
                    sp.dma_start(extra_row[:], dram["group_extra"]).then_inc(spans_in, 16)
                    sp.dma_start(lo0[:], dram["group_lo"][:, 0:1].broadcast_to([P, 1])).then_inc(spans_in, 16)
                if after(q, 6):
                    sp.wait_ge(listed, 1)
                    sp.dma_start(dram["group_end"], end_row[:]).then_inc(steps_out, 16)
                    sp.dma_start(dram["group_step"], step_row[:]).then_inc(steps_out, 16)
                if after(q, 8):
                    sp.wait_ge(iotas, 1)
                    sp.wait_ge(steps_out, 32)
                    several = sp.value_load(ctl[0:1, 1:2], min_val=0, max_val=1)
                    with sp.If(several == 0):
                        sp.dma_start(dram["item_group"][:, 0:NG], group_row[:]).then_inc(items_out, 16)
                        sp.dma_start(dram["item_base"][:, 0:NG], lo_row[:]).then_inc(items_out, 16)
                        sp.dma_start(dram["sum_base"][:, SUM_LAG:SUM_LAG + NG], lo_row[:]).then_inc(items_out, 16)
                        sp.dma_start(dram["item_base_f"][:, 0:NG], work_row[:]).then_inc(items_out, 16)
                    sp.dma_start(dram["sum_base"][:, 0:SUM_LAG], first[:]).then_inc(items_out, 16)

            over_quads(sp, step, NQ, LAG, PEEL)
            several = sp.value_load(ctl[0:1, 1:2], min_val=0, max_val=1)
            with sp.If(several == 1):
                sp.dma_start(end_all, dram["group_end"].broadcast_to([P, NG])).then_inc(steps_in, 16)
                sp.dma_start(step_all, dram["group_step"].broadcast_to([P, NG])).then_inc(steps_in, 16)
                sp.wait_ge(items, 1)
                sp.dma_start(dram["item_group"].rearrange("a (p j) -> (a p) j", p=P), group_int).then_inc(items_out, 16)
                sp.dma_start(dram["item_base"].rearrange("a (p j) -> (a p) j", p=P), base_int).then_inc(items_out, 16)
                sp.dma_start(dram["sum_base"][:, SUM_LAG:SUM_LAG + P * J].rearrange("a (p j) -> (a p) j", p=P),
                             base_int).then_inc(items_out, 16)
                sp.dma_start(dram["item_base_f"].rearrange("a (p j) -> (a p) j", p=P), base_f).then_inc(items_out, 16)
            sp.wait_ge(items_out, 16 * 5)
            sp.wait_ge(y_out, 16)
            for out in emb_out:
                sp.wait_ge(out, 16 * NB // 2)
            for s in range(SLOTS):
                if NQ > s:
                    sp.wait_ge(stored[s], 32 * ((NQ - s - 1) // SLOTS + 1))

        @block.vector
        def _(dve):
            done = [0]

            def then(instruction):
                done[0] += 1
                instruction.then_inc(listing, 1)
                dve.wait_ge(listing, done[0])

            nc.vector.memset(eps[:], EPS)
            nc.vector.memset(log_height[:], 0.5 * math.log(NB))
            nc.vector.memset(first[:], 0)
            nc.vector.memset(one[:], 1.0)
            dve.wait_ge(dst_in, 16)
            nc.vector.tensor_reduce(lo4[:], dst_rows, AX.X, ALU.min)
            then(nc.vector.tensor_reduce(hi4[:], dst_rows, AX.X, ALU.max))
            then(nc.vector.tensor_tensor(span4[:], hi4[:], lo4[:], ALU.subtract))
            nc.vector.tensor_scalar(extra4[:], span4[:], P.bit_length() - 1, None, ALU.arith_shift_right).then_inc(spans, 1)
            dve.wait_ge(w_in, 64)
            nc.vector.tensor_reduce(means[:, 0:2], wab[:], AX.X, ALU.add)
            nc.vector.tensor_reduce(means[:, 2:3], b1[:], AX.X, ALU.add).then_inc(chain, 1)
            dve.wait_ge(chain, 1)
            nc.vector.tensor_scalar(means[:], means[:], 1.0 / D, None, ALU.mult).then_inc(chain, 1)
            dve.wait_ge(chain, 2)
            for k in range(2):
                nc.vector.tensor_scalar(wab[:, k, :], wab[:, k, :], means[:, k:k + 1], None, ALU.subtract)
            nc.vector.tensor_scalar(b1[:, 0, :], b1[:, 0, :], means[:, 2:3], None, ALU.subtract)
            for s in range(SLOTS):
                for t in range(4):
                    last = nc.vector.tensor_copy(a_out[:, s, t, D:D + 1], gate_b[:])
            last.then_inc(centred, 1)
            dve.wait_ge(centred, 1)

            def step(q, s):
                if has_quad(q - 4, NQ):
                    r, z, v = q - 4, s, s % 2
                    dve.wait_ge(part0, r + 1)
                    if reached(r, SLOTS):
                        dve.wait_ge(part2, r - SLOTS + 1)
                    nc.vector.tensor_tensor(rest[:, z], b_ps[v][:], b_out[:, z, :, 0, :], ALU.subtract).then_inc(rest0, 1)
                if has_quad(q - 3, NQ):
                    r, z, v = q - 3, (s - 3) % SLOTS, (s - 3) % 2
                    dve.wait_ge(multiplied, r + 1)
                    if reached(r, SLOTS):
                        dve.wait_ge(stored[z], 32 * (quad_use(r, z) - 1))
                    nc.vector.tensor_tensor(a_out[:, z, :, 0:D], a_ps[v][:], b1[:].broadcast_to([P, 4, D]),
                                            ALU.add).then_inc(a_ready, 1)
                if has_quad(q, NQ):
                    v = s % 2
                    dve.wait_ge(x_in[s], 16 * quad_use(q, s))
                    if reached(q, 2):
                        dve.wait_ge(moments, q - 1)
                    for t in range(4):
                        last = nc.vector.bn_stats(stats[:, v, t, :], x[:, s, t, :])
                    last.then_inc(measured, 1)
                    dve.wait_ge(measured, q + 1)
                    if reached(q, 2):
                        dve.wait_ge(normed_s, q - 1)
                    dve.sem_inc(joining, 1)
                    for t in range(4):
                        last = nc.vector.bn_aggr(mv[:, v, t, :], stats[:, v, t, :])
                    last.then_inc(moments, 1)
                if has_quad(q - 1, NQ):
                    r, z, v = q - 1, (s - 1) % SLOTS, (s - 1) % 2
                    dve.wait_ge(scaled, 2 * r + 2)
                    if reached(r, 2):
                        dve.wait_ge(turned, r - 1)
                    for t in range(4):
                        last = nc.vector.tensor_scalar(normed[:, v, t, :], x[:, z, t, :], mv[:, v, t, 0:1], rstd[:, v, t:t + 1],
                                                       ALU.subtract, ALU.mult)
                    last.then_inc(normed_s, 1)
                if after(q, 3):
                    dve.wait_ge(edges_in, 32)
                    nc.vector.tensor_scalar(far, dist, 1.0, 4.0, ALU.is_gt, ALU.mult).then_inc(clipped, 1)
                    dve.wait_ge(clipped, 1)
                    nc.vector.tensor_scalar(dist, dist, 0.0, 1.0, ALU.max, ALU.min).then_inc(clipped, 1)
                    dve.wait_ge(clipped, 2)
                    nc.vector.tensor_tensor(dist, dist, far, ALU.add).then_inc(clipped, 1)
                if after(q, 2):
                    dve.wait_ge(spans_in, 48)
                    then(nc.vector.tensor_scalar(work_row[:], extra_row[:], 1.0, None, ALU.add))
                    then(nc.vector.tensor_tensor_scan(end_row[:], one[:].broadcast_to([1, NG]), work_row[:], 0.0, ALU.mult, ALU.add))
                    then(nc.vector.tensor_tensor(work_row[:], end_row[:], work_row[:], ALU.subtract))
                    then(nc.vector.scalar_tensor_tensor(out=work_row[:], in0=work_row[:], scalar=-float(P), in1=lo_row[:],
                                                        op0=ALU.mult, op1=ALU.add))
                    nc.vector.memset(step_row[0:1, NG - 1:NG], 0.0)
                    nc.vector.tensor_tensor(step_row[0:1, 0:NG - 1], work_row[0:1, 1:NG], work_row[0:1, 0:NG - 1], ALU.subtract)
                    then(nc.vector.tensor_scalar(total[0:1, 0:1], end_row[0:1, NG - 1:NG], -1.0, None, ALU.add))
                    nc.vector.tensor_copy(work_row[:], lo_row[:])
                    nc.vector.tensor_scalar(ctl[0:1, 0:1], total[0:1, 0:1], UNROLL.bit_length() - 1, None, ALU.arith_shift_right)
                    then(nc.vector.tensor_scalar(ctl[0:1, 1:2], end_row[0:1, NG - 1:NG], float(NG), None, ALU.is_gt))
                    nc.vector.memset(ctl[0:1, 2:4], 0).then_inc(listed, 1)
                if after(q, 6):
                    dve.wait_ge(rooted, 1)
                    nc.vector.tensor_scalar(norm, norm, 1e-12, 1.0 / SQ3, ALU.add, ALU.mult).then_inc(inverted, 1)
                    dve.wait_ge(inverted, 1)
                    nc.vector.reciprocal(norm, norm).then_inc(inverted, 1)

            over_quads(dve, step, NQ, LAG, PEEL)
            for out in emb_out:
                dve.wait_ge(out, 16 * NB // 2)
            nc.vector.memset(agg[:, 1, 4 * C:NP], 0.0).then_inc(cleared, 1)
            dve.wait_ge(cleared, 1)
            several = dve.value_load(ctl[0:1, 1:2], min_val=0, max_val=1)
            with dve.If(several == 1):
                dve.wait_ge(steps_in, 32)
                dve.wait_ge(numbered, 1)
                nc.vector.memset(group_of, 0.0)
                nc.vector.tensor_scalar(base_of, slot, float(P), lo0[:, 0:1], ALU.mult, ALU.add).then_inc(listing, 1)
                dve.wait_ge(listing, done[0] + 1)
                with dve.Fori(0, NG) as g:
                    nc.vector.tensor_scalar(passed, slot, end_all[:, bass.ds(g, 1)], step_all[:, bass.ds(g, 1)],
                                            ALU.is_ge, ALU.mult)
                    nc.vector.scalar_tensor_tensor(out=group_of, in0=slot, scalar=end_all[:, bass.ds(g, 1)],
                                                   in1=group_of, op0=ALU.is_ge, op1=ALU.add).then_inc(listing, 1)
                    dve.wait_ge(listing, 2 * g + done[0] + 2)
                    nc.vector.tensor_tensor(base_of, base_of, passed, ALU.add).then_inc(listing, 1)
                    dve.wait_ge(listing, 2 * g + done[0] + 3)
                summed_all = done[0] + 1 + 2 * NG
                nc.vector.tensor_scalar(live, slot, end_all[:, NG - 1:NG], None, ALU.is_lt)
                nc.vector.tensor_scalar(base_of, base_of, -float(NP - P), None, ALU.add).then_inc(listing, 1)
                dve.wait_ge(listing, summed_all + 1)
                nc.vector.tensor_tensor(group_int, group_of, live, ALU.mult)
                nc.vector.tensor_tensor(base_of, base_of, live, ALU.mult).then_inc(listing, 1)
                dve.wait_ge(listing, summed_all + 2)
                nc.vector.tensor_scalar(base_int, base_of, float(NP - P), None, ALU.add)
                nc.vector.tensor_scalar(base_f, base_of, float(NP - P), None, ALU.add).then_inc(listing, 1)
                dve.wait_ge(listing, summed_all + 3)
                dve.sem_inc(items, 1)

        @block.scalar
        def _(act):
            nc.scalar.preload_act_table_set("natural_log_exp_and_others")
            act.wait_ge(spans, 1)

            def step(q, s):
                if has_quad(q - 3, NQ):
                    r, z, v = q - 3, (s - 3) % SLOTS, (s - 3) % 2
                    act.wait_ge(multiplied, r + 1)
                    if reached(r, SLOTS):
                        act.wait_ge(stored[z], 32 * (quad_use(r, z) - 1))
                    nc.scalar.copy(b_out[:, z, :, 0, :], b_ps[v][:]).then_inc(part0, 1)
                if has_quad(q - 5, NQ):
                    r, z = q - 5, (s - 5) % SLOTS
                    act.wait_ge(rest0, r + 1)
                    nc.scalar.copy(b_out[:, z, :, 1, :], rest[:, z]).then_inc(part1, 1)
                if has_quad(q, NQ):
                    v = s % 2
                    act.wait_ge(moments, q + 1)
                    nc.scalar.activation(rstd[:, v], mv[:, v, :, 1], ACT.Ln, bias=keep["eps"][:]).then_inc(scaled, 1)
                    act.wait_ge(scaled, 2 * q + 1)
                    nc.scalar.activation(rstd[:, v], rstd[:, v], ACT.Exp, scale=-0.5).then_inc(scaled, 1)
                if has_quad(q - 1, NQ):
                    r, v = q - 1, (s - 1) % 2
                    act.wait_ge(turned, r + 1)
                    if reached(r, 2):
                        act.wait_ge(multiplied, r - 1)
                    nc.scalar.activation(hT[:, v], hT_ps[v][:].rearrange("p t d -> p (t d)"), ACT.Relu).then_inc(hT_ready, 1)
                    act.wait_ge(hT_ready, r + 1)
                    nc.scalar.copy(nodes[:, bass.ds(r * QUAD, QUAD)], hT[:, v]).then_inc(kept, 1)
                if after(q, 0):
                    act.dma_start(dist, io["edge_dist"]).then_inc(edges_in, 16)
                    act.dma_start(vec, io["edge_vec"]).then_inc(edges_in, 16)
                if after(q, 2):
                    act.wait_ge(edges_in, 32)
                    for k, square in enumerate((emb[:, 0, :], emb[:, 1, :], norm)):
                        last = nc.scalar.activation(square, vec[:, :, k], ACT.Square)
                    last.then_inc(squared, 1)
                if after(q, 4):
                    act.wait_ge(summed, 2)
                    nc.scalar.activation(norm, norm, ACT.Sqrt).then_inc(rooted, 1)
                    nc.scalar.preload_act_table_set("natural_log_exp_and_others")
                    act.wait_ge(clipped, 3)
                    act.wait_ge(iotas, 1)
                for b in range(NB):
                    if after(q, 4 + b):
                        if b >= 2:
                            act.wait_ge(emb_out[b % 2], 16 * (b // 2))
                        nc.scalar.activation(emb[:, b % 2, :], dist, ACT.Square, bias=centers[:, b:b + 1],
                                             scale=float(NB - 1)).then_inc(shifted, 1)
                        act.wait_ge(shifted, b + 1)
                        nc.scalar.activation(emb[:, b % 2, :], emb[:, b % 2, :], ACT.Exp, bias=log_height[:], scale=-0.5).then_inc(bell, 1)
                        act.wait_ge(bell, b + 1)
                        act.dma_start(dram["emb_edges"][b:b + 1, :].rearrange("a (p c) -> (a p) c", p=P),
                                      emb[:, b % 2, :]).then_inc(emb_out[b % 2], 16)

            over_quads(act, step, NQ, LAG, PEEL)

        @block.gpsimd
        def _(pool):
            nc.gpsimd.iota(group_row[:], [[1, NG]], base=0, channel_multiplier=0)
            nc.gpsimd.iota(centers[:], [[-1, NB]], base=0, channel_multiplier=0, allow_small_or_imprecise_dtypes=True)
            nc.gpsimd.iota(iota[:], [[1, P]], base=0, channel_multiplier=0,
                           allow_small_or_imprecise_dtypes=True).then_inc(iotas, 1)
            nc.gpsimd.memset(agg[:, 0, :], 0.0).then_inc(zeroed, 1)

            def step(q, s):
                if has_quad(q - 5, NQ):
                    r, z = q - 5, (s - 5) % SLOTS
                    pool.wait_ge(part1, r + 1)
                    nc.gpsimd.tensor_tensor(b_out[:, z, :, 2, :], rest[:, z], b_out[:, z, :, 1, :], ALU.subtract).then_inc(part2, 1)
                if after(q, 2):
                    pool.wait_ge(squared, 1)
                    nc.gpsimd.tensor_tensor(norm, norm, emb[:, 0, :], ALU.add).then_inc(summed, 1)
                    pool.wait_ge(summed, 1)
                    nc.gpsimd.tensor_tensor(norm, norm, emb[:, 1, :], ALU.add).then_inc(summed, 1)
                if after(q, 7):
                    pool.wait_ge(inverted, 2)
                    nc.gpsimd.tensor_tensor(vec, vec, norm.unsqueeze(2).broadcast_to([P, C, 3]), ALU.mult).then_inc(unit, 1)
                    pool.wait_ge(unit, 1)
                    pool.dma_start(dram["y_edges"], vec.rearrange("p c k -> p (c k)")).then_inc(y_out, 16)
                if after(q, PEEL - 1):
                    pool.wait_ge(y_out, 16)
                    nc.gpsimd.memset(agg[:, 1, 0:4 * C], 0.0).then_inc(zeroed, 1)

            over_quads(pool, step, NQ, LAG, PEEL)
            pool.wait_ge(normed_s, NQ)
            nc.gpsimd.iota(slot, [[1, J]], base=0, channel_multiplier=J, allow_small_or_imprecise_dtypes=True).then_inc(numbered, 1)
            pool.wait_ge(numbered, 1)
            pool.wait_ge(zeroed, 2)

        @block.tensor
        def _(pe):
            def step(q, s):
                if has_quad(q - 2, NQ):
                    r, v = q - 2, s % 2
                    pe.wait_ge(hT_ready, r + 1)
                    if reached(r, 2):
                        pe.wait_ge(a_ready, r - 1)
                        pe.wait_ge(rest0, r - 1)
                    for k, out in enumerate((a_ps[v], b_ps[v])):
                        for t in range(4):
                            last = nc.tensor.matmul(out[:, t, :], hT[:, v, t * P:(t + 1) * P], wab[:, k, :], start=True, stop=True)
                    last.then_inc(multiplied, 1)
                if has_quad(q - 1, NQ):
                    r, v = q - 1, (s - 1) % 2
                    pe.wait_ge(normed_s, r + 1)
                    if reached(r, 2):
                        pe.wait_ge(hT_ready, r - 1)
                    for t in range(4):
                        last = nc.tensor.transpose(hT_ps[v][:, t, :], normed[:, v, t, :], ident[:])
                    last.then_inc(turned, 1)

            pe.wait_ge(centred, 1)
            over_quads(pe, step, NQ, LAG, PEEL)


def over_items(eng, step, passes, lag):
    for u in range(UNROLL):
        step(u, u, -1)
    with eng.Fori(1, passes) as k:
        for u in range(UNROLL):
            step(k * UNROLL + u, u, -1)
    for u in range(lag):
        step(passes * UNROLL + u, u % UNROLL, u)


def load_pass(nc, engine, table, item, count, highest):
    return nc.values_load_multi_w_load_instructions(
        table[0:1, bass.ds(item, count)], engines=(engine,), min_val=0, max_val=highest,
        skip_runtime_bounds_check_because="node_tables() keeps the list of items within these bounds")[1]


def over_quads(eng, step, NQ, lag, peel):
    first, end = peel // SLOTS, NQ // SLOTS
    for q in range(min(peel, NQ + lag)):
        step(q, q % SLOTS)
    if end > first:
        with eng.Fori(first, end) as k:
            for s in range(SLOTS):
                step(k * SLOTS + s, s)
    for q in range(max(peel, end * SLOTS), NQ + lag):
        step(q, q % SLOTS)


def quad_use(q, s):
    return q // SLOTS + 1 if isinstance(q, int) else (q - s) // SLOTS + 1


def has_quad(q, NQ):
    return not isinstance(q, int) or 0 <= q < NQ


def quad_rows(table, q):
    return table[bass.ds(q * QUAD, QUAD), :].rearrange("(t p) d -> p t d", p=P)


def stage(item, drained, lag):
    return drained < lag and reached(item, lag)


def gated_edges(nc, io, dram, keep, NP, NG, J):
    agg, iota, ident, ctl = keep["agg"], keep["iota"], keep["ident"], keep["ctl"]
    PRE = D + 1
    MIN_PASSES, MAX_PASSES = NG // UNROLL, P * J // UNROLL
    with ExitStack() as ctx:
        def sb(name, shape, dt):
            return ctx.enter_context(nc.sbuf_tensor("gated_" + name, shape, dt))

        def pb(name, shape):
            return ctx.enter_context(nc.psum_tensor("gated_" + name, shape, F32))

        def sem(name):
            return ctx.enter_context(nc.semaphore("gated_" + name))

        w_edge = sb("w_edge", [P, 2, PRE], F32)
        w_mean = sb("w_mean", [P, 2], F32)
        ln_g = sb("ln_g", [P, D], F32)
        ln_b = sb("ln_b", [P, 1, D], F32)
        meta = sb("meta", [P, UNROLL, 2 * TILES], I32)
        base = sb("base", [P, UNROLL], F32)
        feat = sb("feat", [P, UNROLL, GROUP // 2], F32)
        b_win = sb("b_win", [P, BATCH, SPLITS * D], BF16)
        gath = sb("gath", [P, UNROLL, TILES, PRE], F32)
        by_node = sb("by_node", [P, 2, GROUP], BF16)
        by_edge = sb("by_edge", [P, UNROLL, TILES, P], F32)
        pre = sb("pre", [P, 2, TILES, PRE], F32)
        junk = sb("junk", [P, D], F32)
        ss = sb("ss", [P, TILES], F32)
        rstd = sb("rstd", [P, 2, TILES], F32)
        gexp = sb("gexp", [P, 2, TILES], F32)
        gate = sb("gate", [P, 2, TILES], F32)
        msg = sb("msg", [P, 2, TILES, D], F32)
        turned_ps = [pb(f"turned_ps{i}", [P, GROUP]) for i in range(2)]
        pre_ps = [pb(f"pre_ps{i}", [P, 2, 512]) for i in range(2)]
        agg_ps = [pb(f"agg_ps{i}", [P, 512]) for i in range(2)]

        w_in, centred, chain = sem("w_in"), sem("centred"), sem("chain")
        meta_in, edge_in, gathered, base_in, started = (keep[k] for k in ("meta_in", "edge_in", "gathered", "base_in", "started"))
        by_edge_built, turned, by_node_built = sem("by_edge_built"), sem("turned"), sem("by_node_built")
        pre_mm, pre_summed, squares, logs, measured = (sem(n) for n in ("pre_mm", "pre_summed", "squares", "logs", "measured"))
        scaled, normed_s, gated, msg_ready, agg_mm, acc_done = (sem(n) for n in ("scaled", "normed", "gated", "msg_ready", "agg_mm", "acc_done"))
        block = ctx.enter_context(nc.Block())

        def use(item, u):
            return item // UNROLL + 1 if isinstance(item, int) else (item - u) // UNROLL + 1

        @block.sync
        def _(sp):
            passes = sp.value_load(ctl[0:1, 0:1], min_val=MIN_PASSES - 1, max_val=MAX_PASSES - 1) + 1

            loaded = {}

            def step(w, u, drained):
                if u == 0:
                    loaded["group"] = load_pass(nc, mybir.EngineType.SP, dram["item_group"], w, UNROLL, NG - 1)
                    loaded["base"] = load_pass(nc, mybir.EngineType.SP, dram["item_base"], w, UNROLL, NP - P)
                g, first = loaded["group"][u], loaded["base"][u]
                if u % BATCH == 0:
                    if reached(w, UNROLL):
                        sp.wait_ge(by_edge_built, w - UNROLL + BATCH)
                    sp.dma_start(base[:, u:u + BATCH],
                                 dram["item_base_f"][0:1, bass.ds(w, BATCH)].broadcast_to([P, BATCH])).then_inc(base_in[u // BATCH], 16)
                if reached(w, UNROLL):
                    sp.wait_ge(pre_summed, w - UNROLL + 1)
                sp.dma_start(meta[:, u], io["meta"][bass.ds(g, 1)].rearrange("a p k -> (a p) k")).then_inc(meta_in[u], 16)
                sp.dma_start(feat[:, u], io["edge_feat"][bass.ds(g, 1)].rearrange("a p k -> (a p) k")).then_inc(edge_in[u], 16)
                if reached(w, BATCH):
                    sp.wait_ge(pre_mm, w - BATCH + 1)
                sp.dma_start(b_win[:, u % BATCH], dram["b_table"][bass.ds(first, P), :]).then_inc(edge_in[u], 16)

            over_items(sp, step, passes, 0)

        @block.gpsimd
        def _(pool):
            passes = pool.value_load(ctl[0:1, 0:1], min_val=MIN_PASSES - 1, max_val=MAX_PASSES - 1) + 1

            def step(w, u, drained):
                pool.wait_ge(meta_in[u], 16 * use(w, u))
                if reached(w, UNROLL):
                    pool.wait_ge(pre_summed, w - UNROLL + 1)
                pool.sem_inc(started, 1)
                for i in range(TILES):
                    nc.gpsimd.indirect_dma_start(
                        gath[:, u, i, :], None, dram["a_table"],
                        bass.IndirectOffsetOnAxis(ap=meta[:, u, i:i + 1], axis=0)).then_inc(gathered[u], 16)

            over_items(pool, step, passes, 0)

        @block.tensor
        def _(pe):
            passes = pe.value_load(ctl[0:1, 0:1], min_val=MIN_PASSES - 1, max_val=MAX_PASSES - 1) + 1
            pe.wait_ge(centred, 1)

            def step(w, u, drained):
                if stage(w, drained, 1):
                    r, v, z = w - 1, (u - 1) % 2, (u - 1) % UNROLL
                    pe.wait_ge(by_edge_built, r + 1)
                    if reached(r, 2):
                        pe.wait_ge(by_node_built, r - 1)
                    for i in range(TILES):
                        last = nc.tensor.transpose(turned_ps[v][:, i * P:(i + 1) * P], by_edge[:, z, i, :], ident[:])
                    last.then_inc(turned, 1)
                if stage(w, drained, 5):
                    r, v, z = w - 5, (u - 5) % 2, (u - 5) % UNROLL
                    pe.wait_ge(msg_ready, r + 1)
                    if reached(r, 2):
                        pe.wait_ge(acc_done, r - 1)
                    for i in range(TILES):
                        nc.tensor.matmul(agg_ps[v][:, 0:P], msg[:, v, i, :], by_edge[:, z, i, :],
                                         start=(i == 0), stop=(i == TILES - 1))
                    for i in range(TILES):
                        last = nc.tensor.matmul(agg_ps[v][:, P:2 * P], gate[:, v, i:i + 1].broadcast_to([P, P]), by_edge[:, z, i, :],
                                                start=(i == 0), stop=(i == TILES - 1))
                    last.then_inc(agg_mm, 1)
                if stage(w, drained, 2):
                    r, v, z = w - 2, u % 2, (u - 2) % UNROLL
                    pe.wait_ge(edge_in[z], 32 * use(r, z))
                    if reached(r, 2):
                        pe.wait_ge(pre_summed, r - 1)
                    for t in range(2):
                        nc.tensor.matmul(pre_ps[v][:, t, 0:2 * PRE], feat[:, z, t * P:(t + 1) * P],
                                         w_edge[:].rearrange("p h d -> p (h d)"), start=True, stop=False)
                        if t == 0:
                            pe.wait_ge(by_node_built, r + 1)
                        for half in range(2):
                            i = 2 * t + half
                            for k in range(SPLITS):
                                last = nc.tensor.matmul(pre_ps[v][:, t, half * PRE:half * PRE + D],
                                                        by_node[:, v, i * P:(i + 1) * P], b_win[:, z % BATCH, k * D:(k + 1) * D],
                                                        start=False, stop=(half == 1 and k == SPLITS - 1))
                    last.then_inc(pre_mm, 1)

            over_items(pe, step, passes, SUM_LAG)

        @block.vector
        def _(dve):
            passes = dve.value_load(ctl[0:1, 0:1], min_val=MIN_PASSES - 1, max_val=MAX_PASSES - 1) + 1
            dve.wait_ge(w_in, 48)
            nc.vector.tensor_reduce(w_mean[:], w_edge[:, :, 0:D], AX.X, ALU.add).then_inc(chain, 1)
            dve.wait_ge(chain, 1)
            nc.vector.tensor_scalar(w_mean[:], w_mean[:], 1.0 / D, None, ALU.mult).then_inc(chain, 1)
            dve.wait_ge(chain, 2)
            for half in range(2):
                last = nc.vector.tensor_scalar(w_edge[:, half, 0:D], w_edge[:, half, 0:D], w_mean[:, half:half + 1],
                                               None, ALU.subtract)
            last.then_inc(centred, 1)
            loaded = {}

            def step(w, u, drained):
                if u == 0:
                    loaded["first"] = load_pass(nc, mybir.EngineType.DVE, dram["sum_base"], w,
                                                UNROLL if drained < 0 else SUM_LAG, NP - P)
                if stage(w, drained, 3):
                    r, v, z = w - 3, (u - 3) % 2, (u - 3) % UNROLL
                    dve.wait_ge(pre_mm, r + 1)
                    dve.wait_ge(gathered[z], 16 * TILES * use(r, z))
                    if reached(r, 2):
                        dve.wait_ge(normed_s, r - 1)
                    nc.vector.tensor_tensor(
                        pre[:, v].rearrange("p (t h) d -> p t h d", h=2),
                        pre_ps[v][:, :, 0:2 * PRE].rearrange("p t (h d) -> p t h d", h=2),
                        gath[:, z].rearrange("p (t h) d -> p t h d", h=2), ALU.add).then_inc(pre_summed, 1)
                if stage(w, drained, 4):
                    r, v = w - 4, u % 2
                    dve.wait_ge(measured, r + 1)
                    if reached(r, 2):
                        dve.wait_ge(agg_mm, r - 1)
                    nc.vector.tensor_scalar(gate[:, v], gexp[:, v], 1.0, None, ALU.add).then_inc(gated, 1)
                    for i in range(TILES):
                        last = nc.vector.scalar_tensor_tensor(out=msg[:, v, i, :], in0=pre[:, v, i, 0:D],
                                                              scalar=rstd[:, v, i:i + 1], in1=ln_g[:],
                                                              op0=ALU.mult, op1=ALU.mult)
                    last.then_inc(scaled, 1)
                    dve.wait_ge(gated, 2 * r + 1)
                    nc.vector.reciprocal(gate[:, v], gate[:, v]).then_inc(gated, 1)
                    dve.wait_ge(scaled, r + 1)
                    nc.vector.tensor_tensor(msg[:, v], msg[:, v], ln_b[:].broadcast_to([P, TILES, D]),
                                            ALU.add).then_inc(normed_s, 1)
                if stage(w, drained, 0):
                    dve.wait_ge(meta_in[u], 16 * use(w, u))
                    dve.wait_ge(base_in[u // BATCH], 16 * use(w, u))
                    if reached(w, UNROLL):
                        dve.wait_ge(agg_mm, w - UNROLL + 1)
                    nc.vector.scalar_tensor_tensor(
                        out=by_edge[:, u], in0=iota[:].unsqueeze(1).broadcast_to([P, TILES, P]), scalar=base[:, u:u + 1],
                        in1=meta[:, u, TILES:2 * TILES].unsqueeze(2).broadcast_to([P, TILES, P]),
                        op0=ALU.add, op1=ALU.is_equal).then_inc(by_edge_built, 1)
                if stage(w, drained, SUM_LAG):
                    r, v, first = w - SUM_LAG, u % 2, loaded["first"][u]
                    dve.wait_ge(agg_mm, r + 1)
                    if reached(r, 1):
                        dve.wait_ge(acc_done, r)
                    nc.vector.tensor_tensor(agg[:, :, bass.ds(first, P)], agg[:, :, bass.ds(first, P)],
                                            agg_ps[v][:, 0:2 * P].rearrange("p (c n) -> p c n", c=2), ALU.add).then_inc(acc_done, 1)

            over_items(dve, step, passes, SUM_LAG)

        @block.scalar
        def _(act):
            act.dma_start(w_edge[:], io["w1_edges"]).then_inc(w_in, 16)
            act.dma_start(ln_g[:], io["ln_g"].broadcast_to([P, D])).then_inc(w_in, 16)
            act.dma_start(ln_b[:, 0, :], io["ln_b"].broadcast_to([P, D])).then_inc(w_in, 16)
            nc.scalar.preload_act_table_set("natural_log_exp_and_others")
            passes = act.value_load(ctl[0:1, 0:1], min_val=MIN_PASSES - 1, max_val=MAX_PASSES - 1) + 1

            def step(w, u, drained):
                if stage(w, drained, 1):
                    r, v = w - 1, (u - 1) % 2
                    act.wait_ge(turned, r + 1)
                    if reached(r, 2):
                        act.wait_ge(pre_mm, r - 1)
                    nc.scalar.copy(by_node[:, v], turned_ps[v][:]).then_inc(by_node_built, 1)
                if stage(w, drained, 3):
                    r, v = w - 3, (u - 3) % 2
                    act.wait_ge(pre_summed, r + 1)
                    if reached(r, 2):
                        act.wait_ge(normed_s, r - 1)
                        act.wait_ge(gated, 2 * r - 2)
                    if reached(r, 1):
                        act.wait_ge(measured, r)
                    for i in range(TILES):
                        if i or reached(r, 1):
                            act.wait_ge(squares, TILES * r + i)
                        nc.scalar.activation(junk[:], pre[:, v, i, 0:D], ACT.Square,
                                             accum_out=ss[:, i:i + 1]).then_inc(squares, 1)
                    nc.scalar.activation(gexp[:, v], pre[:, v, :, D], ACT.Exp, scale=-1.0)
                    act.wait_ge(squares, TILES * (r + 1))
                    nc.scalar.activation(rstd[:, v], ss[:], ACT.Ln, bias=keep["eps"][:], scale=1.0 / D).then_inc(logs, 1)
                    act.wait_ge(logs, r + 1)
                    nc.scalar.activation(rstd[:, v], rstd[:, v], ACT.Exp, scale=-0.5).then_inc(measured, 1)
                if stage(w, drained, 4):
                    r, v = w - 4, u % 2
                    act.wait_ge(normed_s, r + 1)
                    act.wait_ge(gated, 2 * r + 2)
                    for i in range(TILES):
                        last = nc.scalar.activation(msg[:, v, i, :], msg[:, v, i, :], ACT.Relu,
                                                    scale=gate[:, v, i:i + 1])
                    last.then_inc(msg_ready, 1)

            over_items(act, step, passes, SUM_LAG)


def gru_nodes(nc, io, dram, keep, NP):
    agg, ident, nodes = keep["agg"], keep["ident"], keep["nodes"]
    NQ = NP // QUAD
    UP = 1.0 / float(MUL) ** 0.5
    GRU_LAG, GRU_PEEL, UP_LAG, UP_PEEL = 4, 8, 2, 4
    with ExitStack() as ctx:
        def sb(name, shape, dt):
            return ctx.enter_context(nc.sbuf_tensor("gru_" + name, shape, dt))

        def pb(name):
            return ctx.enter_context(nc.psum_tensor("gru_" + name, [P, QUAD], F32))

        def sem(name):
            return ctx.enter_context(nc.semaphore("gru_" + name))

        w2 = sb("w2", [P, D], F32)
        b2 = sb("b2", [P, 1], F32)
        w_ih = sb("w_ih", [P, 3 * D], F32)
        w_hh = sb("w_hh", [P, 3 * D], F32)
        b_ih = sb("b_ih", [P, 3], F32)
        b_hh = sb("b_hh", [P, 3], F32)
        b_sum = sb("b_sum", [P, 3], F32)
        w_up = sb("w_up", [P, D], F32)
        x = sb("x", [P, SLOTS, 4, D], F32)
        mT = sb("mT", [P, 2, QUAD], F32)
        rT = sb("rT", [P, QUAD], F32)
        zT = sb("zT", [P, 2, QUAD], F32)
        nT = sb("nT", [P, 2, QUAD], F32)
        oT = sb("oT", [P, 2, QUAD], F32)
        x1 = sb("x1", [P, 2, 4, D], F32)
        stats = sb("stats", [P, 2, 4, 6], F32)
        mv = sb("mv", [P, 2, 4, 2], F32)
        mv_all = sb("mv_all", [P, 4 * NQ, 2], F32)
        rstd = sb("rstd", [P, 4 * NQ], F32)
        h2 = sb("h2", [P, 2, 4, D], F32)
        h2T = sb("h2T", [P, 2, QUAD], F32)
        up = sb("up", [P, SLOTS, 4, D], F32)
        m_ps, r_ps, z_ps, i_ps, n_ps, o_ps, h_ps, u_ps = (pb(n) for n in (
            "m_ps", "r_ps", "z_ps", "i_ps", "n_ps", "o_ps", "h_ps", "u_ps"))
        h_pair, u_pair = [h_ps, r_ps], [u_ps, z_ps]

        w_in, biases = sem("w_in"), sem("biases")
        x_in = [sem(f"x_in{s}") for s in range(SLOTS)]
        m_mm, m_copied, rz_mm, in_mm, rz_ready = (sem(n) for n in ("m_mm", "m_copied", "rz_mm", "in_mm", "rz_ready"))
        n_in, n_ready, diff, mixed, o_turned = (sem(n) for n in ("n_in", "n_ready", "diff", "mixed", "o_turned"))
        joining = sem("joining")
        x1_ready, measured, moments, noted, kept, rooted, inverted = (sem(n) for n in (
            "x1_ready", "measured", "moments", "noted", "kept", "rooted", "inverted"))
        normed, h_turned, h2T_ready, u_mm, u_ready = (sem(n) for n in ("normed", "h_turned", "h2T_ready", "u_mm", "u_ready"))
        u_stored = [sem(f"u_stored{s}") for s in range(SLOTS)]
        cleared = sem("cleared")
        block = ctx.enter_context(nc.Block())

        def flat(t):
            return t.rearrange("p t d -> p (t d)")

        @block.sync
        def _(sp):
            for tile, name in ((w2, "w2"), (b2, "b2"), (w_ih, "w_ih"), (w_hh, "w_hh")):
                sp.dma_start(tile[:], io[name]).then_inc(w_in, 16)

            def gru_step(q, s):
                if has_quad(q, NQ):
                    if reached(q, SLOTS):
                        sp.wait_ge(x1_ready, q - SLOTS + 1)
                    sp.dma_start(x[:, s], quad_rows(io["x"], q)).then_inc(x_in[s], 16)

            def up_step(q, s):
                if has_quad(q - 2, NQ):
                    r, z = q - 2, (s - 2) % SLOTS
                    sp.wait_ge(u_ready, r + 1)
                    sp.dma_start(quad_rows(dram["u_table"], r), up[:, z]).then_inc(u_stored[z], 16)

            over_quads(sp, gru_step, NQ, 0, GRU_PEEL)
            over_quads(sp, up_step, NQ, UP_LAG, UP_PEEL)
            for s in range(SLOTS):
                if NQ > s:
                    sp.wait_ge(u_stored[s], 16 * ((NQ - s - 1) // SLOTS + 1))

        @block.tensor
        def _(pe):
            pe.wait_ge(w_in, 16 * 7)

            def gru_step(q, s):
                if has_quad(q, NQ):
                    cols = bass.ds(q * QUAD, QUAD)
                    if reached(q, 1):
                        pe.wait_ge(m_copied, q)
                    nc.tensor.matmul(m_ps[:], w2[:], agg[:, 0, cols], start=True, stop=True).then_inc(m_mm, 1)
                if has_quad(q - 1, NQ):
                    r, v = q - 1, (s - 1) % 2
                    cols = bass.ds(r * QUAD, QUAD)
                    if reached(r, 1):
                        pe.wait_ge(rz_ready, 2 * r)
                    pe.wait_ge(m_copied, r + 1)
                    for k, out in enumerate((r_ps, z_ps)):
                        nc.tensor.matmul(out[:], w_hh[:, k * D:(k + 1) * D], nodes[:, cols], start=True, stop=False)
                        nc.tensor.matmul(out[:], w_ih[:, k * D:(k + 1) * D], mT[:, v], start=False, stop=True).then_inc(rz_mm, 1)
                    if reached(r, 1):
                        pe.wait_ge(n_in, 2 * r)
                    nc.tensor.matmul(n_ps[:], w_hh[:, 2 * D:3 * D], nodes[:, cols], start=True, stop=True)
                    nc.tensor.matmul(i_ps[:], w_ih[:, 2 * D:3 * D], mT[:, v], start=True, stop=True).then_inc(in_mm, 1)
                if has_quad(q - 3, NQ):
                    r, v = q - 3, (s - 3) % 2
                    pe.wait_ge(mixed, 2 * r + 2)
                    if reached(r, 1):
                        pe.wait_ge(x1_ready, r)
                    for t in range(4):
                        last = nc.tensor.transpose(o_ps[:, t * P:(t + 1) * P], oT[:, v, t * P:(t + 1) * P], ident[:])
                    last.then_inc(o_turned, 1)

            def up_step(q, s):
                if has_quad(q - 1, NQ):
                    r, v = q - 1, (s - 1) % 2
                    pe.wait_ge(normed, r + 1)
                    if reached(r, 2):
                        pe.wait_ge(h2T_ready, r - 1)
                    for t in range(4):
                        last = nc.tensor.transpose(h_pair[v][:, t * P:(t + 1) * P], h2[:, v, t, :], ident[:])
                    last.then_inc(h_turned, 1)
                if has_quad(q - 2, NQ):
                    r, v = q - 2, s % 2
                    pe.wait_ge(h2T_ready, r + 1)
                    if reached(r, 2):
                        pe.wait_ge(u_ready, r - 1)
                    for t in range(4):
                        last = nc.tensor.matmul(u_pair[v][:, t * P:(t + 1) * P], h2T[:, v, t * P:(t + 1) * P], w_up[:], start=True, stop=True)
                    last.then_inc(u_mm, 1)

            over_quads(pe, gru_step, NQ, GRU_LAG, GRU_PEEL)
            over_quads(pe, up_step, NQ, UP_LAG, UP_PEEL)

        @block.scalar
        def _(act):
            for tile, name in ((b_ih, "b_ih"), (b_hh, "b_hh"), (w_up, "w_up")):
                act.dma_start(tile[:], io[name]).then_inc(w_in, 16)
            act.wait_ge(biases, 1)

            def gru_step(q, s):
                if has_quad(q - 2, NQ):
                    r, v = q - 2, s % 2
                    act.wait_ge(n_in, 2 * r + 2)
                    nc.scalar.activation(nT[:, v], nT[:, v], ACT.Tanh, bias=b_ih[:, 2:3]).then_inc(n_ready, 1)
                if has_quad(q - 1, NQ):
                    r, v = q - 1, (s - 1) % 2
                    act.wait_ge(rz_mm, 2 * r + 1)
                    if reached(r, 1):
                        act.wait_ge(n_in, 2 * r)
                    nc.scalar.activation(rT[:], r_ps[:], ACT.Sigmoid, bias=b_sum[:, 0:1]).then_inc(rz_ready, 1)
                    act.wait_ge(rz_mm, 2 * r + 2)
                    if reached(r, 2):
                        act.wait_ge(mixed, 2 * r - 3)
                    nc.scalar.activation(zT[:, v], z_ps[:], ACT.Sigmoid, bias=b_sum[:, 1:2]).then_inc(rz_ready, 1)

            def up_step(q, s):
                if has_quad(q - 1, NQ):
                    r, v = q - 1, (s - 1) % 2
                    act.wait_ge(h_turned, r + 1)
                    if reached(r, 2):
                        act.wait_ge(u_mm, r - 1)
                    nc.scalar.activation(h2T[:, v], h_pair[v][:], ACT.Relu).then_inc(h2T_ready, 1)
                if has_quad(q - 2, NQ):
                    r, v, z = q - 2, s % 2, (s - 2) % SLOTS
                    act.wait_ge(u_mm, r + 1)
                    if reached(r, SLOTS):
                        act.wait_ge(u_stored[z], 16 * (quad_use(r, z) - 1))
                    nc.scalar.activation(flat(up[:, z]), u_pair[v][:], ACT.Copy, scale=UP).then_inc(u_ready, 1)

            over_quads(act, gru_step, NQ, GRU_LAG, GRU_PEEL)
            act.wait_ge(noted, NQ)
            nc.scalar.activation(rstd[:], mv_all[:, :, 1], ACT.Sqrt, bias=keep["eps"][:]).then_inc(rooted, 1)
            over_quads(act, up_step, NQ, UP_LAG, UP_PEEL)

        @block.gpsimd
        def _(pool):
            def gru_step(q, s):
                if has_quad(q - 2, NQ):
                    r, v = q - 2, s % 2
                    pool.wait_ge(diff, r + 1)
                    nc.gpsimd.tensor_tensor(oT[:, v], oT[:, v], zT[:, v], ALU.mult).then_inc(mixed, 1)
                    pool.wait_ge(mixed, 2 * r + 1)
                    nc.gpsimd.tensor_tensor(oT[:, v], oT[:, v], nT[:, v], ALU.add).then_inc(mixed, 1)

            over_quads(pool, gru_step, NQ, GRU_LAG, GRU_PEEL)
            pool.wait_ge(m_copied, NQ)
            nc.gpsimd.memset(agg[:], 0.0).then_inc(cleared, 1)
            pool.wait_ge(cleared, 1)

        @block.vector
        def _(dve):
            dve.wait_ge(w_in, 16 * 7)
            nc.vector.tensor_tensor(b_sum[:], b_ih[:], b_hh[:], ALU.add).then_inc(biases, 1)

            def gru_step(q, s):
                if has_quad(q - 4, NQ):
                    r, z, v = q - 4, s, s % 2
                    dve.wait_ge(o_turned, r + 1)
                    dve.wait_ge(x_in[z], 16 * quad_use(r, z))
                    if reached(r, 2):
                        dve.wait_ge(kept, r - 1)
                    nc.vector.tensor_tensor(flat(x1[:, v]), flat(x[:, z]), o_ps[:], ALU.add).then_inc(x1_ready, 1)
                    dve.wait_ge(x1_ready, r + 1)
                    if reached(r, 2):
                        dve.wait_ge(moments, r - 1)
                    dve.sem_inc(joining, 1)
                    for t in range(4):
                        last = nc.vector.bn_stats(stats[:, v, t, :], x1[:, v, t, :])
                    last.then_inc(measured, 1)
                    nc.vector.tensor_copy(nodes[:, bass.ds(r * QUAD, QUAD)], flat(x1[:, v])).then_inc(kept, 1)
                    dve.wait_ge(measured, r + 1)
                    if reached(r, 2):
                        dve.wait_ge(noted, r - 1)
                    dve.sem_inc(joining, 1)
                    for t in range(4):
                        last = nc.vector.bn_aggr(mv[:, v, t, :], stats[:, v, t, :])
                    last.then_inc(moments, 1)
                if has_quad(q, NQ):
                    v = s % 2
                    dve.wait_ge(m_mm, q + 1)
                    if reached(q, 2):
                        dve.wait_ge(in_mm, q - 1)
                    nc.vector.scalar_tensor_tensor(out=mT[:, v], in0=agg[:, 1, bass.ds(q * QUAD, QUAD)], scalar=b2[:, 0:1],
                                                   in1=m_ps[:], op0=ALU.mult, op1=ALU.add).then_inc(m_copied, 1)
                if has_quad(q - 2, NQ):
                    r, v = q - 2, s % 2
                    dve.wait_ge(n_ready, r + 1)
                    if reached(r, 2):
                        dve.wait_ge(o_turned, r - 1)
                    nc.vector.tensor_tensor(oT[:, v], nodes[:, bass.ds(r * QUAD, QUAD)], nT[:, v], ALU.subtract).then_inc(diff, 1)
                if has_quad(q - 4, NQ):
                    r, v = q - 4, s % 2
                    dve.wait_ge(moments, r + 1)
                    nc.vector.tensor_copy(mv_all[:, bass.ds(4 * r, 4), :], mv[:, v]).then_inc(noted, 1)
                if has_quad(q - 1, NQ):
                    r, v = q - 1, (s - 1) % 2
                    dve.wait_ge(in_mm, r + 1)
                    dve.wait_ge(rz_ready, 2 * r + 1)
                    if reached(r, 2):
                        dve.wait_ge(mixed, 2 * r - 2)
                    nc.vector.scalar_tensor_tensor(out=nT[:, v], in0=n_ps[:], scalar=b_hh[:, 2:3], in1=rT[:],
                                                   op0=ALU.add, op1=ALU.mult).then_inc(n_in, 1)
                    dve.wait_ge(n_in, 2 * r + 1)
                    nc.vector.tensor_tensor(nT[:, v], nT[:, v], i_ps[:], ALU.add).then_inc(n_in, 1)

            def up_step(q, s):
                if has_quad(q, NQ):
                    v = s % 2
                    if reached(q, 2):
                        dve.wait_ge(h_turned, q - 1)
                    for t in range(4):
                        last = nc.vector.tensor_scalar(h2[:, v, t, :], nodes[:, bass.ds(q * QUAD + t * P, P)],
                                                       mv_all[:, bass.ds(4 * q + t, 1), 0], rstd[:, bass.ds(4 * q + t, 1)],
                                                       ALU.subtract, ALU.mult)
                    last.then_inc(normed, 1)

            over_quads(dve, gru_step, NQ, GRU_LAG, GRU_PEEL)
            dve.wait_ge(kept, NQ)
            dve.wait_ge(rooted, 1)
            nc.vector.reciprocal(rstd[:], rstd[:]).then_inc(inverted, 1)
            dve.wait_ge(inverted, 1)
            over_quads(dve, up_step, NQ, UP_LAG, UP_PEEL)


def tensor_edges(nc, io, dram, keep, NP, NG, J):
    agg, iota, ctl = keep["agg"], keep["iota"], keep["ctl"]
    MIN_PASSES, MAX_PASSES = NG // UNROLL, P * J // UNROLL
    HALF = GROUP // 2
    KIN = 2 * NB
    VEC = slice(MUL, 4 * MUL)
    with ExitStack() as ctx:
        def sb(name, shape, dt):
            return ctx.enter_context(nc.sbuf_tensor("tensor_" + name, shape, dt))

        def pb(name, shape):
            return ctx.enter_context(nc.psum_tensor("tensor_" + name, shape, F32))

        def sem(name):
            return ctx.enter_context(nc.semaphore("tensor_" + name))

        mlp0 = sb("mlp0", [P, P], F32)
        mlp1 = sb("mlp1", [P, P], F32)
        mlp2 = sb("mlp2", [P, 2 * D], F32)
        bias0 = sb("bias0", [P, 1], F32)
        bias1 = sb("bias1", [P, 1], F32)
        bias2 = sb("bias2", [1, 2 * D], F32)
        bias2_rest = sb("bias2_rest", [1, 2 * D], F32)
        bias2_part = sb("bias2_part", [1, SPLITS, 2 * D], BF16)
        ones = sb("ones", [1, P], BF16)
        meta = sb("meta", [P, UNROLL, 2 * TILES], I32)
        base = sb("base", [P, UNROLL], F32)
        y = sb("y", [P, UNROLL, TILES, 3], F32)
        emb = sb("emb", [P, UNROLL, HALF], F32)
        gath = sb("gath", [P, UNROLL, TILES, D], F32)
        h0 = sb("h0", [P, 2, HALF], F32)
        h1 = sb("h1", [P, 2, HALF], F32)
        by_edge = sb("by_edge", [P, 2, TILES, P], F32)
        msg = sb("msg", [P, 2, TILES, MSG], F32)
        prod = sb("prod", [P, TILES, 3, MUL], F32)
        dot = sb("dot", [P, TILES, MUL], F32)
        h0_ps = pb("h0_ps", [P, 512])
        h1_ps = pb("h1_ps", [P, 512])
        w_ps = [pb(f"w_ps{i}", [P, TILES, D]) for i in range(2)]
        agg_ps = [pb(f"agg_ps{i}", [P, 512]) for i in range(4)]

        w_in, cleared, split, ready = sem("w_in"), sem("cleared"), sem("split"), sem("ready")
        meta_in, edge_in, gathered, base_in, started = (keep[k] for k in ("meta_in", "edge_in", "gathered", "base_in", "started"))
        h0_mm, h0_ready, h1_mm, h1_ready, w_mm = (sem(n) for n in ("h0_mm", "h0_ready", "h1_mm", "h1_ready", "w_mm"))
        built, scal, prods, dots, msg_ready, agg_mm, acc_done = (sem(n) for n in ("built", "scal", "prods", "dots", "msg_ready", "agg_mm", "acc_done"))
        block = ctx.enter_context(nc.Block())

        def use(item, u):
            return item // UNROLL + 1 if isinstance(item, int) else (item - u) // UNROLL + 1

        @block.sync
        def _(sp):
            passes = sp.value_load(ctl[0:1, 0:1], min_val=MIN_PASSES - 1, max_val=MAX_PASSES - 1) + 1
            loaded = {}

            def step(w, u, drained):
                if u == 0:
                    loaded["group"] = load_pass(nc, mybir.EngineType.SP, dram["item_group"], w, UNROLL, NG - 1)
                g = loaded["group"][u]
                if u % BATCH == 0:
                    if reached(w, UNROLL):
                        sp.wait_ge(built, w - UNROLL + BATCH)
                    sp.dma_start(base[:, u:u + BATCH],
                                 dram["item_base_f"][0:1, bass.ds(w, BATCH)].broadcast_to([P, BATCH])).then_inc(base_in[u // BATCH], 16)
                if reached(w, UNROLL):
                    sp.wait_ge(msg_ready, w - UNROLL + 1)
                sp.dma_start(meta[:, u], io["meta"][bass.ds(g, 1)].rearrange("a p k -> (a p) k")).then_inc(meta_in[u], 16)
                if isinstance(w, int) and w == 0:
                    sp.wait_ge(cleared, 1)
                sp.dma_start(y[:, u].rearrange("p i k -> p (i k)"),
                             dram["y_edges"][:, bass.ds(g * (TILES * 3), TILES * 3)]).then_inc(edge_in[u], 16)
                for half in range(2):
                    sp.dma_start(emb[half * NB:(half + 1) * NB, u],
                                 dram["emb_edges"][:, bass.ds(g * GROUP + half * HALF, HALF)]).then_inc(edge_in[u], 16)

            over_items(sp, step, passes, 0)

        @block.gpsimd
        def _(pool):
            passes = pool.value_load(ctl[0:1, 0:1], min_val=MIN_PASSES - 1, max_val=MAX_PASSES - 1) + 1
            meta_before = pool.snap(16 * passes)

            def step(w, u, drained):
                pool.wait_ge(meta_in[u], 16 * use(w, u) + meta_before)
                if reached(w, UNROLL):
                    pool.wait_ge(msg_ready, w - UNROLL + 1)
                pool.sem_inc(started, 1)
                for i in range(TILES):
                    nc.gpsimd.indirect_dma_start(
                        gath[:, u, i, :], None, dram["u_table"],
                        bass.IndirectOffsetOnAxis(ap=meta[:, u, i:i + 1], axis=0)).then_inc(gathered[u], 16)

            over_items(pool, step, passes, 0)

        @block.tensor
        def _(pe):
            passes = pe.value_load(ctl[0:1, 0:1], min_val=MIN_PASSES - 1, max_val=MAX_PASSES - 1) + 1
            edges_before = pe.snap(32 * passes)
            pe.wait_ge(ready, 1)
            pe.wait_ge(w_in, 16 * 6)

            def step(w, u, drained):
                if stage(w, drained, 2):
                    r, v = w - 2, u % 2
                    pe.wait_ge(h1_ready, r + 1)
                    if reached(r, 2):
                        pe.wait_ge(msg_ready, r - 1)
                    for t in range(2):
                        out = w_ps[v][:, 2 * t:2 * t + 2, :].rearrange("p h d -> p (h d)")
                        for k in range(SPLITS):
                            nc.tensor.matmul(out, ones[:], bias2_part[:, k, :], start=(k == 0), stop=False)
                        last = nc.tensor.matmul(out, h1[:, v, t * P:(t + 1) * P], mlp2[:], start=False, stop=True)
                    last.then_inc(w_mm, 1)
                if stage(w, drained, 0):
                    pe.wait_ge(edge_in[u], 48 * use(w, u) + edges_before)
                    if reached(w, 1):
                        pe.wait_ge(h0_ready, w)
                    nc.tensor.matmul(h0_ps[:, 0:HALF], mlp0[:], emb[:, u], start=True, stop=True).then_inc(h0_mm, 1)
                if stage(w, drained, 1):
                    r, v = w - 1, (u + 1) % 2
                    pe.wait_ge(h0_ready, r + 1)
                    if reached(r, 1):
                        pe.wait_ge(h1_ready, r)
                    nc.tensor.matmul(h1_ps[:, 0:HALF], mlp1[:], h0[:, v], start=True, stop=True).then_inc(h1_mm, 1)
                if stage(w, drained, 4):
                    r, v, a = w - 4, u % 2, u % 4
                    pe.wait_ge(msg_ready, r + 1)
                    if reached(r, 4):
                        pe.wait_ge(acc_done, r - 3)
                    for c in range(2):
                        for i in range(TILES):
                            last = nc.tensor.matmul(agg_ps[a][:, c * P:(c + 1) * P],
                                                    msg[:, v, i, MUL + c * P:MUL + (c + 1) * P], by_edge[:, v, i, :],
                                                    start=(i == 0), stop=(i == TILES - 1))
                    last.then_inc(agg_mm, 1)

            over_items(pe, step, passes, SUM_LAG)

        @block.scalar
        def _(act):
            for tile, name in ((mlp0, "mlp0"), (mlp1, "mlp1"), (mlp2, "mlp2"), (bias0, "mlp_b0"), (bias1, "mlp_b1"), (bias2, "mlp_b2")):
                act.dma_start(tile[:], io[name]).then_inc(w_in, 16)
            passes = act.value_load(ctl[0:1, 0:1], min_val=MIN_PASSES - 1, max_val=MAX_PASSES - 1) + 1
            act.wait_ge(w_in, 16 * 6)

            def step(w, u, drained):
                if stage(w, drained, 0):
                    v = u % 2
                    act.wait_ge(h0_mm, w + 1)
                    if reached(w, 2):
                        act.wait_ge(h1_mm, w - 1)
                    nc.scalar.activation(h0[:, v], h0_ps[:, 0:HALF], ACT.Silu, bias=bias0[:]).then_inc(h0_ready, 1)
                if stage(w, drained, 1):
                    r, v = w - 1, (u + 1) % 2
                    act.wait_ge(h1_mm, r + 1)
                    if reached(r, 2):
                        act.wait_ge(w_mm, r - 1)
                    nc.scalar.activation(h1[:, v], h1_ps[:, 0:HALF], ACT.Silu, bias=bias1[:]).then_inc(h1_ready, 1)

            over_items(act, step, passes, 1)

        @block.vector
        def _(dve):
            passes = dve.value_load(ctl[0:1, 0:1], min_val=MIN_PASSES - 1, max_val=MAX_PASSES - 1) + 1
            meta_before = dve.snap(16 * passes)
            edges_before = dve.snap(32 * passes)
            gathers_before = dve.snap(16 * TILES * passes)
            nc.vector.memset(emb[:], 0.0).then_inc(cleared, 1)
            nc.vector.memset(ones[:], 1.0)
            dve.wait_ge(w_in, 16 * 6)
            nc.vector.tensor_copy(bias2_part[:, 0, :], bias2[:]).then_inc(split, 1)
            dve.wait_ge(split, 1)
            nc.vector.tensor_tensor(bias2_rest[:], bias2[:], bias2_part[:, 0, :], ALU.subtract).then_inc(split, 1)
            dve.wait_ge(split, 2)
            nc.vector.tensor_copy(bias2_part[:, 1, :], bias2_rest[:]).then_inc(split, 1)
            dve.wait_ge(split, 3)
            nc.vector.tensor_tensor(bias2_rest[:], bias2_rest[:], bias2_part[:, 1, :], ALU.subtract).then_inc(split, 1)
            dve.wait_ge(split, 4)
            nc.vector.tensor_copy(bias2_part[:, 2, :], bias2_rest[:]).then_inc(ready, 1)

            loaded = {}

            def step(w, u, drained):
                if u == 0:
                    loaded["first"] = load_pass(nc, mybir.EngineType.DVE, dram["sum_base"], w,
                                                UNROLL if drained < 0 else SUM_LAG, NP - P)
                if stage(w, drained, SUM_LAG):
                    r, a, first = w - SUM_LAG, (u - SUM_LAG) % 4, loaded["first"][u]
                    dve.wait_ge(agg_mm, r + 1)
                    if reached(r, 1):
                        dve.wait_ge(acc_done, r)
                    nc.vector.tensor_tensor(agg[:, :, bass.ds(first, P)], agg[:, :, bass.ds(first, P)],
                                            agg_ps[a][:, 0:2 * P].rearrange("p (c n) -> p c n", c=2), ALU.add).then_inc(acc_done, 1)
                if stage(w, drained, 3):
                    r, v, z = w - 3, (u - 3) % 2, (u - 3) % UNROLL
                    dve.wait_ge(meta_in[z], 16 * use(r, z) + meta_before)
                    if reached(r, 2):
                        dve.wait_ge(agg_mm, r - 1)
                    dve.wait_ge(base_in[z // BATCH], 16 * use(r, z) + meta_before)
                    nc.vector.scalar_tensor_tensor(
                        out=by_edge[:, v], in0=iota[:].unsqueeze(1).broadcast_to([P, TILES, P]), scalar=base[:, z:z + 1],
                        in1=meta[:, z, TILES:2 * TILES].unsqueeze(2).broadcast_to([P, TILES, P]),
                        op0=ALU.add, op1=ALU.is_equal).then_inc(built, 1)
                    dve.wait_ge(gathered[z], 16 * TILES * use(r, z) + gathers_before)
                    dve.wait_ge(edge_in[z], 48 * use(r, z) + edges_before)
                    m, g, wt = msg[:, v], gath[:, z], w_ps[v]
                    vec = g[:, :, VEC].rearrange("p i (c k) -> p i c k", c=3)
                    if reached(r, 1):
                        dve.wait_ge(dots, r)
                    nc.vector.tensor_tensor(prod[:], vec, y[:, z].unsqueeze(3).broadcast_to([P, TILES, 3, MUL]),
                                            ALU.mult).then_inc(prods, 1)
                    dve.wait_ge(w_mm, r + 1)
                    nc.vector.tensor_tensor(m[:, :, 0:2 * MUL].rearrange("p i (j k) -> p i j k", j=2),
                                            wt[:, :, 0:2 * MUL].rearrange("p i (j k) -> p i j k", j=2),
                                            g[:, :, 0:MUL].unsqueeze(2).broadcast_to([P, TILES, 2, MUL]), ALU.mult).then_inc(scal, 1)
                    dve.wait_ge(prods, r + 1)
                    if reached(r, 1):
                        dve.wait_ge(msg_ready, r)
                    nc.vector.tensor_reduce(dot[:], prod[:].rearrange("p i c k -> p i k c"), AX.X, ALU.add).then_inc(dots, 1)
                    nc.vector.tensor_tensor(m[:, :, 3 * MUL:6 * MUL].rearrange("p i (c k) -> p i c k", c=3), vec,
                                            wt[:, :, 3 * MUL:4 * MUL].unsqueeze(2).broadcast_to([P, TILES, 3, MUL]), ALU.mult)
                    dve.wait_ge(scal, r + 1)
                    nc.vector.tensor_tensor(m[:, :, 6 * MUL:9 * MUL].rearrange("p i (c k) -> p i c k", c=3),
                                            m[:, :, 0:MUL].unsqueeze(2).broadcast_to([P, TILES, 3, MUL]),
                                            y[:, z].unsqueeze(3).broadcast_to([P, TILES, 3, MUL]), ALU.mult)
                    dve.wait_ge(dots, r + 1)
                    nc.vector.scalar_tensor_tensor(out=m[:, :, 2 * MUL:3 * MUL], in0=dot[:], scalar=1.0 / SQ3,
                                                   in1=wt[:, :, 2 * MUL:3 * MUL], op0=ALU.mult, op1=ALU.mult).then_inc(msg_ready, 1)

            over_items(dve, step, passes, SUM_LAG)


def output_nodes(nc, io, dram, keep, NP):
    agg, nodes = keep["agg"], keep["nodes"]
    NQ = NP // QUAD
    LAG, PEEL = 3, 4
    SCALE = 1.0 / (float(2 * MUL) ** 0.5 * 16.0)
    with ExitStack() as ctx:
        def sb(name, shape, dt):
            return ctx.enter_context(nc.sbuf_tensor("final_" + name, shape, dt))

        def sem(name):
            return ctx.enter_context(nc.semaphore("final_" + name))

        w_out = sb("w_out", [P, 2, D], F32)
        sums = sb("sums", [P, SLOTS, 2, QUAD], F32)
        out = sb("out", [P, SLOTS, QUAD], F32)
        out_ps = [ctx.enter_context(nc.psum_tensor(f"final_out_ps{i}", [P, QUAD], F32)) for i in range(SLOTS)]
        w_in = sem("w_in")
        stored = [sem(f"stored{s}") for s in range(SLOTS)]
        copied = [sem("copied0"), sem("copied1")]
        out_mm, out_ready = sem("out_mm"), sem("out_ready")
        block = ctx.enter_context(nc.Block())

        @block.sync
        def _(sp):
            sp.dma_start(w_out[:], io["w_out"]).then_inc(w_in, 16)

            def step(q, s):
                if has_quad(q - 3, NQ):
                    r, z = q - 3, (s - 3) % SLOTS
                    sp.wait_ge(out_ready, r + 1)
                    sp.dma_start(quad_rows(io["out"], r), out[:, z].rearrange("p (t d) -> p t d", d=D)).then_inc(stored[z], 16)

            over_quads(sp, step, NQ, LAG, PEEL)
            for s in range(SLOTS):
                if NQ > s:
                    sp.wait_ge(stored[s], 16 * ((NQ - s - 1) // SLOTS + 1))

        @block.scalar
        def _(act):
            def step(q, s):
                if has_quad(q, NQ):
                    if reached(q, SLOTS):
                        act.wait_ge(out_mm, q - SLOTS + 1)
                    nc.scalar.copy(sums[:, s, 0], agg[:, 0, bass.ds(q * QUAD, QUAD)]).then_inc(copied[0], 1)

            over_quads(act, step, NQ, LAG, PEEL)

        @block.tensor
        def _(pe):
            pe.wait_ge(w_in, 16)

            def step(q, s):
                if has_quad(q - 1, NQ):
                    r, z = q - 1, (s - 1) % SLOTS
                    for c in range(2):
                        pe.wait_ge(copied[c], r + 1)
                    if reached(r, SLOTS):
                        pe.wait_ge(out_ready, r - SLOTS + 1)
                    for t in range(4):
                        for c in range(2):
                            last = nc.tensor.matmul(out_ps[z][:, t * P:(t + 1) * P], sums[:, z, c, t * P:(t + 1) * P], w_out[:, c, :],
                                                    start=(c == 0), stop=(c == 1))
                    last.then_inc(out_mm, 1)

            over_quads(pe, step, NQ, LAG, PEEL)

        @block.vector
        def _(dve):
            def step(q, s):
                if has_quad(q, NQ):
                    if reached(q, SLOTS):
                        dve.wait_ge(out_mm, q - SLOTS + 1)
                    nc.vector.tensor_copy(sums[:, s, 1], agg[:, 1, bass.ds(q * QUAD, QUAD)]).then_inc(copied[1], 1)
                if has_quad(q - 2, NQ):
                    r, z = q - 2, (s - 2) % SLOTS
                    dve.wait_ge(out_mm, r + 1)
                    if reached(r, SLOTS):
                        dve.wait_ge(stored[z], 16 * (quad_use(r, z) - 1))
                    nc.vector.scalar_tensor_tensor(out=out[:, z], in0=out_ps[z][:], scalar=SCALE, in1=nodes[:, bass.ds(r * QUAD, QUAD)],
                                                   op0=ALU.mult, op1=ALU.add).then_inc(out_ready, 1)

            over_quads(dve, step, NQ, LAG, PEEL)


def kernel(**inputs):
    import numpy as np
    import concourse.bacc as bacc
    from concourse.bass_utils import run_bass_kernel_spmd

    a = {k: np.asarray(v) for k, v in inputs.items()}
    N, E = a["x"].shape[0], a["src"].shape[0]
    NP, NG, J = layout(N, E)
    EP = NG * GROUP

    def padded(rows, n, value=0):
        out = np.full((n,) + rows.shape[1:], value, rows.dtype)
        out[:rows.shape[0]] = rows
        return out

    def by_tile(edges):
        v = edges.reshape(NG, 2, 2, P, -1)
        return np.ascontiguousarray(v.transpose(0, 3, 2, 1, 4)).reshape(NG, P, TILES, -1)

    src, dst = padded(a["src"], EP), padded(a["dst"], EP, N)
    feat = padded(a["edge_attr_64"], EP).reshape(NG, 2, GROUP // 2, ED)
    vec = by_tile(padded(a["edge_attr_3"], EP))
    w1 = a["L0_gnn_W1"]
    f32 = np.float32
    w1_edges = np.zeros((2, ED, 2, D + 1), f32)
    mlp0, mlp1 = np.zeros((P, 2, HID), f32), np.zeros((2, HID, 2, HID), f32)
    mlp2 = np.zeros((2, HID, 2, D), f32)
    order = [1, 0, 3, 2]
    w3 = a["L1_gnn_mlp_w2"].reshape(HID, 4, MUL)[:, order].reshape(HID, D)
    b3 = a["L1_gnn_mlp_b2"].reshape(4, MUL)[order].reshape(D)
    for half in range(2):
        w1_edges[half, :, half, 0:D] = w1[2 * D:]
        w1_edges[half, :, half, D] = a["L0_gnn_gate_w"][:, 0]
        mlp0[half * NB:(half + 1) * NB, half] = a["L1_gnn_mlp_w0"]
        mlp1[half, :, half] = a["L1_gnn_mlp_w1"]
        mlp2[half, :, half] = w3
    w_up = np.zeros((D, 4, MUL), f32)
    w_up[0:MUL, 0] = a["L1_gnn_W_up0"]
    w_out = np.zeros((8, MUL, D), f32)
    w_out[0, :, 0:MUL] = a["L1_gnn_W_out0"][0:MUL]
    w_out[1, :, 0:MUL] = a["L1_gnn_W_out0"][MUL:]
    for c in range(3):
        w_up[MUL + c::3, 1 + c] = a["L1_gnn_W_up1"]
        w_out[2 + c, :, MUL + c::3] = a["L1_gnn_W_out1"][MUL:]
        w_out[5 + c, :, MUL + c::3] = a["L1_gnn_W_out1"][0:MUL]

    arrays = {
        "x": padded(a["x"], NP),
        "meta": np.concatenate([by_tile(src), by_tile(dst)], axis=2)[..., 0],
        "dst_flat": dst.reshape(1, EP),
        "edge_feat": feat.transpose(0, 1, 3, 2).reshape(NG, P, GROUP // 2),
        "edge_vec": vec.transpose(1, 0, 2, 3).reshape(P, NG * TILES, 3),
        "edge_dist": padded(a["edge_weight"], EP).reshape(P, EP // P),
        "ident": np.eye(P, dtype=f32),
        "w1_nodes": w1[:2 * D].reshape(2, D, D).transpose(1, 0, 2),
        "b1": a["L0_gnn_b1"].reshape(1, D),
        "w1_edges": w1_edges.reshape(P, 2, D + 1),
        "gate_b": a["L0_gnn_gate_b"].reshape(1, 1),
        "ln_g": a["L0_gnn_ln_g"].reshape(1, D),
        "ln_b": a["L0_gnn_ln_b"].reshape(1, D),
        "w2": a["L0_gnn_W2"],
        "b2": a["L0_gnn_b2"].reshape(D, 1),
        "w_ih": a["L0_gnn_W_ih"].T,
        "w_hh": a["L0_gnn_W_hh"].T,
        "b_ih": a["L0_gnn_b_ih"].reshape(3, D).T,
        "b_hh": a["L0_gnn_b_hh"].reshape(3, D).T,
        "w_up": w_up.reshape(D, D),
        "mlp0": mlp0.reshape(P, P),
        "mlp1": mlp1.reshape(P, P),
        "mlp2": mlp2.reshape(P, 2 * D),
        "mlp_b0": np.concatenate([a["L1_gnn_mlp_b0"]] * 2).reshape(P, 1),
        "mlp_b1": np.concatenate([a["L1_gnn_mlp_b1"]] * 2).reshape(P, 1),
        "mlp_b2": np.concatenate([b3, b3]).reshape(1, 2 * D),
        "w_out": w_out.reshape(2, P, D).transpose(1, 0, 2),
    }
    arrays = {k: np.ascontiguousarray(v) for k, v in arrays.items()}
    nc = bacc.Bacc("TRN2", target_bir_lowering=False, num_devices=1)
    io = {k: nc.dram_tensor(f"in_{k}", v.shape, mybir.dt.from_np(v.dtype), kind="ExternalInput").ap() for k, v in arrays.items()}
    io["out"] = nc.dram_tensor("out_nodes", (NP, D), F32, kind="ExternalOutput").ap()
    program(nc, io, N, E)
    result = run_bass_kernel_spmd(nc, [{f"in_{k}": v for k, v in arrays.items()}], core_ids=[0])
    return result.results[0]["out_nodes"][:N]
```
